# Optimizing a Trainium2 kernel written in Bass

```python
import numpy as np
import jax
import jax.numpy as jnp

def _softmax(x, axis=-1):
    return jax.nn.softmax(x, axis=axis)

def _gelu(x):
    return jax.nn.gelu(x, approximate=True)

def _silu(x):
    return jax.nn.silu(x)

def _sigmoid(x):
    return jax.nn.sigmoid(x)

def _layernorm(x, axis=-1, eps=1e-05):
    m = jnp.mean(x, axis=axis, keepdims=True)
    v = jnp.var(x, axis=axis, keepdims=True)
    return (x - m) / jnp.sqrt(v + eps)

def _scatter_add(tgt, idx, src, axis=0):
    return tgt.at[idx].add(src)

def _segment_sum(src, seg, n):
    return jax.ops.segment_sum(src, seg, n)
kernel_name = 'mk_gnn_ffn_d4_gnn_r16_c016ce'

def setup_inputs(seed: int=0):
    np.random.seed(seed)
    _w = jnp.asarray

    def _rec_inputs():
        import jax
        import jax.numpy as jnp
        _gk = jax.random.key(seed)
        x = -0.0002117 + 1 * jax.random.normal(jax.random.fold_in(_gk, 1), (3125, 256), jnp.float32)
        _s = jax.random.randint(jax.random.fold_in(_gk, 2), (50000,), 0, 3125, jnp.int32)
        _d = jax.random.randint(jax.random.fold_in(_gk, 3), (50000,), 0, 3125, jnp.int32)
        _loop = jnp.arange(3125, dtype=jnp.int32)
        src = jnp.concatenate([_s, _d, _loop])
        dst = jnp.concatenate([_d, _s, _loop])
        _o = jnp.argsort(dst, stable=True)
        src = src[_o]
        dst = dst[_o]
        edge_attr_8 = -0.00019784 + 0.999804 * jax.random.normal(jax.random.fold_in(_gk, 12), (103125, 8), jnp.float32)
        edge_weight = jax.random.uniform(jax.random.fold_in(_gk, 14), (103125,), jnp.float32, 0.0, 1)
        return (x, src, dst, edge_attr_8, edge_weight)
    x, src, dst, edge_attr_8, edge_weight = _rec_inputs()

    def _L0_gnn_setup():
        import jax, jax.numpy as jnp
        import numpy as np
        N = 6250
        E = 50000
        FEAT = 256
        HEADS = 8
        HEAD_DIM = FEAT // HEADS
        SCALING = HEAD_DIM ** (-0.5)
        key = jax.random.key(seed)
        ks = jax.random.split(key, 8)
        w_scale = (2.0 / (FEAT + FEAT)) ** 0.5
        return {'nfeat': jax.random.normal(ks[0], (N, FEAT), dtype=jnp.float32), 'attn_bias': jax.random.normal(ks[1], (E, HEADS), dtype=jnp.float32), 'Wq': jax.random.normal(ks[2], (FEAT, FEAT), dtype=jnp.float32) * w_scale, 'Wk': jax.random.normal(ks[3], (FEAT, FEAT), dtype=jnp.float32) * w_scale, 'Wv': jax.random.normal(ks[4], (FEAT, FEAT), dtype=jnp.float32) * w_scale, 'Wo': jax.random.normal(ks[5], (FEAT, FEAT), dtype=jnp.float32) * w_scale, 'src': jax.random.randint(ks[6], (E,), 0, N, dtype=jnp.int32), 'dst': jax.random.randint(ks[7], (E,), 0, N, dtype=jnp.int32)}
    _L0_gnn_all = _L0_gnn_setup()
    _L0_gnn_in = {k: v for k, v in _L0_gnn_all.items() if k in ('Wq', 'Wk', 'Wv', 'Wo')}
    del _L0_gnn_all

    def _L0_ffn_setup():
        import jax, jax.numpy as jnp
        import numpy as np
        E, D, H, TOP_K = (6, 256, 256, 2)
        ROUTER_H = D // 2
        key = jax.random.key(seed)
        ks = jax.random.split(key, 12)
        s = 1.0 / np.sqrt(D)
        sh = 1.0 / np.sqrt(H)
        sr = 1.0 / np.sqrt(ROUTER_H)
        return {'features': jax.random.normal(ks[0], (8, 256, D), dtype=jnp.float32), 'router_w1': jax.random.uniform(ks[1], (D, ROUTER_H), jnp.float32, -s, s), 'router_b1': jnp.zeros((ROUTER_H,), jnp.float32), 'router_w2': jax.random.uniform(ks[2], (ROUTER_H, E), jnp.float32, -sr, sr), 'router_b2': jnp.zeros((E,), jnp.float32), 'expert_w1': jax.random.uniform(ks[3], (E, D, H), jnp.float32, -s, s), 'expert_b1': jnp.zeros((E, H), jnp.float32), 'expert_w2': jax.random.uniform(ks[4], (E, H, H), jnp.float32, -sh, sh), 'expert_b2': jnp.zeros((E, H), jnp.float32), 'expert_w3': jax.random.uniform(ks[5], (E, H, D), jnp.float32, -sh, sh), 'expert_b3': jnp.zeros((E, D), jnp.float32)}
    _L0_ffn_all = _L0_ffn_setup()
    _L0_ffn_in = {k: v for k, v in _L0_ffn_all.items() if k in ('router_w1', 'router_b1', 'router_w2', 'router_b2', 'expert_w1', 'expert_b1', 'expert_w2', 'expert_b2', 'expert_w3', 'expert_b3')}
    del _L0_ffn_all

    def _L1_gnn_setup():
        import jax, jax.numpy as jnp
        import numpy as np
        N, IN_CH, HEADS, OUT_CH, E = (3125, 256, 4, 64, 50000)
        key = jax.random.key(seed)
        k1, k2, k3, k4, k5 = jax.random.split(key, 5)
        x = jax.random.normal(k1, (N, IN_CH), dtype=jnp.float32)
        edge_index = jax.random.randint(k2, (2, E), 0, N, dtype=jnp.int64)
        bw = float(np.sqrt(6.0 / (IN_CH + HEADS * OUT_CH)))
        ba = float(np.sqrt(6.0 / (HEADS + OUT_CH)))
        weight = jax.random.uniform(k3, (IN_CH, HEADS * OUT_CH), jnp.float32, -bw, bw)
        attn_l = jax.random.uniform(k4, (HEADS, OUT_CH), jnp.float32, -ba, ba)
        attn_r = jax.random.uniform(k5, (HEADS, OUT_CH), jnp.float32, -ba, ba)
        return {'x': x, 'edge_index': edge_index, 'weight': weight, 'attn_l': attn_l, 'attn_r': attn_r}
    _L1_gnn_all = _L1_gnn_setup()
    _L1_gnn_in = {k: v for k, v in _L1_gnn_all.items() if k in ('weight', 'attn_l', 'attn_r')}
    del _L1_gnn_all

    def _L1_ffn_setup():
        import jax, jax.numpy as jnp
        import numpy as np
        BN_EPS = 0.001

        def _bn(h, g, b, m, v):
            return g * (h - m) * jax.lax.rsqrt(v + BN_EPS) + b
        key = jax.random.key(seed)
        ks = jax.random.split(key, 8)
        B, F, Df = (256, 64, 256)
        E, H, D = (8, 256, 256)
        s1 = 1.0 / np.sqrt(Df)
        s2 = 1.0 / np.sqrt(H)
        return {'x': jax.random.normal(ks[0], (B, F, Df), jnp.float32), 'Wr': jax.random.normal(ks[1], (Df, E), jnp.float32) * s1, 'br': jnp.zeros((E,), jnp.float32), 'W1': jax.random.normal(ks[2], (E, Df, H), jnp.float32) * s1, 'b1': jnp.zeros((E, H), jnp.float32), 'g1': jnp.ones((E, H), jnp.float32), 'be1': jnp.zeros((E, H), jnp.float32), 'm1': jnp.zeros((E, H), jnp.float32), 'v1': jnp.ones((E, H), jnp.float32), 'W2': jax.random.normal(ks[3], (E, H, H), jnp.float32) * s2, 'b2': jnp.zeros((E, H), jnp.float32), 'g2': jnp.ones((E, H), jnp.float32), 'be2': jnp.zeros((E, H), jnp.float32), 'm2': jnp.zeros((E, H), jnp.float32), 'v2': jnp.ones((E, H), jnp.float32), 'Wo': jax.random.normal(ks[4], (E, H, D), jnp.float32) * s2, 'bo': jnp.zeros((E, D), jnp.float32)}
    _L1_ffn_all = _L1_ffn_setup()
    _L1_ffn_in = {k: v for k, v in _L1_ffn_all.items() if k in ('Wr', 'br', 'W1', 'b1', 'g1', 'be1', 'm1', 'v1', 'W2', 'b2', 'g2', 'be2', 'm2', 'v2', 'Wo', 'bo')}
    del _L1_ffn_all

    def _L2_gnn_setup():
        import jax, jax.numpy as jnp
        import numpy as np
        N = 6250
        E = 100000
        C_IN = 256
        H = 2
        D = 128
        ALPHA = 0.2
        key = jax.random.key(seed)
        ks = jax.random.split(key, 5)
        x = jax.random.normal(ks[0], (N, C_IN), dtype=jnp.float32)
        edge_index = jax.random.randint(ks[1], (2, E), 0, N, dtype=jnp.int64)
        W = jax.random.normal(ks[2], (H, D, C_IN), dtype=jnp.float32) * 0.05
        b = jax.random.normal(ks[3], (H, D), dtype=jnp.float32) * 0.05
        a = jax.random.normal(ks[4], (H, 2 * D), dtype=jnp.float32) * 0.05
        return {'x': x, 'edge_index': edge_index, 'W': W, 'b': b, 'a': a, 'n': N}
    _L2_gnn_all = _L2_gnn_setup()
    _L2_gnn_in = {k: v for k, v in _L2_gnn_all.items() if k in ('W', 'b', 'a')}
    del _L2_gnn_all

    def _L2_ffn_setup():
        import jax, jax.numpy as jnp
        import numpy as np
        IN_CH = 256
        OUT_CH = 256
        key = jax.random.key(seed)
        kx, kw, kb = jax.random.split(key, 3)
        x = jax.random.normal(kx, (8, 256, IN_CH), dtype=jnp.float32)
        bound = 1.0 / np.sqrt(IN_CH)
        weight = jax.random.uniform(kw, (OUT_CH, IN_CH), dtype=jnp.float32, minval=-bound, maxval=bound)
        bias = jax.random.uniform(kb, (OUT_CH,), dtype=jnp.float32, minval=-bound, maxval=bound)
        return {'x': x, 'weight': weight, 'bias': bias}
    _L2_ffn_all = _L2_ffn_setup()
    _L2_ffn_in = {k: v for k, v in _L2_ffn_all.items() if k in ('weight', 'bias')}
    del _L2_ffn_all

    def _L3_gnn_setup():
        import jax, jax.numpy as jnp
        import numpy as np
        N_NODES = 6250
        N_EDGES = 100000
        IN_FEATS = 256
        OUT_FEATS = 256
        key = jax.random.key(seed)
        k_h, k_norm, k_w, k_b, k_src, k_dst = jax.random.split(key, 6)
        stdv = 1.0 / np.sqrt(OUT_FEATS)
        return {'h': jax.random.normal(k_h, (N_NODES, IN_FEATS), dtype=jnp.float32), 'sym_norm': jax.random.uniform(k_norm, (N_EDGES,), dtype=jnp.float32), 'W': jax.random.uniform(k_w, (IN_FEATS, OUT_FEATS), dtype=jnp.float32, minval=-stdv, maxval=stdv), 'b': jax.random.uniform(k_b, (OUT_FEATS,), dtype=jnp.float32, minval=-stdv, maxval=stdv), 'src': jax.random.randint(k_src, (N_EDGES,), 0, N_NODES, dtype=jnp.int32), 'dst': jax.random.randint(k_dst, (N_EDGES,), 0, N_NODES, dtype=jnp.int32)}
    _L3_gnn_all = _L3_gnn_setup()
    _L3_gnn_in = {k: v for k, v in _L3_gnn_all.items() if k in ('W', 'b')}
    del _L3_gnn_all

    def _L3_ffn_setup():
        import jax, jax.numpy as jnp
        import numpy as np
        E = 8
        K = 2
        D = 256
        H = 512
        DOUT = 256
        EPS = 1e-05
        key = jax.random.key(seed)
        ks = jax.random.split(key, 9)
        s = 0.02
        return {'x': jax.random.normal(ks[0], (4, 512, D), jnp.float32), 'gamma': 1.0 + 0.05 * jax.random.normal(ks[1], (D,), jnp.float32), 'beta': 0.05 * jax.random.normal(ks[2], (D,), jnp.float32), 'Wr': 0.01 * jax.random.normal(ks[3], (D, E), jnp.float32), 'br': jnp.zeros((E,), jnp.float32), 'W1': s * jax.random.normal(ks[4], (E, D, H), jnp.float32), 'b1': s * jax.random.normal(ks[5], (E, H), jnp.float32), 'W2': s * jax.random.normal(ks[6], (E, H, DOUT), jnp.float32), 'b2': s * jax.random.normal(ks[7], (E, DOUT), jnp.float32)}
    _L3_ffn_all = _L3_ffn_setup()
    _L3_ffn_in = {k: v for k, v in _L3_ffn_all.items() if k in ('gamma', 'beta', 'Wr', 'br', 'W1', 'b1', 'W2', 'b2')}
    del _L3_ffn_all
    return {'x': x, 'src': src, 'dst': dst, 'edge_attr_8': edge_attr_8, 'edge_weight': edge_weight, 'L0_gnn_Wq': _L0_gnn_in['Wq'], 'L0_gnn_Wk': _L0_gnn_in['Wk'], 'L0_gnn_Wv': _L0_gnn_in['Wv'], 'L0_gnn_Wo': _L0_gnn_in['Wo'], 'L0_ffn_router_w1': _L0_ffn_in['router_w1'], 'L0_ffn_router_b1': _L0_ffn_in['router_b1'], 'L0_ffn_router_w2': _L0_ffn_in['router_w2'], 'L0_ffn_router_b2': _L0_ffn_in['router_b2'], 'L0_ffn_expert_w1': _L0_ffn_in['expert_w1'], 'L0_ffn_expert_b1': _L0_ffn_in['expert_b1'], 'L0_ffn_expert_w2': _L0_ffn_in['expert_w2'], 'L0_ffn_expert_b2': _L0_ffn_in['expert_b2'], 'L0_ffn_expert_w3': _L0_ffn_in['expert_w3'], 'L0_ffn_expert_b3': _L0_ffn_in['expert_b3'], 'L1_gnn_weight': _L1_gnn_in['weight'], 'L1_gnn_attn_l': _L1_gnn_in['attn_l'], 'L1_gnn_attn_r': _L1_gnn_in['attn_r'], 'L1_ffn_Wr': _L1_ffn_in['Wr'], 'L1_ffn_br': _L1_ffn_in['br'], 'L1_ffn_W1': _L1_ffn_in['W1'], 'L1_ffn_b1': _L1_ffn_in['b1'], 'L1_ffn_g1': _L1_ffn_in['g1'], 'L1_ffn_be1': _L1_ffn_in['be1'], 'L1_ffn_m1': _L1_ffn_in['m1'], 'L1_ffn_v1': _L1_ffn_in['v1'], 'L1_ffn_W2': _L1_ffn_in['W2'], 'L1_ffn_b2': _L1_ffn_in['b2'], 'L1_ffn_g2': _L1_ffn_in['g2'], 'L1_ffn_be2': _L1_ffn_in['be2'], 'L1_ffn_m2': _L1_ffn_in['m2'], 'L1_ffn_v2': _L1_ffn_in['v2'], 'L1_ffn_Wo': _L1_ffn_in['Wo'], 'L1_ffn_bo': _L1_ffn_in['bo'], 'L2_gnn_W': _L2_gnn_in['W'], 'L2_gnn_b': _L2_gnn_in['b'], 'L2_gnn_a': _L2_gnn_in['a'], 'L2_ffn_weight': _L2_ffn_in['weight'], 'L2_ffn_bias': _L2_ffn_in['bias'], 'L3_gnn_W': _L3_gnn_in['W'], 'L3_gnn_b': _L3_gnn_in['b'], 'L3_ffn_gamma': _L3_ffn_in['gamma'], 'L3_ffn_beta': _L3_ffn_in['beta'], 'L3_ffn_Wr': _L3_ffn_in['Wr'], 'L3_ffn_br': _L3_ffn_in['br'], 'L3_ffn_W1': _L3_ffn_in['W1'], 'L3_ffn_b1': _L3_ffn_in['b1'], 'L3_ffn_W2': _L3_ffn_in['W2'], 'L3_ffn_b2': _L3_ffn_in['b2']}

def reference(x, src, dst, edge_attr_8, edge_weight, L0_gnn_Wq, L0_gnn_Wk, L0_gnn_Wv, L0_gnn_Wo, L0_ffn_router_w1, L0_ffn_router_b1, L0_ffn_router_w2, L0_ffn_router_b2, L0_ffn_expert_w1, L0_ffn_expert_b1, L0_ffn_expert_w2, L0_ffn_expert_b2, L0_ffn_expert_w3, L0_ffn_expert_b3, L1_gnn_weight, L1_gnn_attn_l, L1_gnn_attn_r, L1_ffn_Wr, L1_ffn_br, L1_ffn_W1, L1_ffn_b1, L1_ffn_g1, L1_ffn_be1, L1_ffn_m1, L1_ffn_v1, L1_ffn_W2, L1_ffn_b2, L1_ffn_g2, L1_ffn_be2, L1_ffn_m2, L1_ffn_v2, L1_ffn_Wo, L1_ffn_bo, L2_gnn_W, L2_gnn_b, L2_gnn_a, L2_ffn_weight, L2_ffn_bias, L3_gnn_W, L3_gnn_b, L3_ffn_gamma, L3_ffn_beta, L3_ffn_Wr, L3_ffn_br, L3_ffn_W1, L3_ffn_b1, L3_ffn_W2, L3_ffn_b2):
    import jax
    import jax.numpy as jnp

    def _L0_gnn_ref(nfeat, attn_bias, Wq, Wk, Wv, Wo, src, dst):
        import jax, jax.numpy as jnp
        import numpy as np
        N = 6250
        E = 50000
        FEAT = 256
        HEADS = 8
        HEAD_DIM = FEAT // HEADS
        SCALING = HEAD_DIM ** (-0.5)
        n = nfeat.shape[0]
        q = (nfeat @ Wq.T).reshape(n, HEADS, HEAD_DIM) / SCALING
        k = (nfeat @ Wk.T).reshape(n, HEADS, HEAD_DIM)
        v = (nfeat @ Wv.T).reshape(n, HEADS, HEAD_DIM)
        attn = jnp.einsum('ehd,ehd->eh', k[src], q[dst])
        attn = attn + attn_bias
        m = jax.ops.segment_max(attn, dst, num_segments=n)
        a = jnp.exp(attn - m[dst])
        s = jax.ops.segment_sum(a, dst, num_segments=n)
        a = a / s[dst]
        out = jax.ops.segment_sum(v[src] * a[:, :, None], dst, num_segments=n)
        return out.reshape(n, FEAT) @ Wo.T

    def _L0_ffn_ref(features, router_w1, router_b1, router_w2, router_b2, expert_w1, expert_b1, expert_w2, expert_b2, expert_w3, expert_b3):
        import jax, jax.numpy as jnp
        import numpy as np
        E, D, H, TOP_K = (6, 256, 256, 2)
        ROUTER_H = D // 2
        rh = jax.nn.relu(features @ router_w1 + router_b1)
        expert_logits = jax.nn.softmax(rh @ router_w2 + router_b2, axis=-1)
        top_w, top_i = jax.lax.top_k(expert_logits, TOP_K)
        routing_weights = jax.nn.softmax(top_w, axis=-1)
        h1 = jax.nn.relu(jnp.einsum('bsd,edh->bseh', features, expert_w1) + expert_b1)
        h2 = jax.nn.relu(jnp.einsum('bseh,ehf->bsef', h1, expert_w2) + expert_b2)
        expert_out = jnp.einsum('bsef,efo->bseo', h2, expert_w3) + expert_b3
        sel = jnp.take_along_axis(expert_out, top_i[:, :, :, None], axis=2)
        combined = jnp.sum(sel * routing_weights[..., None], axis=2)
        return combined

    def _L1_gnn_ref(x, edge_index, weight, attn_l, attn_r):
        import jax, jax.numpy as jnp
        import numpy as np
        N, IN_CH, HEADS, OUT_CH, E = (3125, 256, 4, 64, 50000)
        heads, out_ch = attn_l.shape
        n = x.shape[0]
        xt = jnp.matmul(x, weight).reshape(-1, heads, out_ch)
        row, col = (edge_index[0], edge_index[1])
        alpha_l = jnp.einsum('ehd,hd->eh', xt[row], attn_l)
        alpha_r = jnp.einsum('ehd,hd->eh', xt[col], attn_r)
        alpha = jax.nn.softmax(jax.nn.leaky_relu(alpha_l + alpha_r, 0.01), axis=1)
        tmp = jnp.einsum('nh,nhd->nd', alpha[:n], xt[col[:n]])
        out = jnp.broadcast_to(tmp[:, None, :], (n, heads, out_ch))
        return out.reshape(n, heads * out_ch)

    def _L1_ffn_ref(x, Wr, br, W1, b1, g1, be1, m1, v1, W2, b2, g2, be2, m2, v2, Wo, bo):
        import jax, jax.numpy as jnp
        import numpy as np
        BN_EPS = 0.001

        def _bn(h, g, b, m, v):
            return g * (h - m) * jax.lax.rsqrt(v + BN_EPS) + b
        feat = jnp.mean(x, axis=0)
        w = jax.nn.softmax(feat @ Wr + br, axis=-1)
        h = jnp.einsum('bfd,edh->bfeh', x, W1) + b1
        h = jax.nn.relu(_bn(h, g1, be1, m1, v1))
        h = jnp.einsum('bfeh,ehk->bfek', h, W2) + b2
        h = jax.nn.relu(_bn(h, g2, be2, m2, v2))
        y = jnp.einsum('bfeh,ehd->bfed', h, Wo) + bo
        return jnp.einsum('bfed,fe->bfd', y, w)

    def _L2_gnn_ref(x, edge_index, W, b, a, n):
        import jax, jax.numpy as jnp
        import numpy as np
        N = 6250
        E = 100000
        C_IN = 256
        H = 2
        D = 128
        ALPHA = 0.2
        src = edge_index[0]
        dst = edge_index[1]

        def head(Wh, bh, ah):
            h = x @ Wh.T + bh
            s_src = h @ ah[:D]
            s_dst = h @ ah[D:]
            score = s_src[src] + s_dst[dst]
            lrelu = jnp.where(score > 0, score, ALPHA * score)
            e = jnp.exp(-lrelu)
            row_sum = jax.ops.segment_sum(e, src, num_segments=n)
            num = jax.ops.segment_sum(e[:, None] * h[dst], src, num_segments=n)
            h_prime = num / row_sum[:, None]
            return jax.nn.elu(h_prime)
        outs = jax.vmap(head)(W, b, a)
        return jnp.moveaxis(outs, 0, 1).reshape(x.shape[0], H * D)

    def _L2_ffn_ref(x, weight, bias):
        import jax, jax.numpy as jnp
        import numpy as np
        IN_CH = 256
        OUT_CH = 256
        return jnp.einsum('bsi,oi->bso', x, weight) + bias

    def _L3_gnn_ref(h, sym_norm, W, b, src, dst):
        import jax, jax.numpy as jnp
        import numpy as np
        N_NODES = 6250
        N_EDGES = 100000
        IN_FEATS = 256
        OUT_FEATS = 256
        n_nodes = h.shape[0]
        hw = jnp.matmul(h, W)
        msg = hw[src] * sym_norm[:, None]
        agg = jax.ops.segment_sum(msg, dst, num_segments=n_nodes)
        return jax.nn.relu(agg + b)

    def _L3_ffn_ref(x, gamma, beta, Wr, br, W1, b1, W2, b2):
        import jax, jax.numpy as jnp
        import numpy as np
        E = 8
        K = 2
        D = 256
        H = 512
        DOUT = 256
        EPS = 1e-05
        mu = jnp.mean(x, axis=-1, keepdims=True)
        var = jnp.mean(jnp.square(x - mu), axis=-1, keepdims=True)
        xn = (x - mu) * jax.lax.rsqrt(var + EPS) * gamma + beta
        logits = jnp.einsum('bsd,de->bse', xn, Wr) + br
        top_vals, top_idx = jax.lax.top_k(logits, K)
        w = jax.nn.softmax(top_vals, axis=-1)
        w_full = jnp.einsum('bsk,bske->bse', w, jax.nn.one_hot(top_idx, E, dtype=w.dtype))
        y = jnp.zeros(x.shape[:-1] + (DOUT,), x.dtype)
        for e in range(E):
            h = jax.nn.gelu(jnp.einsum('bsd,dh->bsh', xn, W1[e]) + b1[e], approximate=False)
            y_e = jnp.einsum('bsh,hd->bsd', h, W2[e]) + b2[e]
            y = y + y_e * w_full[..., e, None]
        return y
    edge_index = jnp.stack([src, dst])
    x = x + _L0_gnn_ref(_layernorm(x, axis=-1), edge_attr_8, L0_gnn_Wq, L0_gnn_Wk, L0_gnn_Wv, L0_gnn_Wo, src, dst)
    x = x + _L0_ffn_ref(_layernorm(x, axis=-1)[None], L0_ffn_router_w1, L0_ffn_router_b1, L0_ffn_router_w2, L0_ffn_router_b2, L0_ffn_expert_w1, L0_ffn_expert_b1, L0_ffn_expert_w2, L0_ffn_expert_b2, L0_ffn_expert_w3, L0_ffn_expert_b3)[0]
    x = x + _L1_gnn_ref(_layernorm(x, axis=-1), edge_index, L1_gnn_weight, L1_gnn_attn_l, L1_gnn_attn_r)
    x = x + _L1_ffn_ref(_layernorm(x, axis=-1)[None], L1_ffn_Wr, L1_ffn_br, L1_ffn_W1, L1_ffn_b1, L1_ffn_g1, L1_ffn_be1, L1_ffn_m1, L1_ffn_v1, L1_ffn_W2, L1_ffn_b2, L1_ffn_g2, L1_ffn_be2, L1_ffn_m2, L1_ffn_v2, L1_ffn_Wo, L1_ffn_bo)[0]
    x = x + _L2_gnn_ref(_layernorm(x, axis=-1), edge_index, L2_gnn_W, L2_gnn_b, L2_gnn_a, 3125)
    x = x + _L2_ffn_ref(_layernorm(x, axis=-1)[None], L2_ffn_weight, L2_ffn_bias)[0]
    x = x + _L3_gnn_ref(_layernorm(x, axis=-1), edge_weight, L3_gnn_W, L3_gnn_b, src, dst)
    x = x + _L3_ffn_ref(_layernorm(x, axis=-1)[None], L3_ffn_gamma, L3_ffn_beta, L3_ffn_Wr, L3_ffn_br, L3_ffn_W1, L3_ffn_b1, L3_ffn_W2, L3_ffn_b2)[0]
    return x

_drawn_inputs = setup_inputs


def setup_inputs(seed=0):
    import zlib

    import numpy as np

    out = dict(_drawn_inputs(seed))
    spreads = {'L0_ffn_router_b1': (0.0, 0.282),
     'L0_ffn_router_b2': (0.0, 0.1),
     'L0_ffn_expert_b1': (0.0, 0.54),
     'L0_ffn_expert_b2': (0.0, 0.1),
     'L0_ffn_expert_b3': (0.0, 0.1),
     'L1_ffn_br': (0.0, 0.321),
     'L1_ffn_b1': (0.0, 0.273),
     'L1_ffn_g1': (1.0, 0.2),
     'L1_ffn_be1': (0.0, 0.297),
     'L1_ffn_m1': (0.0, 0.293),
     'L1_ffn_v1': (1.0, 0.6),
     'L1_ffn_b2': (0.0, 0.1),
     'L1_ffn_g2': (1.0, 0.2),
     'L1_ffn_be2': (0.0, 0.1),
     'L1_ffn_m2': (0.0, 0.1),
     'L1_ffn_v2': (1.0, 0.2),
     'L1_ffn_bo': (0.0, 0.1),
     'L3_ffn_br': (0.0, 0.422)}
    factors = {'L3_gnn_b': 5.837,
     'L3_ffn_gamma': 8.0,
     'L3_ffn_beta': 8.0,
     'L3_ffn_Wr': 3.266,
     'L3_ffn_b1': 25.99,
     'L3_ffn_b2': 8.0}
    for name, (base, spread) in spreads.items():
        noise = np.random.default_rng([zlib.crc32(name.encode()), seed]).standard_normal(out[name].shape)
        drawn = base * np.exp(spread * noise) if base else spread * noise
        out[name] = jnp.asarray(drawn.astype(out[name].dtype))
    for name, factor in factors.items():
        out[name] = (out[name] * factor).astype(out[name].dtype)
    return out
```

```python
import concourse.bass as bass
from concourse import mybir
from contextlib import ExitStack

fp32 = mybir.dt.float32
i32 = mybir.dt.int32
bf16 = mybir.dt.bfloat16
ALU = mybir.AluOpType
ACT = mybir.ActivationFunctionType
AX = mybir.AxisListType

P = 128
N = 3125
F = 256
E = 103125
TILES = -(-N // P)
NP = TILES * P
GROUP = 5
GROUPS = TILES // GROUP
EPS = 1e-5


class Scope:

    def __init__(self, nc, ctx, name):
        self.nc, self.ctx, self.name, self.sems = nc, ctx, name, []
        ctx.callback(self.clear)

    def sb(self, name, shape, dt=fp32):
        return self.ctx.enter_context(self.nc.sbuf_tensor(f"{self.name}_{name}", shape, dt))

    def ps(self, name, shape, dt=fp32):
        return self.ctx.enter_context(self.nc.psum_tensor(f"{self.name}_{name}", shape, dt))

    def sem(self, name):
        self.sems.append(self.nc.alloc_semaphore(f"{self.name}_{name}"))
        return self.sems[-1]

    def clear(self):
        self.nc.clear_and_free_semaphores(self.sems)
        self.nc.all_engine_barrier()


def rows(dram, g, n):
    return dram[bass.ds(g * n, n), :].rearrange("(t p) d -> p t d", p=P)


def across(vector, n):
    return vector.rearrange("(a n) -> a n", a=1).to_broadcast([P, n])


def projection_phase(nc, name, ident_dram, a_dram, w_drams, out_drams, res_dram=None, bias_dram=None,
                     layernorm=True, dots=()):
    nout = sum(w.shape[1] for w in w_drams)
    row = sum(o.shape[1] for o in out_drams)
    cuts = [(n, min(n + 512, nout)) for n in range(0, nout, 512)]
    with ExitStack() as ctx:
        s = Scope(nc, ctx, name)
        ident = s.sb("ident", [P, P])
        w = s.sb("w", [P, 2, nout])
        bias = s.sb("bias", [P, nout]) if bias_dram is not None else None
        dotv = [s.sb(f"dotv{i}", [P, F]) for i in range(len(dots))]
        a = s.sb("a", [P, GROUP, F])
        res = s.sb("res", [P, GROUP, F]) if res_dram is not None else None
        stats = s.sb("stats", [P, GROUP, 6])
        mv = s.sb("mv", [P, GROUP, 2])
        std = s.sb("std", [P, GROUP])
        rstd = s.sb("rstd", [P, GROUP])
        epsb = s.sb("epsb", [P, 1])
        xn = s.sb("xn", [P, GROUP, F]) if layernorm else a
        xT = s.sb("xT", [P, GROUP, 2, P])
        prod = s.sb("prod", [P, F])
        og = s.sb("og", [P, GROUP, row])
        tp = s.ps("tp", [P, 3 * 512])
        po = [s.ps(f"po{i}", [P, 1024]) for i in range(2)]
        const_loaded = s.sem("const_loaded")
        eps_set = s.sem("eps_set")
        a_loaded = s.sem("a_loaded")
        res_loaded = s.sem("res_loaded")
        var_ready = s.sem("var_ready")
        std_ready = s.sem("std_ready")
        xn_ready = s.sem("xn_ready")
        turned = s.sem("turned")
        xT_ready = s.sem("xT_ready")
        product_ready = s.sem("product_ready")
        tile_out = s.sem("tile_out")
        stored = [s.sem(f"stored{i}") for i in range(len(out_drams))]
        n_const = 1 + len(w_drams) + (bias is not None) + len(dots)
        with nc.Block() as block:

            @block.sync
            def _(sp):
                sp.dma_start(ident[:], ident_dram).then_inc(const_loaded, 16)
                at = 0
                for m in w_drams:
                    sp.dma_start(w[:, :, at:at + m.shape[1]], m.rearrange("(k p) n -> p k n", p=P))\
                        .then_inc(const_loaded, 16)
                    at += m.shape[1]
                if bias is not None:
                    sp.dma_start(bias[:], across(bias_dram, nout)).then_inc(const_loaded, 16)
                for v, (vec, _) in zip(dotv, dots):
                    sp.dma_start(v[:], across(vec, F)).then_inc(const_loaded, 16)
                with sp.Fori(0, GROUPS) as g:
                    sp.wait_ge(turned, g)
                    sp.dma_start(a[:], rows(a_dram, g, GROUP * P)).then_inc(a_loaded, 16)
                    if res is not None:
                        sp.wait_ge(tile_out, GROUP * g)
                        sp.dma_start(res[:], rows(res_dram, g, GROUP * P)).then_inc(res_loaded, 16)

            @block.gpsimd
            def _(pool):
                pool.memset(epsb[:], EPS).then_inc(eps_set, 1)
                with pool.Fori(0, GROUPS) as g:
                    pool.wait_ge(tile_out, GROUP * g + GROUP)
                    at = 0
                    for i, o in enumerate(out_drams):
                        pool.dma_start(rows(o, g, GROUP * P), og[:, :, at:at + o.shape[1]]).then_inc(stored[i], 16)
                        at += o.shape[1]
                for i in range(len(out_drams)):
                    pool.wait_ge(stored[i], 16 * GROUPS)

            @block.scalar
            def _(act):
                act.wait_ge(eps_set, 1)
                with act.Fori(0, GROUPS) as g:
                    if layernorm:
                        act.wait_ge(var_ready, g + 1)
                        act.activation(std[:], mv[:, :, 1], ACT.Sqrt, bias=epsb[:, 0:1]).then_inc(std_ready, 1)
                    act.wait_ge(turned, g + 1)
                    act.wait_ge(product_ready, GROUP * g)
                    act.activation(xT[:].rearrange("p t k n -> p (t k n)"), tp[:, 0:2 * GROUP * P],
                                   ACT.Copy).then_inc(xT_ready, 1)

            @block.tensor
            def _(pe):
                pe.wait_ge(const_loaded, 16 * n_const)
                with pe.Fori(0, GROUPS) as g:
                    if layernorm:
                        pe.wait_ge(xn_ready, g + 1)
                    else:
                        pe.wait_ge(a_loaded, 16 * g + 16)
                    pe.wait_ge(xT_ready, g)
                    for t in range(GROUP):
                        for k in range(2):
                            c = (t * 2 + k) * P
                            last = nc.tensor.transpose(tp[:, c:c + P], xn[:, t, k * P:(k + 1) * P], ident[:])
                    last.then_inc(turned, 1)
                    pe.wait_ge(xT_ready, g + 1)
                    for t in range(GROUP):
                        pe.wait_ge(tile_out, GROUP * g + max(t - 1, 0))
                        for n0, n1 in cuts:
                            for k in range(2):
                                last = nc.tensor.matmul(po[t % 2][:, n0:n1], xT[:, t, k, :], w[:, k, n0:n1],
                                                        start=(k == 0), stop=(k == 1))
                        last.then_inc(product_ready, 1)

            @block.vector
            def _(dve):
                dve.wait_ge(const_loaded, 16 * n_const)
                with dve.Fori(0, GROUPS) as g:
                    if layernorm:
                        dve.wait_ge(a_loaded, 16 * g + 16)
                        for t in range(GROUP):
                            dve.bn_stats(stats[:, t, :], a[:, t, :])
                        dve.drain()
                        for t in range(GROUP):
                            last = dve.bn_aggr(mv[:, t, :], stats[:, t, :])
                        last.then_inc(var_ready, 1)
                        dve.wait_ge(std_ready, g + 1)
                        dve.reciprocal(rstd[:], std[:])
                        dve.drain()
                        for t in range(GROUP):
                            last = dve.tensor_scalar(xn[:, t, :], a[:, t, :], mv[:, t, 0:1], rstd[:, t:t + 1],
                                                     ALU.subtract, ALU.mult)
                        last.then_inc(xn_ready, 1)
                    if res is not None:
                        dve.wait_ge(res_loaded, 16 * g + 16)
                    for i in range(len(out_drams)):
                        dve.wait_ge(stored[i], 16 * g)
                    for t in range(GROUP):
                        dve.wait_ge(product_ready, GROUP * g + t + 1)
                        src = po[t % 2][:, 0:nout]
                        out = og[:, t, 0:nout]
                        if bias is not None:
                            dve.tensor_tensor(out, src, bias[:], ALU.add)
                            if res is not None:
                                dve.drain()
                                dve.tensor_tensor(out, out, res[:, t, :], ALU.add)
                        elif res is not None:
                            dve.tensor_tensor(out, src, res[:, t, :], ALU.add)
                        else:
                            dve.tensor_copy(out, src)
                        at = nout
                        for v, (_, heads) in zip(dotv, dots):
                            dve.drain()
                            dve.tensor_tensor(prod[:], out, v[:], ALU.mult)
                            dve.drain()
                            dve.tensor_reduce(og[:, t, at:at + heads],
                                              prod[:].rearrange("p (h d) -> p h d", h=heads), AX.X, ALU.add)
                            at += heads
                        dve.drain().then_inc(tile_out, 1)


def moe_phase(nc, name, ident_dram, x_dram, out_dram, router, gate, w1, hidden_act, w2, w3, b3, inner_norm=None):
    Ex, _, H = w1.shape
    MB = H // P
    deep = w2 is not None
    KC = 2 if deep else MB
    halves = [(0, 3), (3, GROUP)]
    routed = len(router) == 4
    with ExitStack() as ctx:
        s = Scope(nc, ctx, name)
        ident = s.sb("ident", [P, P])
        wa = s.sb("wa", [P, Ex, 2, H])
        wb = s.sb("wb", [P, Ex, 2, F]) if deep else None
        wc = s.sb("wc", [P, Ex, KC, F])
        bc = s.sb("bc", [Ex, F])
        if routed:
            rw1 = s.sb("rw1", [P, 2, P])
            rb1 = s.sb("rb1", [P, 1])
            rw2 = s.sb("rw2", [P, Ex])
            rh = s.sb("rh", [P, GROUP * P])
        else:
            rw = s.sb("rw", [P, 2, Ex])
        rb = s.sb("rb", [P, Ex])
        sizes = [MB] + [2] * deep
        hb = [s.sb(f"hb{i}", [P, Ex, m]) for i, m in enumerate(sizes)]
        hs = [s.sb(f"hs{i}", [P, Ex, m]) if len(act) == 6 else None for i, (m, act) in enumerate(zip(sizes, hidden_act))]
        bn = [[s.sb(f"bn{i}{j}", [P, Ex, m]) for j in range(4)] if len(act) == 6 else None
              for i, (m, act) in enumerate(zip(sizes, hidden_act))]
        if inner_norm:
            gamma = s.sb("gamma", [P, F])
            beta = s.sb("beta", [P, F])
        epsb = s.sb("epsb", [P, 2])
        x = s.sb("x", [P, GROUP, F])
        stats = s.sb("stats", [P, GROUP, 6])
        mv = s.sb("mv", [P, GROUP, 2])
        std = s.sb("std", [P, GROUP])
        rstd = s.sb("rstd", [P, GROUP])
        xn = s.sb("xn", [P, GROUP, F])
        xT = s.sb("xT", [P, 2, GROUP * P])
        h1 = s.sb("h1", [P, MB, GROUP * P])
        h2 = s.sb("h2", [P, 2, GROUP * P]) if deep else None
        last_h = h2 if deep else h1
        acc = s.sb("acc", [P, GROUP, F])
        before = s.sb("before", [P, Ex, Ex])
        steps = s.sb("steps", [P, Ex, Ex], i32)
        z = s.sb("z", [P, GROUP, Ex])
        z2 = s.sb("z2", [P, GROUP, Ex])
        ex = s.sb("ex", [P, GROUP, Ex])
        gates = s.sb("gates", [P, GROUP, Ex])
        sel = s.sb("sel", [P, GROUP, Ex])
        top = s.sb("top", [P, GROUP])
        total = s.sb("total", [P, GROUP])
        over = s.sb("over", [P, Ex, Ex])
        same = s.sb("same", [P, Ex, Ex])
        gT = s.sb("gT", [Ex, GROUP * P])
        pA = s.ps("pA", [P, 4, 512])
        pC = s.ps("pC", [P, 3 * 512])
        pR = s.ps("pR", [P, 512])
        const_loaded = s.sem("const_loaded")
        pool_set = s.sem("pool_set")
        bn_ready = s.sem("bn_ready")
        bn_std = s.sem("bn_std")
        x_loaded = s.sem("x_loaded")
        var_ready = s.sem("var_ready")
        std_ready = s.sem("std_ready")
        xn_ready = s.sem("xn_ready")
        turned = s.sem("turned")
        xT_ready = s.sem("xT_ready")
        router_hidden = s.sem("router_hidden")
        router_act = s.sem("router_act")
        logits_ready = s.sem("logits_ready")
        logits_read = s.sem("logits_read")
        shifted = s.sem("shifted")
        exp_ready = s.sem("exp_ready")
        gates_ready = s.sem("gates_ready")
        gT_turned = s.sem("gT_turned")
        gT_ready = s.sem("gT_ready")
        base_ready = s.sem("base_ready")
        base_added = s.sem("base_added")
        hidden_product = s.sem("hidden_product")
        hidden_ready = s.sem("hidden_ready")
        expert_out = s.sem("expert_out")
        combined = s.sem("combined")
        stored = s.sem("stored")
        HID = Ex * 2 * (MB + 2 * deep)
        banks = [(0, 2), (2, 4), (4, 5)]
        BANKS = len(banks)
        OUT = Ex * BANKS
        norms = 2 if inner_norm else 1
        exps = 2 if gate == "softmax_top2_softmax" else 1
        n_bn = sum(b is not None for b in bn)
        loads = [(ident[:], ident_dram)]
        loads += [(wa[:, e], w1[e].rearrange("(k p) n -> p k n", p=P)) for e in range(Ex)]
        loads += [(wb[:, e], w2[e].rearrange("(k p) n -> p k n", p=P)) for e in range(Ex)] if deep else []
        loads += [(wc[:, e], w3[e].rearrange("(k p) n -> p k n", p=P)) for e in range(Ex)]
        loads += [(bc[:], b3)]
        if routed:
            loads += [(rw1[:], router[0].rearrange("(k p) n -> p k n", p=P)),
                      (rb1[:], router[1].rearrange("(p a) -> p a", a=1)), (rw2[:], router[2])]
        else:
            loads += [(rw[:], router[0].rearrange("(k p) n -> p k n", p=P))]
        loads += [(rb[:], across(router[-1], Ex))]
        if inner_norm:
            loads += [(gamma[:], across(inner_norm[0], F)), (beta[:], across(inner_norm[1], F))]
        by_feature = []
        for i, act in enumerate(hidden_act):
            by_feature += [(hb[i], act[1])]
            if len(act) == 6:
                by_feature += list(zip(bn[i], act[2:]))
        for to, of in by_feature:
            loads += [(to[:, e, :], of[e].rearrange("(m p) -> p m", p=P)) for e in range(Ex)]

        with nc.Block() as block:

            @block.sync
            def _(sp):
                for to, of in loads:
                    sp.dma_start(to, of, allow_slow_non_contiguous=True).then_inc(const_loaded, 16)
                with sp.Fori(0, GROUPS) as g:
                    sp.wait_ge(base_added, BANKS * g)
                    sp.dma_start(x[:], rows(x_dram, g, GROUP * P)).then_inc(x_loaded, 16)

            @block.gpsimd
            def _(pool):
                pool.memset(epsb[:, 0:1], EPS)
                pool.memset(epsb[:, 1:2], 1e-3)
                pool.iota(steps[:], [[-1, Ex], [1, Ex]], base=0, channel_multiplier=0)
                pool.drain().then_inc(pool_set, 1)
                with pool.Fori(0, GROUPS) as g:
                    pool.wait_ge(combined, OUT * g + OUT)
                    pool.dma_start(rows(out_dram, g, GROUP * P), acc[:]).then_inc(stored, 16)
                pool.wait_ge(stored, 16 * GROUPS)

            @block.scalar
            def _(act):
                act.wait_ge(pool_set, 1)
                act.wait_ge(const_loaded, 16 * len(loads))
                for b in bn:
                    if b is not None:
                        act.activation(b[3][:], b[3][:], ACT.Sqrt, bias=epsb[:, 1:2]).then_inc(bn_std, 1)
                if n_bn:
                    act.wait_ge(bn_ready, 1)
                with act.Fori(0, GROUPS) as g:
                    for i in range(norms):
                        act.wait_ge(var_ready, norms * g + i + 1)
                        act.activation(std[:], mv[:, :, 1], ACT.Sqrt, bias=epsb[:, 0:1]).then_inc(std_ready, 1)
                    act.wait_ge(turned, g + 1)
                    act.activation(xT[:].rearrange("p k (t n) -> p t k n", n=P),
                                   pC[:, 0:2 * GROUP * P].rearrange("p (t k n) -> p t k n", k=2, n=P),
                                   ACT.Copy).then_inc(xT_ready, 1)
                    if routed:
                        for i, (t0, t1) in enumerate(halves):
                            act.wait_ge(router_hidden, 2 * g + i + 1)
                            act.activation(rh[:, t0 * P:t1 * P], pA[:, i, 0:(t1 - t0) * P], ACT.Relu,
                                           bias=rb1[:, 0:1]).then_inc(router_act, 1)
                    for i in range(exps):
                        act.wait_ge(shifted, exps * g + i + 1)
                        act.activation(ex[:], z2[:], ACT.Exp).then_inc(exp_ready, 1)
                    j = 0
                    for e in range(Ex):
                        for layer, m_n in enumerate(sizes):
                            to = (h1, h2)[layer]
                            for t0, t1 in halves:
                                for m in range(m_n):
                                    act.wait_ge(hidden_product, HID * g + j + 1)
                                    scale = hs[layer][:, e, m:m + 1] if hs[layer] is not None else 1.0
                                    act.activation(to[:, m, t0 * P:t1 * P], pA[:, j % 4, 0:(t1 - t0) * P],
                                                   hidden_act[layer][0], bias=hb[layer][:, e, m:m + 1],
                                                   scale=scale).then_inc(hidden_ready, 1)
                                    j += 1

            @block.tensor
            def _(pe):
                pe.wait_ge(const_loaded, 16 * len(loads))
                with pe.Fori(0, GROUPS) as g:
                    pe.wait_ge(xn_ready, norms * g + norms)
                    pe.wait_ge(combined, OUT * g)
                    for t in range(GROUP):
                        for k in range(2):
                            c = (t * 2 + k) * P
                            last = nc.tensor.transpose(pC[:, c:c + P], xn[:, t, k * P:(k + 1) * P], ident[:])
                    last.then_inc(turned, 1)
                    pe.wait_ge(xT_ready, g + 1)
                    pe.wait_ge(hidden_ready, HID * g)
                    if routed:
                        for i, (t0, t1) in enumerate(halves):
                            for k in range(2):
                                last = nc.tensor.matmul(pA[:, i, 0:(t1 - t0) * P], rw1[:, k, :],
                                                        xT[:, k, t0 * P:t1 * P], start=(k == 0), stop=(k == 1))
                            last.then_inc(router_hidden, 1)
                        pe.wait_ge(router_act, 2 * g + 2)
                    pe.wait_ge(logits_read, g)
                    for t in range(GROUP):
                        if routed:
                            last = nc.tensor.matmul(pR[:, t * Ex:(t + 1) * Ex], rh[:, t * P:(t + 1) * P], rw2[:],
                                                    start=True, stop=True)
                        else:
                            for k in range(2):
                                last = nc.tensor.matmul(pR[:, t * Ex:(t + 1) * Ex], xT[:, k, t * P:(t + 1) * P],
                                                        rw[:, k, :], start=(k == 0), stop=(k == 1))
                    last.then_inc(logits_ready, 1)
                    j = 0
                    for e in range(Ex):
                        done = {}
                        for layer, m_n in enumerate(sizes):
                            w, of = ((wa, xT), (wb, h1))[layer]
                            for h, (t0, t1) in enumerate(halves):
                                if layer:
                                    pe.wait_ge(hidden_ready, HID * g + done[0, h])
                                for m in range(m_n):
                                    pe.wait_ge(hidden_ready, HID * g + max(j - 3, 0))
                                    for k in range(2):
                                        last = nc.tensor.matmul(pA[:, j % 4, 0:(t1 - t0) * P],
                                                                w[:, e, k, m * P:(m + 1) * P],
                                                                of[:, k, t0 * P:t1 * P],
                                                                start=(k == 0), stop=(k == 1))
                                    last.then_inc(hidden_product, 1)
                                    j += 1
                                done[layer, h] = j
                        if e == 0:
                            pe.wait_ge(gates_ready, g + 1)
                            for t in range(GROUP):
                                last = nc.tensor.transpose(pC[0:Ex, t * P:(t + 1) * P], gates[:, t, :], ident[:])
                            last.then_inc(gT_turned, 1)
                            pe.wait_ge(gT_ready, g + 1)
                            for t in range(GROUP):
                                last = nc.tensor.matmul(pC[:, t * F:(t + 1) * F], gT[:, t * P:(t + 1) * P], bc[:],
                                                        start=True, stop=True)
                            last.then_inc(base_ready, 1)
                        for b, (t0, t1) in enumerate(banks):
                            pe.wait_ge(hidden_ready, HID * g + done[len(sizes) - 1, 0 if t1 <= 3 else 1])
                            if e == 0:
                                pe.wait_ge(base_added, BANKS * g + b + 1)
                            else:
                                pe.wait_ge(combined, OUT * g + BANKS * (e - 1) + b + 1)
                            for t in range(t0, t1):
                                for k in range(KC):
                                    last = nc.tensor.matmul(pC[:, t * F:(t + 1) * F],
                                                            last_h[:, k, t * P:(t + 1) * P], wc[:, e, k, :],
                                                            start=(k == 0), stop=(k == KC - 1))
                            last.then_inc(expert_out, 1)

            @block.vector
            def _(dve):
                dve.wait_ge(const_loaded, 16 * len(loads))
                dve.wait_ge(pool_set, 1)
                dve.tensor_scalar(before[:], steps[:], 0.0, None, ALU.is_lt)
                if n_bn:
                    dve.wait_ge(bn_std, n_bn)
                    for i, b in enumerate(bn):
                        if b is not None:
                            g_, be_, m_, sd_ = b
                            dve.reciprocal(sd_[:], sd_[:])
                            dve.drain()
                            dve.tensor_tensor(hs[i][:], g_[:], sd_[:], ALU.mult)
                            dve.tensor_tensor(hb[i][:], hb[i][:], m_[:], ALU.subtract)
                            dve.drain()
                            dve.tensor_tensor(hb[i][:], hb[i][:], hs[i][:], ALU.mult)
                            dve.drain()
                            dve.tensor_tensor(hb[i][:], hb[i][:], be_[:], ALU.add)
                    dve.drain().then_inc(bn_ready, 1)
                else:
                    dve.drain()
                with dve.Fori(0, GROUPS) as g:
                    dve.wait_ge(x_loaded, 16 * g + 16)
                    for i in range(norms):
                        of = x if i == 0 else xn
                        for t in range(GROUP):
                            dve.bn_stats(stats[:, t, :], of[:, t, :])
                        dve.drain()
                        for t in range(GROUP):
                            last = dve.bn_aggr(mv[:, t, :], stats[:, t, :])
                        last.then_inc(var_ready, 1)
                        dve.wait_ge(std_ready, norms * g + i + 1)
                        dve.reciprocal(rstd[:], std[:])
                        dve.drain()
                        for t in range(GROUP):
                            last = dve.tensor_scalar(xn[:, t, :], of[:, t, :], mv[:, t, 0:1], rstd[:, t:t + 1],
                                                     ALU.subtract, ALU.mult)
                        if i == 1:
                            dve.drain()
                            every = [P, GROUP, F]
                            dve.tensor_tensor(xn[:], xn[:], gamma[:].rearrange("p (a n) -> p a n", a=1).to_broadcast(every), ALU.mult)
                            dve.drain()
                            last = dve.tensor_tensor(xn[:], xn[:], beta[:].rearrange("p (a n) -> p a n", a=1).to_broadcast(every), ALU.add)
                        last.then_inc(xn_ready, 1)
                        dve.wait_ge(xn_ready, norms * g + i + 1)
                    ge = [P, GROUP, Ex]

                    def wide(v):
                        return v[:].rearrange("p (t a) -> p t a", a=1).to_broadcast(ge)

                    dve.wait_ge(logits_ready, g + 1)
                    dve.tensor_tensor(z[:], pR[:, 0:GROUP * Ex].rearrange("p (t e) -> p t e", e=Ex),
                                      rb[:].rearrange("p (a e) -> p a e", a=1).to_broadcast(ge),
                                      ALU.add).then_inc(logits_read, 1)
                    dve.drain()
                    for i in range(exps):
                        if i == exps - 1 and gate != "softmax":
                            for t in range(GROUP):
                                pairs = [P, Ex, Ex]
                                zj = z[:, t, :].rearrange("p (a e) -> p a e", a=1).to_broadcast(pairs)
                                ze = z[:, t, :].rearrange("p (e a) -> p e a", a=1).to_broadcast(pairs)
                                dve.tensor_tensor(over[:], zj, ze, ALU.is_gt)
                                dve.tensor_tensor(same[:], zj, ze, ALU.is_equal)
                                dve.drain()
                                dve.tensor_tensor(same[:], same[:], before[:], ALU.mult)
                                dve.drain()
                                dve.tensor_tensor(over[:], over[:], same[:], ALU.add)
                                dve.drain()
                                dve.tensor_reduce(sel[:, t, :], over[:], AX.X, ALU.add)
                                dve.drain()
                                dve.tensor_scalar(sel[:, t, :], sel[:, t, :], 1.5, None, ALU.is_lt)
                        dve.tensor_reduce(top[:], z[:], AX.X, ALU.max)
                        dve.drain()
                        dve.tensor_tensor(z2[:], z[:], wide(top), ALU.subtract).then_inc(shifted, 1)
                        dve.wait_ge(exp_ready, exps * g + i + 1)
                        if i == exps - 1 and gate != "softmax":
                            dve.tensor_tensor(ex[:], ex[:], sel[:], ALU.mult)
                            dve.drain()
                        dve.tensor_reduce(total[:], ex[:], AX.X, ALU.add)
                        dve.drain()
                        dve.reciprocal(total[:], total[:])
                        dve.drain()
                        to = gates if i == exps - 1 else z
                        last = dve.tensor_tensor(to[:], ex[:], wide(total), ALU.mult)
                        if i < exps - 1:
                            dve.drain()
                    last.then_inc(gates_ready, 1)
                    dve.wait_ge(gT_turned, g + 1)
                    dve.tensor_copy(gT[:], pC[0:Ex, 0:GROUP * P]).then_inc(gT_ready, 1)
                    dve.wait_ge(base_ready, g + 1)
                    dve.wait_ge(stored, 16 * g)
                    for t0, t1 in banks:
                        dve.tensor_tensor(acc[:, t0:t1, :], x[:, t0:t1, :],
                                          pC[:, t0 * F:t1 * F].rearrange("p (t n) -> p t n", n=F),
                                          ALU.add).then_inc(base_added, 1)
                    dve.wait_ge(base_added, BANKS * g + BANKS)
                    for e in range(Ex):
                        for b, (t0, t1) in enumerate(banks):
                            dve.wait_ge(expert_out, OUT * g + BANKS * e + b + 1)
                            if e:
                                dve.wait_ge(combined, OUT * g + BANKS * (e - 1) + b + 1)
                            for t in range(t0, t1):
                                last = dve.scalar_tensor_tensor(acc[:, t, :], pC[:, t * F:(t + 1) * F],
                                                                gates[:, t, e:e + 1], acc[:, t, :],
                                                                ALU.mult, ALU.add)
                            last.then_inc(combined, 1)


def ffn0(nc, a, x, out):
    p = "L0_ffn_"
    moe_phase(nc, "ffn0", a["ident"], x, out,
              (a[p + "router_w1"], a[p + "router_b1"], a[p + "router_w2"], a[p + "router_b2"]),
              "softmax_top2_softmax", a[p + "expert_w1"],
              [(ACT.Relu, a[p + "expert_b1"]), (ACT.Relu, a[p + "expert_b2"])],
              a[p + "expert_w2"], a[p + "expert_w3"], a[p + "expert_b3"])


def ffn1(nc, a, x, out):
    p = "L1_ffn_"
    moe_phase(nc, "ffn1", a["ident"], x, out, (a[p + "Wr"], a[p + "br"]), "softmax", a[p + "W1"],
              [(ACT.Relu, *(a[p + n + str(i)] for n in ("b", "g", "be", "m", "v"))) for i in (1, 2)],
              a[p + "W2"], a[p + "Wo"], a[p + "bo"])


def ffn3(nc, a, x, out):
    p = "L3_ffn_"
    moe_phase(nc, "ffn3", a["ident"], x, out, (a[p + "Wr"], a[p + "br"]), "top2_softmax", a[p + "W1"],
              [(ACT.Gelu, a[p + "b1"])], None, a[p + "W2"], a[p + "b2"],
              inner_norm=(a[p + "gamma"], a[p + "beta"]))


R = 4
SETS = 4
SLOTS = 64
MAIN = SLOTS // R
LOOP_TILES = TILES + 1
ALL_TILES = TILES + 2
ROWS = LOOP_TILES * P
COLS = -(-E // P)
N_MAIN, N_EXTRA, BASE, EXTRA_BASE, USES = 0, 1, 2, 3, 4
NODE, START, DEGREE, TARGET = 0, 1, 2, 3


def order_phase(nc, name, a, key_dram, order_dram, keys_dram, perm, counts):
    BLOCK = 13
    BLOCKS = COLS // BLOCK
    assert BLOCKS * BLOCK == COLS and BLOCKS % 2 == 0
    with ExitStack() as ctx:
        s = Scope(nc, ctx, name)
        key = s.sb("key", [P, COLS], i32)
        part = s.sb("part", [P, COLS], i32)
        low = s.sb("low", [P, COLS], bf16)
        high = s.sb("high", [P, COLS], bf16)
        iota_low = s.sb("iota_low", [P, P], bf16)
        one_low = [s.sb(f"one_low{u}", [P, BLOCK, P], bf16) for u in range(2)]
        one_high = [s.sb(f"one_high{u}", [P, BLOCK, TILES], bf16) for u in range(2)]
        zero = s.sb("zero", [P, P], bf16)
        before = s.sb("before", [P, P])
        ones = s.sb("ones", [P, P])
        node = s.sb("node", [P, ALL_TILES], i32)
        nodef = s.sb("nodef", [P, TILES])
        target = s.sb("target", [P, ALL_TILES], i32)
        deg = s.sb("deg", [P, TILES])
        total = s.sb("total", [P, TILES])
        start = s.sb("start", [P, TILES])
        onesf = s.sb("onesf", [P, ALL_TILES])
        sortkey = s.sb("sortkey", [P, TILES])
        every = s.sb("every", [P, TILES * P])
        above = s.sb("above", [P, TILES * P], bf16)
        rankf = s.sb("rankf", [P, TILES])
        rank = s.sb("rank", [P, TILES], i32)
        record = s.sb("record", [P, TILES, 4], i32)
        spare = s.sb("spare", [P, 2, 4], i32)
        degf = s.sb("degf", [P, TILES])
        most = s.sb("most", [P, TILES])
        bodies = s.sb("bodies", [P, ALL_TILES], i32)
        work = s.sb("work", [P, ALL_TILES], i32)
        workf = s.sb("workf", [P, ALL_TILES])
        sumf = s.sb("sumf", [P, ALL_TILES])
        p_deg = s.ps("p_deg", [P, 512])
        p_sum = s.ps("p_sum", [P, 512])
        key_loaded = s.sem("key_loaded")
        const_loaded = s.sem("const_loaded")
        pool_set = s.sem("pool_set")
        zero_set = s.sem("zero_set")
        hot_ready = [s.sem(f"hot_ready{u}") for u in range(2)]
        hot_used = [s.sem(f"hot_used{u}") for u in range(2)]
        deg_summed = s.sem("deg_summed")
        deg_ready = s.sem("deg_ready")
        prefix_ready = s.sem("prefix_ready")
        sortkey_ready = s.sem("sortkey_ready")
        sortkey_stored = s.sem("sortkey_stored")
        every_loaded = s.sem("every_loaded")
        record_ready = s.sem("record_ready")
        scattered = s.sem("scattered")
        perm_loaded = s.sem("perm_loaded")
        degf_ready = s.sem("degf_ready")
        most_ready = s.sem("most_ready")
        done = s.sem("done")
        with nc.Block() as block:

            @block.sync
            def _(sp):
                sp.dma_start(key[:], key_dram.rearrange("(p t) -> p t", p=P)).then_inc(key_loaded, 16)
                sp.dma_start(before[:], a["before"]).then_inc(const_loaded, 16)
                sp.wait_ge(sortkey_ready, 1)
                sp.dma_start(keys_dram.rearrange("(k p) -> p k", p=P), sortkey[:],
                             allow_slow_non_contiguous=True).then_inc(sortkey_stored, 16)
                sp.wait_ge(sortkey_stored, 16)
                sp.dma_start(every[:], across(keys_dram, TILES * P)).then_inc(every_loaded, 16)
                sp.wait_ge(scattered, 16 * TILES)
                sp.dma_start(perm[:, 0:TILES, :], order_dram.rearrange("(k p) c -> p k c", p=P)).then_inc(perm_loaded, 16)

            @block.gpsimd
            def _(pool):
                pool.iota(iota_low[:], [[1, P]], base=0, channel_multiplier=0, allow_small_or_imprecise_dtypes=True)
                pool.iota(node[:], [[P, ALL_TILES]], base=0, channel_multiplier=1)
                pool.memset(ones[:], 1.0)
                pool.memset(onesf[:], 1.0)
                pool.memset(spare[:], 0)
                pool.drain().then_inc(pool_set, 1)
                for k in range(TILES):
                    if k == 0:
                        pool.wait_ge(record_ready, 1)
                    pool.indirect_dma_start(out=order_dram, in_=record[:, k, :], in_offset=None,
                                            out_offset=bass.IndirectOffsetOnAxis(ap=rank[:, k:k + 1], axis=0))\
                        .then_inc(scattered, 16)
                pool.wait_ge(degf_ready, 1)
                pool.partition_all_reduce(most[:], degf[:], P, bass.bass_isa.ReduceOp.max).then_inc(most_ready, 1)
                pool.wait_ge(scattered, 16 * TILES)

            @block.tensor
            def _(pe):
                pe.wait_ge(zero_set, 1)
                nc.tensor.matmul(p_deg[:, 0:TILES], zero[:], zero[:, 0:TILES], start=True, stop=False)
                with pe.Fori(0, BLOCKS // 2) as i:
                    for u in range(2):
                        pe.wait_ge(hot_ready[u], i + 1)
                        for t in range(BLOCK):
                            last = nc.tensor.matmul(p_deg[:, 0:TILES], one_low[u][:, t, :], one_high[u][:, t, :],
                                                    start=False, stop=False)
                        last.then_inc(hot_used[u], 1)
                nc.tensor.matmul(p_deg[:, 0:TILES], zero[:], zero[:, 0:TILES], start=False, stop=True).then_inc(deg_summed, 1)
                pe.wait_ge(const_loaded, 16)
                pe.wait_ge(pool_set, 1)
                pe.wait_ge(deg_ready, 1)
                nc.tensor.matmul(p_sum[:, 0:TILES], before[:], deg[:], start=True, stop=True)
                nc.tensor.matmul(p_sum[:, 256:256 + TILES], ones[:], deg[:], start=True, stop=True)\
                    .then_inc(prefix_ready, 1)

            @block.vector
            def _(dve):
                dve.memset(zero[:], 0.0).then_inc(zero_set, 1)
                dve.wait_ge(key_loaded, 16)
                dve.wait_ge(pool_set, 1)
                dve.tensor_scalar(part[:], key[:], P - 1, None, ALU.bitwise_and)
                dve.drain()
                dve.tensor_copy(low[:], part[:])
                dve.drain()
                dve.tensor_scalar(part[:], key[:], 7, None, ALU.logical_shift_right)
                dve.drain()
                dve.tensor_copy(high[:], part[:])
                dve.drain()
                with dve.Fori(0, BLOCKS // 2) as i:
                    for u in range(2):
                        dve.wait_ge(hot_used[u], i)
                        at = bass.ds((i * 2 + u) * BLOCK, BLOCK)
                        dve.tensor_tensor(one_low[u][:], iota_low[:].rearrange("p (a n) -> p a n", a=1).to_broadcast([P, BLOCK, P]),
                                          low[:, at].rearrange("p (t a) -> p t a", a=1).to_broadcast([P, BLOCK, P]),
                                          ALU.is_equal)
                        dve.tensor_tensor(one_high[u][:], iota_low[:, 0:TILES].rearrange("p (a n) -> p a n", a=1).to_broadcast([P, BLOCK, TILES]),
                                          high[:, at].rearrange("p (t a) -> p t a", a=1).to_broadcast([P, BLOCK, TILES]),
                                          ALU.is_equal)
                        dve.drain().then_inc(hot_ready[u], 1)
                dve.wait_ge(deg_summed, 1)
                dve.tensor_copy(deg[:], p_deg[:, 0:TILES]).then_inc(deg_ready, 1)
                dve.tensor_copy(nodef[:], node[:, 0:TILES])
                dve.drain()
                dve.tensor_scalar(sortkey[:], deg[:], 4000.0, 4096.0, ALU.min, ALU.mult)
                dve.drain()
                dve.tensor_tensor(sortkey[:], sortkey[:], nodef[:], ALU.add)
                dve.drain().then_inc(sortkey_ready, 1)
                dve.wait_ge(prefix_ready, 1)
                dve.tensor_copy(total[:], p_sum[:, 256:256 + TILES])
                dve.drain()
                dve.tensor_tensor_scan(start[:], onesf[:, 0:TILES], total[:], 0.0, ALU.mult, ALU.add)
                dve.drain()
                dve.tensor_tensor(start[:], start[:], total[:], ALU.subtract)
                dve.drain()
                dve.tensor_tensor(start[:], start[:], p_sum[:, 0:TILES], ALU.add)
                dve.drain()
                dve.tensor_copy(record[:, :, NODE], node[:, 0:TILES])
                dve.tensor_copy(record[:, :, START], start[:])
                dve.tensor_copy(record[:, :, DEGREE], deg[:])
                dve.tensor_copy(record[:, :, TARGET], node[:, 0:TILES])
                dve.wait_ge(every_loaded, 16)
                for k in range(TILES):
                    dve.tensor_scalar(above[:], every[:], sortkey[:, k:k + 1], 0.0, ALU.is_gt, ALU.add,
                                      accum_out=rankf[:, k:k + 1])
                    dve.drain()
                dve.tensor_copy(rank[:], rankf[:])
                dve.drain().then_inc(record_ready, 1)
                for k in range(2):
                    dve.tensor_copy(perm[:, TILES + k, NODE:NODE + 1], node[:, 0:1])
                    dve.tensor_copy(perm[:, TILES + k, START:TARGET], spare[:, k, START:TARGET])
                    dve.tensor_copy(perm[:, TILES + k, TARGET:TARGET + 1], node[:, TILES:TILES + 1])
                dve.wait_ge(perm_loaded, 16)
                dve.tensor_copy(degf[:], perm[:, 0:TILES, DEGREE]).then_inc(degf_ready, 1)
                dve.wait_ge(most_ready, 1)
                dve.memset(workf[:], 1.0)
                dve.drain()
                dve.tensor_scalar(workf[:, 0:TILES], most[:], float(R - 1), float(R), ALU.add, ALU.max)
                dve.drain()
                dve.tensor_scalar(workf[:, TILES:ALL_TILES], workf[:, TILES:ALL_TILES], float(R - 1), None, ALU.add)
                dve.drain()
                dve.tensor_copy(bodies[:], workf[:])
                dve.drain()
                dve.tensor_scalar(bodies[:], bodies[:], R.bit_length() - 1, None, ALU.logical_shift_right)
                dve.drain()
                table = counts[:].rearrange("p (k c) -> p k c", c=8)
                dve.tensor_scalar(table[:, :, N_MAIN], bodies[0:1, :], float(MAIN), None, ALU.min)
                dve.tensor_scalar(table[:, :, N_EXTRA], bodies[0:1, :], float(MAIN), 0.0, ALU.subtract, ALU.max)
                dve.drain()

                def sum_before(to, of):
                    dve.tensor_copy(workf[0:1, :], of)
                    dve.drain()
                    dve.tensor_tensor_scan(sumf[0:1, :], onesf[0:1, :], workf[0:1, :], 0.0, ALU.mult, ALU.add)
                    dve.drain()
                    dve.tensor_tensor(sumf[0:1, :], sumf[0:1, :], workf[0:1, :], ALU.subtract)
                    dve.drain()
                    dve.tensor_copy(to, sumf[0:1, :])
                    dve.drain()

                sum_before(table[:, :, BASE], bodies[0:1, :])
                sum_before(table[:, :, EXTRA_BASE], table[:, :, N_EXTRA])
                for u in range(SETS):
                    dve.tensor_scalar(work[0:1, :], table[:, :, N_MAIN], float(SETS - 1 - u), None, ALU.add)
                    dve.drain()
                    dve.tensor_scalar(work[0:1, :], work[0:1, :], SETS.bit_length() - 1, None, ALU.logical_shift_right)
                    dve.drain()
                    sum_before(table[:, :, USES + u], work[0:1, :])
                dve.drain().then_inc(done, 1)
                dve.wait_ge(done, 1)


def neighbour_phase(nc, name, kind, a, perm, counts, table, own_table, res_table, src_dram, edge_dram, out_dram,
                    bias_dram=None):
    attend, separable, weighted = (kind == k for k in ("attend", "separable", "weighted"))
    row = table.shape[1]
    own_row = own_table.shape[1] if own_table is not None else 0
    edge_row = edge_dram.shape[1] if edge_dram is not None else 0
    HEADS = {"attend": 8, "separable": 2, "weighted": 1}[kind]
    HD = F // HEADS
    MSG = HEADS * (HD + (not weighted))
    BIG = 1e30
    with ExitStack() as ctx:
        s = Scope(nc, ctx, name)
        node_at = [s.sb(f"node_at{u}", [P, 4], i32) for u in range(2)]
        target_at = [s.sb(f"target_at{u}", [P, 1], i32) for u in range(2)]
        index = [s.sb(f"index{u}", [P, SLOTS], i32) for u in range(2)]
        edge = [s.sb(f"edge{u}", [P, SLOTS * edge_row]) for u in range(2)] if edge_row else None
        own = [s.sb(f"own{u}", [P, own_row]) for u in range(2)] if own_row else None
        res = [s.sb(f"res{u}", [P, F]) for u in range(2)] if res_table is not None else None
        got = [s.sb(f"got{i}", [P, R, row]) for i in range(SETS)]
        start_x = s.sb("start_x", [P, 1], i32)
        index_x = s.sb("index_x", [P, R], i32)
        edge_x = s.sb("edge_x", [P, R * edge_row]) if edge_row else None
        slot = s.sb("slot", [P, SLOTS])
        degree = s.sb("degree", [P, 1])
        valid = s.sb("valid", [P, SLOTS])
        valid_x = s.sb("valid_x", [P, R])
        left = s.sb("left", [P, 1])
        filled = s.sb("filled", [P, 1])
        out = [s.sb(f"out{u}", [P, F]) for u in range(2)]
        msg = [s.sb(f"msg{v}", [P, R, HEADS, HD + (not weighted)]) for v in range(2)]
        ident = s.sb("ident", [P, P])
        if attend:
            q = s.sb("q", [P, F])
            prod = s.sb("prod", [P, R, F])
            score = s.sb("score", [P, R + 1, HEADS])
            peak = s.sb("peak", [P, HEADS])
            pen = s.sb("pen", [P, SLOTS])
            pen_x = s.sb("pen_x", [P, R])
            acc = s.sb("acc", [P, MSG])
            weight = [s.sb(f"weight{v}", [P, R + 1, HEADS]) for v in range(2)]
            inv = s.sb("inv", [P, HEADS])
        if separable:
            score = s.sb("score", [P, R, HEADS])
            reach = s.sb("reach", [P, SLOTS, HEADS])
            reach_x = s.sb("reach_x", [P, R, HEADS])
            pen = s.sb("pen", [P, SLOTS])
            pen_x = s.sb("pen_x", [P, R])
            inv = s.sb("inv", [P, HEADS])
            low = s.sb("low", [P, F])
            high = s.sb("high", [P, F])
            none = s.sb("none", [P, 1])
        if weighted:
            bias = s.sb("bias", [P, F])
            high = s.sb("high", [P, F])
        zero = s.sb("zero", [P, MSG])
        p_msg = [s.ps(f"p_msg{u}", [P, 512]) for u in range(2)]
        const_loaded = s.sem("const_loaded")
        pool_set = s.sem("pool_set")
        node_ready = s.sem("node_ready")
        index_loaded = [s.sem(f"index_loaded{u}") for u in range(2)]
        edge_loaded = [s.sem(f"edge_loaded{u}") for u in range(2)]
        own_loaded = [s.sem(f"own_loaded{u}") for u in range(2)]
        res_loaded = [s.sem(f"res_loaded{u}") for u in range(2)]
        sums_free = s.sem("sums_free")
        gathered = [s.sem(f"gathered{i}") for i in range(SETS)]
        released = [s.sem(f"released{i}") for i in range(SETS)]
        extra_done = s.sem("extra_done")
        start_x_ready = s.sem("start_x_ready")
        index_x_loaded = s.sem("index_x_loaded")
        edge_x_loaded = s.sem("edge_x_loaded")
        gathered_x = s.sem("gathered_x")
        pool_waited = s.sem("pool_waited")
        shifted = s.sem("shifted")
        weights_ready = s.sem("weights_ready")
        messages_ready = s.sem("messages_ready")
        summed = s.sem("summed")
        zeroed = s.sem("zeroed")
        tile_summed = s.sem("tile_summed")
        final_shifted = s.sem("final_shifted")
        final_exp = s.sem("final_exp")
        out_ready = s.sem("out_ready")
        scattered = [s.sem(f"scattered{u}") for u in range(2)]

        def rows_at(ap):
            return bass.IndirectOffsetOnAxis(ap=ap, axis=0)

        def count(eng, t, column, low, high):
            return eng.value_load(counts[0:1, bass.ds(t * 8 + column, 1)], min_val=low, max_val=high)

        def bodies(eng, pair, u, main, extra, between=None):
            t = pair * 2 + u
            n_main = count(eng, t, N_MAIN, 1, MAIN)
            n_extra = count(eng, t, N_EXTRA, 0, E)
            base = count(eng, t, BASE, 0, E)
            extra_base = count(eng, t, EXTRA_BASE, 0, E)
            uses = [count(eng, t, USES + i, 0, E) for i in range(SETS)] if eng is nc.vector else None
            main(0, 0, base, uses[0] if uses else None, True)
            for st in range(1, SETS):
                with eng.If(n_main > st):
                    main(st, st * R, base + st, uses[st] if uses else None, False)
            with eng.If(n_main > SETS):
                with eng.Fori(1, (n_main + SETS - 1) // SETS) as i:
                    for st in range(SETS):
                        with eng.If(i * SETS + st < n_main):
                            main(st, (i * SETS + st) * R, base + i * SETS + st, uses[st] + i if uses else None, False)
            if between:
                between(n_main, base + n_main)
            with eng.If(n_extra > 0):
                with eng.Fori(0, n_extra) as i:
                    extra(base + n_main + i, extra_base + i)

        with nc.Block() as block:

            @block.sync
            def _(sp):
                sp.dma_start(ident[:], a["ident"]).then_inc(const_loaded, 16)
                if weighted:
                    sp.dma_start(bias[:], across(bias_dram, F)).then_inc(const_loaded, 16)

            @block.gpsimd
            def _(pool):
                pool.iota(slot[:], [[1, SLOTS]], base=0, channel_multiplier=0, allow_small_or_imprecise_dtypes=True)
                pool.memset(zero[:], 0.0)
                pool.drain().then_inc(pool_set, 1)

                def wait_apart(sem, value):
                    pool.wait_ge(sem, value)
                    pool.sem_inc(pool_waited, 1)

                def prefetch(u):
                    node = node_at[u][:, NODE:NODE + 1]
                    start = node_at[u][:, START:START + 1]
                    pool.indirect_dma_start(out=index[u][:], out_offset=None, in_=src_dram, in_offset=rows_at(start))\
                        .then_inc(index_loaded[u], 16)
                    if edge_row:
                        pool.indirect_dma_start(out=edge[u][:], out_offset=None, in_=edge_dram, in_offset=rows_at(start))\
                            .then_inc(edge_loaded[u], 16)
                    if own_row:
                        pool.indirect_dma_start(out=own[u][:], out_offset=None, in_=own_table, in_offset=rows_at(node))\
                            .then_inc(own_loaded[u], 16)
                    if res is not None:
                        pool.indirect_dma_start(out=res[u][:], out_offset=None, in_=res_table, in_offset=rows_at(node))\
                            .then_inc(res_loaded[u], 16)

                def scatter(u):
                    pool.indirect_dma_start(out=out_dram, in_=out[u][:], in_offset=None,
                                            out_offset=rows_at(target_at[u][:, 0:1])).then_inc(scattered[u], 16)

                pool.wait_ge(node_ready, 1)
                prefetch(0)
                with pool.Fori(0, LOOP_TILES // 2) as pair:
                    for u in range(2):
                        t = pair * 2 + u
                        n_main = count(pool, t, N_MAIN, 1, MAIN)
                        uses = [count(pool, t, USES + i, 0, E) for i in range(SETS)]
                        pool.wait_ge(index_loaded[u], 16 * pair + 16)

                        def gather(j):
                            st = j % SETS
                            wait_apart(released[st], uses[st] + j // SETS)
                            for r in range(R):
                                pool.indirect_dma_start(out=got[st][:, r, :], out_offset=None, in_=table,
                                                        in_offset=rows_at(index[u][:, j * R + r:j * R + r + 1]))\
                                    .then_inc(gathered[st], 16)

                        for j in range(MAIN):
                            if j == 0:
                                gather(j)
                            else:
                                with pool.If(n_main > j):
                                    gather(j)
                            if j == 4:
                                wait_apart(node_ready, t + 2)
                                prefetch(1 - u)
                        n_extra = count(pool, t, N_EXTRA, 0, E)
                        with pool.If(n_extra > 0):
                            extra_base = count(pool, t, EXTRA_BASE, 0, E)
                            with pool.Fori(0, n_extra) as i:
                                wait_apart(start_x_ready, extra_base + i + 1)
                                pool.indirect_dma_start(out=index_x[:], out_offset=None, in_=src_dram,
                                                        in_offset=rows_at(start_x[:, 0:1])).then_inc(index_x_loaded, 16)
                                if edge_row:
                                    pool.indirect_dma_start(out=edge_x[:], out_offset=None, in_=edge_dram,
                                                            in_offset=rows_at(start_x[:, 0:1])).then_inc(edge_x_loaded, 16)
                                wait_apart(index_x_loaded, (extra_base + i + 1) * 16)
                                for r in range(R):
                                    pool.indirect_dma_start(out=got[0][:, r, :], out_offset=None, in_=table,
                                                            in_offset=rows_at(index_x[:, r:r + 1])).then_inc(gathered_x, 16)
                            wait_apart(extra_done, extra_base + n_extra)
                        if u == 0:
                            with pool.If(pair > 0):
                                wait_apart(out_ready, t)
                                scatter(1)
                        else:
                            wait_apart(out_ready, t)
                            scatter(0)
                pool.wait_ge(out_ready, LOOP_TILES)
                scatter(1)
                for u in range(2):
                    pool.wait_ge(scattered[u], 16 * (LOOP_TILES // 2))
                pool.wait_ge(index_loaded[0], 16 * (LOOP_TILES // 2) + 16)
                if edge_row:
                    pool.wait_ge(edge_loaded[0], 16 * (LOOP_TILES // 2) + 16)
                if own_row:
                    pool.wait_ge(own_loaded[0], 16 * (LOOP_TILES // 2) + 16)
                if res is not None:
                    pool.wait_ge(res_loaded[0], 16 * (LOOP_TILES // 2) + 16)

            @block.scalar
            def _(act):
                if not weighted:
                    with act.Fori(0, LOOP_TILES // 2) as pair:
                        for u in range(2):

                            def body(b, v):
                                act.wait_ge(shifted, b + 1)
                                if attend:
                                    act.activation(weight[v][:], score[:], ACT.Exp).then_inc(weights_ready, 1)
                                else:
                                    act.activation(msg[v][:, :, :, HD], score[:], ACT.Exp, scale=-1.0)\
                                       .then_inc(weights_ready, 1)

                            bodies(act, pair, u, lambda st, slots, b, use, first: body(b, st % 2), lambda b, x: body(b, 0))
                            if separable:
                                act.wait_ge(final_shifted, pair * 2 + u + 1)
                                act.activation(low[:], low[:], ACT.Exp).then_inc(final_exp, 1)

            @block.tensor
            def _(pe):
                pe.wait_ge(const_loaded, 16 + 16 * weighted)
                pe.wait_ge(pool_set, 1)
                with pe.Fori(0, LOOP_TILES // 2) as pair:
                    for u in range(2):
                        if not attend:
                            pe.wait_ge(sums_free, pair * 2 + u + 1)
                            nc.tensor.matmul(p_msg[u][:, 0:MSG], ident[:], zero[:], start=True, stop=False)

                        def body(b, v):
                            pe.wait_ge(messages_ready, b + 1)
                            for r in range(R):
                                last = nc.tensor.matmul(p_msg[0 if attend else u][:, 0:MSG], ident[:],
                                                        msg[v][:, r].rearrange("p h d -> p (h d)"),
                                                        start=attend and r == 0, stop=attend and r == R - 1)
                            last.then_inc(summed, 1)

                        bodies(pe, pair, u, lambda st, slots, b, use, first: body(b, st % 2), lambda b, x: body(b, 0))
                        if not attend:
                            nc.tensor.matmul(p_msg[u][:, 0:MSG], ident[:], zero[:], start=False, stop=True)\
                                .then_inc(tile_summed, 1)

            @block.vector
            def _(dve):
                def heads(ap, n=HEADS):
                    return ap.rearrange("p (h d) -> p h d", h=n)

                def over(ap, shape, pattern, **kw):
                    return ap.rearrange(pattern, **kw).to_broadcast(shape)

                def set_node(u, t):
                    dve.tensor_copy(node_at[u][:].rearrange("p (a c) -> p a c", a=1), perm[:, bass.ds(t, 1), :])\
                        .then_inc(node_ready, 1)

                dve.wait_ge(pool_set, 1)
                dve.wait_ge(const_loaded, 16 + 16 * weighted)
                set_node(0, 0)
                dve.sem_inc(sums_free, 2)
                dve.sem_inc(summed, 1)
                with dve.Fori(0, LOOP_TILES // 2) as pair:
                    for u in range(2):
                        t = pair * 2 + u
                        dve.wait_ge(node_ready, t + 1)
                        dve.wait_ge(index_loaded[u], 16 * pair + 16)
                        dve.tensor_copy(degree[:], node_at[u][:, DEGREE:DEGREE + 1])
                        dve.wait_ge(scattered[u], 16 * pair)
                        dve.tensor_copy(target_at[u][:], node_at[u][:, TARGET:TARGET + 1])
                        if u == 0:
                            dve.wait_ge(index_loaded[1], 16 * pair)
                        set_node(1 - u, t + 1)
                        dve.drain()
                        dve.tensor_scalar(valid[:], slot[:], degree[:, 0:1], None, ALU.is_lt)
                        dve.tensor_scalar(filled[:], degree[:], 0.0, None, ALU.is_gt)
                        dve.tensor_scalar(left[:], degree[:], float(SLOTS), None, ALU.subtract)
                        dve.tensor_scalar(start_x[:], node_at[u][:, START:START + 1], float(SLOTS), None, ALU.add)
                        dve.drain()
                        if edge_row:
                            dve.wait_ge(edge_loaded[u], 16 * pair + 16)
                        if own_row:
                            dve.wait_ge(own_loaded[u], 16 * pair + 16)
                        if attend:
                            ev = edge[u][:].rearrange("p (s h) -> p s h", h=HEADS)
                            dve.tensor_tensor(ev, ev, over(valid[:], [P, SLOTS, HEADS], "p (s a) -> p s a", a=1), ALU.mult)
                            dve.tensor_scalar(pen[:], valid[:], 1.0, BIG, ALU.subtract, ALU.mult)
                            dve.tensor_scalar(q[:], own[u][:], float(HD) ** 0.5, None, ALU.mult)
                            dve.memset(acc[:], 0.0)
                            dve.memset(score[:, R, :], -BIG)
                            dve.drain()
                            dve.tensor_tensor(ev, ev, over(pen[:], [P, SLOTS, HEADS], "p (s a) -> p s a", a=1), ALU.add)
                            dve.drain()
                        if separable:
                            dve.tensor_scalar(pen[:], valid[:], 1.0, -BIG, ALU.subtract, ALU.mult)
                            dve.drain()
                            dve.tensor_tensor(reach[:], over(own[u][:, F:F + 2], [P, SLOTS, HEADS], "p (a h) -> p a h", a=1),
                                              over(pen[:], [P, SLOTS, HEADS], "p (s a) -> p s a", a=1), ALU.add)
                            dve.drain()
                        if weighted:
                            dve.tensor_tensor(edge[u][:], edge[u][:], valid[:], ALU.mult)
                            dve.drain()

                        def fold(b, v):
                            dve.tensor_tensor(heads(acc[:]), heads(acc[:]),
                                              over(weight[v][:, R, :], [P, HEADS, HD + 1], "p (h a) -> p h a", a=1), ALU.mult)
                            dve.drain()
                            dve.wait_ge(summed, b + 2)
                            dve.tensor_tensor(acc[:], acc[:], p_msg[0][:, 0:MSG], ALU.add)

                        def body(st, v, b, ev, first):
                            rows_ = got[st]
                            by_head = [P, R, HEADS, HD]
                            if attend:
                                dve.tensor_tensor(prod[:], rows_[:, :, 0:F], over(q[:], [P, R, F], "p (a n) -> p a n", a=1), ALU.mult)
                                dve.drain()
                                dve.tensor_reduce(score[:, 0:R, :].rearrange("p r h -> p (r h)"),
                                                  prod[:].rearrange("p r (h d) -> p (r h) d", d=HD), AX.X, ALU.add)
                                dve.drain()
                                flat = score[:, 0:R, :].rearrange("p r h -> p (r h)")
                                dve.tensor_tensor(flat, flat, ev, ALU.add)
                                dve.drain()
                                dve.tensor_reduce(peak[:], score[:].rearrange("p r h -> p h r"), AX.X, ALU.max)
                                dve.drain()
                                dve.tensor_tensor(score[:], score[:], over(peak[:], [P, R + 1, HEADS], "p (a h) -> p a h", a=1),
                                                  ALU.subtract).then_inc(shifted, 1)
                                if not first:
                                    fold(b - 1, 1 - v)
                                dve.wait_ge(weights_ready, b + 1)
                                dve.tensor_copy(score[:, R, :], peak[:])
                                dve.tensor_copy(msg[v][:, :, :, HD], weight[v][:, 0:R, :])
                                dve.tensor_tensor(msg[v][:, :, :, 0:HD],
                                                  rows_[:, :, F:2 * F].rearrange("p r (h d) -> p r h d", h=HEADS),
                                                  weight[v][:, 0:R, :].rearrange("p r (h a) -> p r h a", a=1).to_broadcast(by_head),
                                                  ALU.mult)
                            if separable:
                                dve.tensor_tensor(score[:], rows_[:, :, F + 2:F + 4], ev, ALU.add)
                                dve.drain()
                                dve.wait_ge(summed, b)
                                dve.scalar_tensor_tensor(score[:], score[:], 0.2, score[:], ALU.mult, ALU.max)\
                                   .then_inc(shifted, 1)
                                dve.wait_ge(weights_ready, b + 1)
                                dve.tensor_tensor(msg[v][:, :, :, 0:HD],
                                                  rows_[:, :, 0:F].rearrange("p r (h d) -> p r h d", h=HEADS),
                                                  msg[v][:, :, :, HD:HD + 1].to_broadcast(by_head), ALU.mult)
                            if weighted:
                                dve.wait_ge(summed, b)
                                dve.tensor_tensor(msg[v][:, :, 0, :], rows_[:, :, 0:F], over(ev, [P, R, F], "p (r a) -> p r a", a=1),
                                                  ALU.mult)
                            dve.drain().then_inc(messages_ready, 1)

                        def main(st, slots, b, use, first):
                            dve.wait_ge(gathered[st], (use + 1) * (16 * R))
                            if separable:
                                ev = reach[:, bass.ds(slots, R), :]
                            else:
                                ev = edge[u][:, bass.ds(slots * edge_row, R * edge_row)]
                            body(st, st % 2, b, ev, first)
                            dve.drain().then_inc(released[st], 1)

                        def last_fold(n_main, b):
                            with dve.If((n_main & 1) > 0):
                                fold(b - 1, 0)
                            with dve.If((n_main & 1) < 1):
                                fold(b - 1, 1)
                            dve.drain()

                        def extra(b, x):
                            dve.drain().then_inc(start_x_ready, 1)
                            dve.tensor_scalar(valid_x[:], slot[:, 0:R], left[:, 0:1], None, ALU.is_lt)
                            dve.drain()
                            dve.tensor_scalar(left[:], left[:], float(R), None, ALU.subtract)
                            by_slot = "p (r a) -> p r a"
                            if edge_row:
                                dve.wait_ge(edge_x_loaded, (x + 1) * 16)
                                ex = edge_x[:].rearrange("p (s h) -> p s h", s=R)
                                dve.tensor_tensor(ex, ex, over(valid_x[:], [P, R, edge_row], by_slot, a=1), ALU.mult)
                            if attend:
                                dve.tensor_scalar(pen_x[:], valid_x[:], 1.0, BIG, ALU.subtract, ALU.mult)
                                dve.drain()
                                dve.tensor_tensor(ex, ex, over(pen_x[:], [P, R, edge_row], by_slot, a=1), ALU.add)
                            if separable:
                                dve.tensor_scalar(pen_x[:], valid_x[:], 1.0, -BIG, ALU.subtract, ALU.mult)
                                dve.drain()
                                dve.tensor_tensor(reach_x[:], over(own[u][:, F:F + 2], [P, R, HEADS], "p (a h) -> p a h", a=1),
                                                  over(pen_x[:], [P, R, HEADS], by_slot, a=1), ALU.add)
                            dve.drain()
                            dve.wait_ge(gathered_x, (x + 1) * (16 * R))
                            dve.tensor_scalar(start_x[:], start_x[:], float(R), None, ALU.add)
                            dve.wait_ge(summed, b + 1)
                            body(0, 0, b, reach_x[:] if separable else edge_x[:], True)
                            if attend:
                                fold(b, 0)
                            dve.drain().then_inc(extra_done, 1)

                        bodies(dve, pair, u, main, extra, last_fold if attend else None)

                        if attend:
                            dve.reciprocal(inv[:], heads(acc[:])[:, :, HD])
                            dve.drain()
                            dve.tensor_scalar(inv[:], inv[:], filled[:, 0:1], None, ALU.mult)
                            dve.drain()
                            dve.tensor_tensor(heads(out[u][:]), heads(acc[:])[:, :, 0:HD],
                                              inv[:].rearrange("p (h a) -> p h a", a=1).to_broadcast([P, HEADS, HD]), ALU.mult)
                        if separable:
                            dve.wait_ge(tile_summed, t + 1)
                            dve.wait_ge(res_loaded[u], 16 * pair + 16)
                            dve.tensor_scalar(none[:], filled[:], -1.0, 1.0, ALU.mult, ALU.add)
                            dve.drain()
                            sums = heads(p_msg[u][:, 0:MSG])
                            dve.tensor_scalar(inv[:], sums[:, :, HD], none[:, 0:1], None, ALU.add)
                            dve.drain()
                            dve.reciprocal(inv[:], inv[:])
                            dve.drain()
                            dve.tensor_tensor(heads(high[:]), sums[:, :, 0:HD],
                                              inv[:].rearrange("p (h a) -> p h a", a=1).to_broadcast([P, HEADS, HD]), ALU.mult)
                            dve.drain()
                            dve.tensor_scalar(low[:], high[:], 0.0, None, ALU.min).then_inc(final_shifted, 1)
                            dve.scalar_tensor_tensor(high[:], high[:], 0.0, res[u][:], ALU.max, ALU.add)
                            dve.drain()
                            dve.wait_ge(final_exp, t + 1)
                            dve.scalar_tensor_tensor(out[u][:], low[:], -1.0, high[:], ALU.add, ALU.add)
                        if weighted:
                            dve.wait_ge(tile_summed, t + 1)
                            dve.wait_ge(res_loaded[u], 16 * pair + 16)
                            dve.tensor_tensor(high[:], p_msg[u][:, 0:F], bias[:], ALU.add)
                            dve.drain()
                            dve.scalar_tensor_tensor(out[u][:], high[:], 0.0, res[u][:], ALU.max, ALU.add)
                        dve.drain().then_inc(sums_free, 1)
                        dve.drain().then_inc(out_ready, 1)


def mix_phase(nc, name, src_dram, dst_dram, table, x_dram, out_dram):
    HEADS = 4
    HD = F // HEADS
    row = table.shape[1]
    with ExitStack() as ctx:
        s = Scope(nc, ctx, name)
        left_at = s.sb("left_at", [P, TILES], i32)
        right_at = s.sb("right_at", [P, TILES], i32)
        left = s.sb("left", [P, TILES, row])
        right = s.sb("right", [P, TILES, row])
        x = s.sb("x", [P, TILES, F])
        score = s.sb("score", [P, TILES, HEADS])
        alpha = s.sb("alpha", [P, TILES, HEADS])
        top = s.sb("top", [P, TILES])
        mixed = s.sb("mixed", [P, GROUP, F])
        mean = s.sb("mean", [P, GROUP, HD])
        at_loaded = s.sem("at_loaded")
        x_loaded = s.sem("x_loaded")
        gathered = [s.sem(f"gathered{g}") for g in range(GROUPS)]
        shifted = s.sem("shifted")
        exp_ready = s.sem("exp_ready")
        out_ready = s.sem("out_ready")
        stored = s.sem("stored")
        with nc.Block() as block:

            @block.sync
            def _(sp):
                for to, of in ((left_at, src_dram), (right_at, dst_dram)):
                    sp.dma_start(to[:], of[0:NP, :].rearrange("(k p) a -> p (k a)", p=P),
                                 allow_slow_non_contiguous=True).then_inc(at_loaded, 16)
                sp.dma_start(x[:], x_dram.rearrange("(k p) n -> p k n", p=P)).then_inc(x_loaded, 16)
                for g in range(GROUPS):
                    sp.wait_ge(out_ready, g + 1)
                    sp.dma_start(out_dram[g * GROUP * P:(g + 1) * GROUP * P, :].rearrange("(k p) n -> p k n", p=P),
                                 x[:, g * GROUP:(g + 1) * GROUP, :]).then_inc(stored, 16)
                sp.wait_ge(stored, 16 * GROUPS)

            @block.gpsimd
            def _(pool):
                pool.wait_ge(at_loaded, 32)
                for k in range(TILES):
                    for to, at in ((left, left_at), (right, right_at)):
                        pool.indirect_dma_start(out=to[:, k, :], out_offset=None, in_=table,
                                                in_offset=bass.IndirectOffsetOnAxis(ap=at[:, k:k + 1], axis=0))\
                            .then_inc(gathered[k // GROUP], 16)

            @block.scalar
            def _(act):
                for g in range(GROUPS):
                    t = slice(g * GROUP, (g + 1) * GROUP)
                    act.wait_ge(shifted, g + 1)
                    act.activation(alpha[:, t, :], score[:, t, :], ACT.Exp).then_inc(exp_ready, 1)

            @block.vector
            def _(dve):
                for g in range(GROUPS):
                    t = slice(g * GROUP, (g + 1) * GROUP)

                    def by_tile(v):
                        return v.rearrange("p (t a) -> p t a", a=1).to_broadcast([P, GROUP, HEADS])

                    dve.wait_ge(gathered[g], 2 * GROUP * 16)
                    dve.tensor_tensor(score[:, t, :], left[:, t, F:F + HEADS], right[:, t, F + HEADS:F + 2 * HEADS], ALU.add)
                    dve.drain()
                    dve.scalar_tensor_tensor(score[:, t, :], score[:, t, :], 0.01, score[:, t, :], ALU.mult, ALU.max)
                    dve.drain()
                    dve.tensor_reduce(top[:, t], score[:, t, :], AX.X, ALU.max)
                    dve.drain()
                    dve.tensor_tensor(score[:, t, :], score[:, t, :], by_tile(top[:, t]), ALU.subtract).then_inc(shifted, 1)
                    dve.wait_ge(exp_ready, g + 1)
                    dve.tensor_reduce(top[:, t], alpha[:, t, :], AX.X, ALU.add)
                    dve.drain()
                    dve.reciprocal(top[:, t], top[:, t])
                    dve.drain()
                    dve.tensor_tensor(alpha[:, t, :], alpha[:, t, :], by_tile(top[:, t]), ALU.mult)
                    dve.drain()
                    dve.tensor_tensor(mixed[:].rearrange("p t (h d) -> p t h d", h=HEADS),
                                      right[:, t, 0:F].rearrange("p t (h d) -> p t h d", h=HEADS),
                                      alpha[:, t, :].rearrange("p t (h a) -> p t h a", a=1).to_broadcast([P, GROUP, HEADS, HD]),
                                      ALU.mult)
                    dve.drain()
                    dve.tensor_reduce(mean[:], mixed[:].rearrange("p t (h d) -> p t d h", h=HEADS), AX.X, ALU.add)
                    dve.drain()
                    if g == 0:
                        dve.wait_ge(x_loaded, 16)
                    xh = x[:, t, :].rearrange("p t (h d) -> p t h d", h=HEADS)
                    dve.tensor_tensor(xh, xh, mean[:].rearrange("p t (a d) -> p t a d", a=1).to_broadcast([P, GROUP, HEADS, HD]),
                                      ALU.add).then_inc(out_ready, 1)


def build_program(nc, a, out):
    def dram(name, shape, dt=fp32):
        return nc.dram_tensor(name, shape, dt, kind="Internal").ap()

    ident = a["ident"]
    order = dram("order", (NP, 4), i32)
    sort_keys = dram("sort_keys", (NP,))
    kv, q = dram("kv", (NP, 2 * F)), dram("q", (NP, F))
    attended = dram("attended", (ROWS, F))
    xs = [a["x"]] + [dram(f"x{i}", (ROWS if i in (5, 7) else NP, F)) for i in range(1, 8)]
    xt = dram("xt", (NP, F + 8))
    h = dram("h", (NP, F + 4))
    hw = dram("hw", (NP, F))
    with nc.sbuf_tensor("perm", [P, ALL_TILES, 4], i32) as perm, \
            nc.sbuf_tensor("counts", [1, ALL_TILES * 8], i32) as counts:
        order_phase(nc, "order", a, a["dst_key"], order, sort_keys, perm, counts)
        projection_phase(nc, "qkv", ident, xs[0], [a["L0_gnn_Wk"], a["L0_gnn_Wv"], a["L0_gnn_Wq"]], [kv, q])
        neighbour_phase(nc, "gnn0", "attend", a, perm, counts, kv, q, None, a["src"], a["edge_attr_8"], attended)
        projection_phase(nc, "wo", ident, attended, [a["L0_gnn_Wo"]], [xs[1]], res_dram=xs[0], layernorm=False)
        ffn0(nc, a, xs[1], xs[2])
        projection_phase(nc, "xt", ident, xs[2], [a["L1_gnn_weight"]], [xt],
                         dots=((a["L1_gnn_attn_l"], 4), (a["L1_gnn_attn_r"], 4)))
        mix_phase(nc, "gnn1", a["src"], a["dst"], xt, xs[2], xs[3])
        ffn1(nc, a, xs[3], xs[4])
        projection_phase(nc, "h", ident, xs[4], [a["L2_gnn_W"]], [h], bias_dram=a["L2_gnn_b"],
                         dots=((a["L2_gnn_a_src"], 2), (a["L2_gnn_a_dst"], 2)))
        neighbour_phase(nc, "gnn2", "separable", a, perm, counts, h, h, xs[4], a["src"], None, xs[5])
        projection_phase(nc, "ffn2", ident, xs[5], [a["L2_ffn_weight"]], [xs[6]], res_dram=xs[5],
                         bias_dram=a["L2_ffn_bias"])
        projection_phase(nc, "hw", ident, xs[6], [a["L3_gnn_W"]], [hw])
        neighbour_phase(nc, "gnn3", "weighted", a, perm, counts, hw, None, xs[6], a["src"], a["edge_weight"], xs[7],
                        bias_dram=a["L3_gnn_b"])
        ffn3(nc, a, xs[7], out)


def lay_out(inputs):
    import numpy as np

    a = {k: np.asarray(v) for k, v in inputs.items()}

    def padded(v, n, value=0):
        return np.concatenate([v, np.full((n - v.shape[0],) + v.shape[1:], value, v.dtype)])

    spare = E + 2 * P
    a["x"] = padded(a["x"], NP)
    a["dst_key"] = padded(a["dst"], COLS * P, 4095)
    for k in ("src", "dst", "edge_weight"):
        a[k] = padded(a[k].reshape(E, 1), spare)
    a["edge_attr_8"] = padded(a["edge_attr_8"], spare)
    for k in ("q", "k", "v", "o"):
        a[f"L0_gnn_W{k}"] = a[f"L0_gnn_W{k}"].T
    a["L1_gnn_attn_l"] = a["L1_gnn_attn_l"].reshape(F)
    a["L1_gnn_attn_r"] = a["L1_gnn_attn_r"].reshape(F)
    a["L2_gnn_W"] = a["L2_gnn_W"].reshape(F, F).T
    a["L2_gnn_b"] = a["L2_gnn_b"].reshape(F)
    vectors = a.pop("L2_gnn_a")
    a["L2_gnn_a_src"] = vectors[:, :F // 2].reshape(F)
    a["L2_gnn_a_dst"] = vectors[:, F // 2:].reshape(F)
    a["L2_ffn_weight"] = a["L2_ffn_weight"].T
    a["ident"] = np.eye(P, dtype=np.float32)
    a["before"] = np.triu(np.ones((P, P), np.float32), 1)
    return {k: np.ascontiguousarray(v) for k, v in a.items()}


def kernel(**inputs):
    import concourse.bacc as bacc
    from concourse.bass_utils import run_bass_kernel_spmd

    nc = bacc.Bacc("TRN2", target_bir_lowering=False, num_devices=1)
    laid = lay_out(inputs)
    arrays = {f"in_{k}": v for k, v in laid.items()}
    args = {k: nc.dram_tensor(f"in_{k}", v.shape, mybir.dt.from_np(v.dtype), kind="ExternalInput").ap()
            for k, v in laid.items()}
    out = nc.dram_tensor("out_x", (NP, F), fp32, kind="ExternalOutput").ap()
    build_program(nc, args, out)
    result = run_bass_kernel_spmd(nc, [arrays], core_ids=[0])
    return result.results[0]["out_x"][:N]
```

```python
import concourse.bass as bass
from concourse import mybir
from contextlib import ExitStack

fp32 = mybir.dt.float32
i32 = mybir.dt.int32
bf16 = mybir.dt.bfloat16
ALU = mybir.AluOpType
ACT = mybir.ActivationFunctionType
AX = mybir.AxisListType

P = 128
N = 3125
F = 256
E = 103125
TILES = -(-N // P)
NP = TILES * P
GROUP = 5
GROUPS = TILES // GROUP
EPS = 1e-5


class Scope:

    def __init__(self, nc, ctx, name):
        self.nc, self.ctx, self.name, self.sems = nc, ctx, name, []
        ctx.callback(self.clear)

    def sb(self, name, shape, dt=fp32):
        return self.ctx.enter_context(self.nc.sbuf_tensor(f"{self.name}_{name}", shape, dt))

    def ps(self, name, shape, dt=fp32):
        return self.ctx.enter_context(self.nc.psum_tensor(f"{self.name}_{name}", shape, dt))

    def sem(self, name):
        self.sems.append(self.nc.alloc_semaphore(f"{self.name}_{name}"))
        return self.sems[-1]

    def clear(self):
        self.nc.clear_and_free_semaphores(self.sems)
        self.nc.all_engine_barrier()


def rows(dram, g, n):
    return dram[bass.ds(g * n, n), :].rearrange("(t p) d -> p t d", p=P)


def across(vector, n):
    return vector.rearrange("(a n) -> a n", a=1).to_broadcast([P, n])


def projection_phase(nc, name, ident_dram, a_dram, w_drams, out_drams, res_dram=None, bias_dram=None,
                     layernorm=True, dots=(), beside=None):
    nout = sum(w.shape[1] for w in w_drams)
    row = sum(o.shape[1] for o in out_drams)
    cuts = [(n, min(n + 512, nout)) for n in range(0, nout, 512)]
    with ExitStack() as ctx:
        s = Scope(nc, ctx, name)
        ident = s.sb("ident", [P, P])
        w = s.sb("w", [P, 2, nout])
        bias = s.sb("bias", [P, nout]) if bias_dram is not None else None
        dotv = [s.sb(f"dotv{i}", [P, F]) for i in range(len(dots))]
        a = s.sb("a", [P, GROUP, F])
        res = s.sb("res", [P, GROUP, F]) if res_dram is not None else None
        stats = s.sb("stats", [P, GROUP, 6])
        mv = s.sb("mv", [P, GROUP, 2])
        std = s.sb("std", [P, GROUP])
        rstd = s.sb("rstd", [P, GROUP])
        epsb = s.sb("epsb", [P, 1])
        xn = s.sb("xn", [P, GROUP, F]) if layernorm else a
        xT = s.sb("xT", [P, GROUP, 2, P])
        prod = s.sb("prod", [P, F])
        og = s.sb("og", [P, GROUP, row])
        tp = s.ps("tp", [P, 3 * 512])
        po = [s.ps(f"po{i}", [P, 1024]) for i in range(2)]
        const_loaded = s.sem("const_loaded")
        eps_set = s.sem("eps_set")
        a_loaded = s.sem("a_loaded")
        res_loaded = s.sem("res_loaded")
        var_ready = s.sem("var_ready")
        std_ready = s.sem("std_ready")
        xn_ready = s.sem("xn_ready")
        turned = s.sem("turned")
        xT_ready = s.sem("xT_ready")
        product_ready = s.sem("product_ready")
        tile_out = s.sem("tile_out")
        stored = [s.sem(f"stored{i}") for i in range(len(out_drams))]
        n_const = 1 + len(w_drams) + (bias is not None) + len(dots)
        add_more = beside(s) if beside else None

        def load(sp, g):
            sp.dma_start(a[:], rows(a_dram, g, GROUP * P)).then_inc(a_loaded, 16)

        def load_res(sp, g):
            if res is not None:
                sp.dma_start(res[:], rows(res_dram, g, GROUP * P)).then_inc(res_loaded, 16)

        def store(sp, g):
            at = 0
            for i, o in enumerate(out_drams):
                sp.dma_start(rows(o, g, GROUP * P), og[:, :, at:at + o.shape[1]]).then_inc(stored[i], 16)
                at += o.shape[1]

        with nc.Block() as block:

            @block.sync
            def _(sp):
                sp.dma_start(ident[:], ident_dram).then_inc(const_loaded, 16)
                at = 0
                for m in w_drams:
                    sp.dma_start(w[:, :, at:at + m.shape[1]], m.rearrange("(k p) n -> p k n", p=P))\
                        .then_inc(const_loaded, 16)
                    at += m.shape[1]
                if bias is not None:
                    sp.dma_start(bias[:], across(bias_dram, nout)).then_inc(const_loaded, 16)
                for v, (vec, _) in zip(dotv, dots):
                    sp.dma_start(v[:], across(vec, F)).then_inc(const_loaded, 16)
                load(sp, 0)
                load_res(sp, 0)
                with sp.Fori(0, GROUPS - 1) as g:
                    sp.wait_ge(turned, g + 1)
                    load(sp, g + 1)
                    sp.wait_ge(tile_out, GROUP * g + GROUP)
                    load_res(sp, g + 1)
                    store(sp, g)
                sp.wait_ge(tile_out, GROUP * GROUPS)
                store(sp, GROUPS - 1)
                for i in range(len(out_drams)):
                    sp.wait_ge(stored[i], 16 * GROUPS)

            @block.gpsimd
            def _(pool):
                pool.memset(epsb[:], EPS).then_inc(eps_set, 1)
                if add_more:
                    add_more(pool)

            @block.scalar
            def _(act):
                act.wait_ge(eps_set, 1)
                with act.Fori(0, GROUPS) as g:
                    if layernorm:
                        act.wait_ge(var_ready, g + 1)
                        act.activation(std[:], mv[:, :, 1], ACT.Sqrt, bias=epsb[:, 0:1]).then_inc(std_ready, 1)
                    act.wait_ge(turned, g + 1)
                    act.wait_ge(product_ready, GROUP * g)
                    act.activation(xT[:].rearrange("p t k n -> p (t k n)"), tp[:, 0:2 * GROUP * P],
                                   ACT.Copy).then_inc(xT_ready, 1)

            @block.tensor
            def _(pe):
                pe.wait_ge(const_loaded, 16 * n_const)
                with pe.Fori(0, GROUPS) as g:
                    if layernorm:
                        pe.wait_ge(xn_ready, g + 1)
                    else:
                        pe.wait_ge(a_loaded, 16 * g + 16)
                    pe.wait_ge(xT_ready, g)
                    for t in range(GROUP):
                        for k in range(2):
                            c = (t * 2 + k) * P
                            last = nc.tensor.transpose(tp[:, c:c + P], xn[:, t, k * P:(k + 1) * P], ident[:])
                    last.then_inc(turned, 1)
                    pe.wait_ge(xT_ready, g + 1)
                    for t in range(GROUP):
                        pe.wait_ge(tile_out, GROUP * g + max(t - 1, 0))
                        for n0, n1 in cuts:
                            for k in range(2):
                                last = nc.tensor.matmul(po[t % 2][:, n0:n1], xT[:, t, k, :], w[:, k, n0:n1],
                                                        start=(k == 0), stop=(k == 1))
                        last.then_inc(product_ready, 1)

            @block.vector
            def _(dve):
                dve.wait_ge(const_loaded, 16 * n_const)
                with dve.Fori(0, GROUPS) as g:
                    if layernorm:
                        dve.wait_ge(a_loaded, 16 * g + 16)
                        for t in range(GROUP):
                            dve.bn_stats(stats[:, t, :], a[:, t, :])
                        dve.drain()
                        for t in range(GROUP):
                            last = dve.bn_aggr(mv[:, t, :], stats[:, t, :])
                        last.then_inc(var_ready, 1)
                        dve.wait_ge(std_ready, g + 1)
                        dve.reciprocal(rstd[:], std[:])
                        dve.drain()
                        for t in range(GROUP):
                            last = dve.tensor_scalar(xn[:, t, :], a[:, t, :], mv[:, t, 0:1], rstd[:, t:t + 1],
                                                     ALU.subtract, ALU.mult)
                        last.then_inc(xn_ready, 1)
                    if res is not None:
                        dve.wait_ge(res_loaded, 16 * g + 16)
                    for i in range(len(out_drams)):
                        dve.wait_ge(stored[i], 16 * g)
                    for t in range(GROUP):
                        dve.wait_ge(product_ready, GROUP * g + t + 1)
                        src = po[t % 2][:, 0:nout]
                        out = og[:, t, 0:nout]
                        if bias is not None:
                            dve.tensor_tensor(out, src, bias[:], ALU.add)
                            if res is not None:
                                dve.drain()
                                dve.tensor_tensor(out, out, res[:, t, :], ALU.add)
                        elif res is not None:
                            dve.tensor_tensor(out, src, res[:, t, :], ALU.add)
                        else:
                            dve.tensor_copy(out, src)
                        at = nout
                        for v, (_, heads) in zip(dotv, dots):
                            dve.drain()
                            dve.tensor_tensor(prod[:], out, v[:], ALU.mult)
                            dve.drain()
                            dve.tensor_reduce(og[:, t, at:at + heads],
                                              prod[:].rearrange("p (h d) -> p h d", h=heads), AX.X, ALU.add)
                            at += heads
                        dve.drain().then_inc(tile_out, 1)


def moe_phase(nc, name, ident_dram, x_dram, out_dram, router, gate, w1, hidden_act, w2, w3, b3, inner_norm=None,
              beside=None):
    Ex, _, H = w1.shape
    MB = H // P
    deep = w2 is not None
    KC = 2 if deep else MB
    halves = [(0, 3), (3, GROUP)]
    routed = len(router) == 4
    with ExitStack() as ctx:
        s = Scope(nc, ctx, name)
        ident = s.sb("ident", [P, P])
        wa = s.sb("wa", [P, Ex, 2, H])
        wb = s.sb("wb", [P, Ex, 2, F]) if deep else None
        wc = s.sb("wc", [P, Ex, KC, F])
        bc = s.sb("bc", [Ex, F])
        if routed:
            rw1 = s.sb("rw1", [P, 2, P])
            rb1 = s.sb("rb1", [P, 1])
            rw2 = s.sb("rw2", [P, Ex])
            rh = s.sb("rh", [P, GROUP * P])
        else:
            rw = s.sb("rw", [P, 2, Ex])
        rb = s.sb("rb", [P, Ex])
        sizes = [MB] + [2] * deep
        hb = [s.sb(f"hb{i}", [P, Ex, m]) for i, m in enumerate(sizes)]
        hs = [s.sb(f"hs{i}", [P, Ex, m]) if len(act) == 6 else None for i, (m, act) in enumerate(zip(sizes, hidden_act))]
        bn = [[s.sb(f"bn{i}{j}", [P, Ex, m]) for j in range(4)] if len(act) == 6 else None
              for i, (m, act) in enumerate(zip(sizes, hidden_act))]
        if inner_norm:
            gamma = s.sb("gamma", [P, F])
            beta = s.sb("beta", [P, F])
        epsb = s.sb("epsb", [P, 2])
        x = s.sb("x", [P, GROUP, F])
        stats = s.sb("stats", [P, GROUP, 6])
        mv = s.sb("mv", [P, GROUP, 2])
        std = s.sb("std", [P, GROUP])
        rstd = s.sb("rstd", [P, GROUP])
        xn = s.sb("xn", [P, GROUP, F])
        xT = s.sb("xT", [P, 2, GROUP * P])
        h1 = s.sb("h1", [P, MB, GROUP * P])
        h2 = s.sb("h2", [P, 2, GROUP * P]) if deep else None
        last_h = h2 if deep else h1
        acc = s.sb("acc", [P, GROUP, F])
        before = s.sb("before", [P, Ex, Ex])
        steps = s.sb("steps", [P, Ex, Ex], i32)
        z = s.sb("z", [P, GROUP, Ex])
        z2 = s.sb("z2", [P, GROUP, Ex])
        ex = s.sb("ex", [P, GROUP, Ex])
        gates = s.sb("gates", [P, GROUP, Ex])
        sel = s.sb("sel", [P, GROUP, Ex])
        top = s.sb("top", [P, GROUP])
        total = s.sb("total", [P, GROUP])
        over = s.sb("over", [P, Ex, Ex])
        same = s.sb("same", [P, Ex, Ex])
        gT = s.sb("gT", [Ex, GROUP * P])
        pA = s.ps("pA", [P, 4, 512])
        pC = s.ps("pC", [P, 3 * 512])
        pR = s.ps("pR", [P, 512])
        const_loaded = s.sem("const_loaded")
        pool_set = s.sem("pool_set")
        bn_ready = s.sem("bn_ready")
        bn_std = s.sem("bn_std")
        x_loaded = s.sem("x_loaded")
        var_ready = s.sem("var_ready")
        std_ready = s.sem("std_ready")
        xn_ready = s.sem("xn_ready")
        turned = s.sem("turned")
        xT_ready = s.sem("xT_ready")
        router_hidden = s.sem("router_hidden")
        router_act = s.sem("router_act")
        logits_ready = s.sem("logits_ready")
        logits_read = s.sem("logits_read")
        shifted = s.sem("shifted")
        exp_ready = s.sem("exp_ready")
        gates_ready = s.sem("gates_ready")
        gT_turned = s.sem("gT_turned")
        gT_ready = s.sem("gT_ready")
        base_ready = s.sem("base_ready")
        base_added = s.sem("base_added")
        hidden_product = s.sem("hidden_product")
        hidden_ready = s.sem("hidden_ready")
        expert_out = s.sem("expert_out")
        combined = s.sem("combined")
        stored = s.sem("stored")
        HID = Ex * 2 * (MB + 2 * deep)
        banks = [(0, 2), (2, 4), (4, 5)]
        BANKS = len(banks)
        OUT = Ex * BANKS
        norms = 2 if inner_norm else 1
        exps = 2 if gate == "softmax_top2_softmax" else 1
        n_bn = sum(b is not None for b in bn)
        loads = [(ident[:], ident_dram)]
        loads += [(wa[:, e], w1[e].rearrange("(k p) n -> p k n", p=P)) for e in range(Ex)]
        loads += [(wb[:, e], w2[e].rearrange("(k p) n -> p k n", p=P)) for e in range(Ex)] if deep else []
        loads += [(wc[:, e], w3[e].rearrange("(k p) n -> p k n", p=P)) for e in range(Ex)]
        loads += [(bc[:], b3)]
        if routed:
            loads += [(rw1[:], router[0].rearrange("(k p) n -> p k n", p=P)),
                      (rb1[:], router[1].rearrange("(p a) -> p a", a=1)), (rw2[:], router[2])]
        else:
            loads += [(rw[:], router[0].rearrange("(k p) n -> p k n", p=P))]
        loads += [(rb[:], across(router[-1], Ex))]
        if inner_norm:
            loads += [(gamma[:], across(inner_norm[0], F)), (beta[:], across(inner_norm[1], F))]
        by_feature = []
        for i, act in enumerate(hidden_act):
            by_feature += [(hb[i], act[1])]
            if len(act) == 6:
                by_feature += list(zip(bn[i], act[2:]))
        for to, of in by_feature:
            loads += [(to[:, e, :], of[e].rearrange("(m p) -> p m", p=P)) for e in range(Ex)]

        add_more = beside(s) if beside else None

        with nc.Block() as block:

            @block.sync
            def _(sp):
                sp.dma_start(x[:], rows(x_dram, 0, GROUP * P)).then_inc(x_loaded, 16)
                for to, of in loads:
                    sp.dma_start(to, of, allow_slow_non_contiguous=True).then_inc(const_loaded, 16)
                with sp.Fori(0, GROUPS - 1) as g:
                    sp.wait_ge(base_added, BANKS * g + BANKS)
                    sp.dma_start(x[:], rows(x_dram, g + 1, GROUP * P)).then_inc(x_loaded, 16)
                    sp.wait_ge(combined, OUT * g + OUT)
                    sp.dma_start(rows(out_dram, g, GROUP * P), acc[:]).then_inc(stored, 16)
                sp.wait_ge(combined, OUT * GROUPS)
                sp.dma_start(rows(out_dram, GROUPS - 1, GROUP * P), acc[:]).then_inc(stored, 16)
                sp.wait_ge(stored, 16 * GROUPS)

            @block.gpsimd
            def _(pool):
                pool.memset(epsb[:, 0:1], EPS)
                pool.memset(epsb[:, 1:2], 1e-3)
                pool.iota(steps[:], [[-1, Ex], [1, Ex]], base=0, channel_multiplier=0)
                pool.drain().then_inc(pool_set, 1)
                if add_more:
                    add_more(pool)

            @block.scalar
            def _(act):
                act.wait_ge(pool_set, 1)
                act.wait_ge(const_loaded, 16 * len(loads))
                for b in bn:
                    if b is not None:
                        act.activation(b[3][:], b[3][:], ACT.Sqrt, bias=epsb[:, 1:2]).then_inc(bn_std, 1)
                if n_bn:
                    act.wait_ge(bn_ready, 1)
                with act.Fori(0, GROUPS) as g:
                    for i in range(norms):
                        act.wait_ge(var_ready, norms * g + i + 1)
                        act.activation(std[:], mv[:, :, 1], ACT.Sqrt, bias=epsb[:, 0:1]).then_inc(std_ready, 1)
                    act.wait_ge(turned, g + 1)
                    act.activation(xT[:].rearrange("p k (t n) -> p t k n", n=P),
                                   pC[:, 0:2 * GROUP * P].rearrange("p (t k n) -> p t k n", k=2, n=P),
                                   ACT.Copy).then_inc(xT_ready, 1)
                    if routed:
                        for i, (t0, t1) in enumerate(halves):
                            act.wait_ge(router_hidden, 2 * g + i + 1)
                            act.activation(rh[:, t0 * P:t1 * P], pA[:, i, 0:(t1 - t0) * P], ACT.Relu,
                                           bias=rb1[:, 0:1]).then_inc(router_act, 1)
                    for i in range(exps):
                        act.wait_ge(shifted, exps * g + i + 1)
                        act.activation(ex[:], z2[:], ACT.Exp).then_inc(exp_ready, 1)
                    j = 0
                    for e in range(Ex):
                        for layer, m_n in enumerate(sizes):
                            to = (h1, h2)[layer]
                            for t0, t1 in halves:
                                for m in range(m_n):
                                    act.wait_ge(hidden_product, HID * g + j + 1)
                                    scale = hs[layer][:, e, m:m + 1] if hs[layer] is not None else 1.0
                                    act.activation(to[:, m, t0 * P:t1 * P], pA[:, j % 4, 0:(t1 - t0) * P],
                                                   hidden_act[layer][0], bias=hb[layer][:, e, m:m + 1],
                                                   scale=scale).then_inc(hidden_ready, 1)
                                    j += 1

            @block.tensor
            def _(pe):
                pe.wait_ge(const_loaded, 16 * len(loads))
                with pe.Fori(0, GROUPS) as g:
                    pe.wait_ge(xn_ready, norms * g + norms)
                    pe.wait_ge(combined, OUT * g)
                    for t in range(GROUP):
                        for k in range(2):
                            c = (t * 2 + k) * P
                            last = nc.tensor.transpose(pC[:, c:c + P], xn[:, t, k * P:(k + 1) * P], ident[:])
                    last.then_inc(turned, 1)
                    pe.wait_ge(xT_ready, g + 1)
                    pe.wait_ge(hidden_ready, HID * g)
                    if routed:
                        for i, (t0, t1) in enumerate(halves):
                            for k in range(2):
                                last = nc.tensor.matmul(pA[:, i, 0:(t1 - t0) * P], rw1[:, k, :],
                                                        xT[:, k, t0 * P:t1 * P], start=(k == 0), stop=(k == 1))
                            last.then_inc(router_hidden, 1)
                        pe.wait_ge(router_act, 2 * g + 2)
                    pe.wait_ge(logits_read, g)
                    for t in range(GROUP):
                        if routed:
                            last = nc.tensor.matmul(pR[:, t * Ex:(t + 1) * Ex], rh[:, t * P:(t + 1) * P], rw2[:],
                                                    start=True, stop=True)
                        else:
                            for k in range(2):
                                last = nc.tensor.matmul(pR[:, t * Ex:(t + 1) * Ex], xT[:, k, t * P:(t + 1) * P],
                                                        rw[:, k, :], start=(k == 0), stop=(k == 1))
                    last.then_inc(logits_ready, 1)
                    j = 0
                    for e in range(Ex):
                        done = {}
                        for layer, m_n in enumerate(sizes):
                            w, of = ((wa, xT), (wb, h1))[layer]
                            for h, (t0, t1) in enumerate(halves):
                                if layer:
                                    pe.wait_ge(hidden_ready, HID * g + done[0, h])
                                for m in range(m_n):
                                    pe.wait_ge(hidden_ready, HID * g + max(j - 3, 0))
                                    for k in range(2):
                                        last = nc.tensor.matmul(pA[:, j % 4, 0:(t1 - t0) * P],
                                                                w[:, e, k, m * P:(m + 1) * P],
                                                                of[:, k, t0 * P:t1 * P],
                                                                start=(k == 0), stop=(k == 1))
                                    last.then_inc(hidden_product, 1)
                                    j += 1
                                done[layer, h] = j
                        if e == 0:
                            pe.wait_ge(gates_ready, g + 1)
                            for t in range(GROUP):
                                last = nc.tensor.transpose(pC[0:Ex, t * P:(t + 1) * P], gates[:, t, :], ident[:])
                            last.then_inc(gT_turned, 1)
                            pe.wait_ge(gT_ready, g + 1)
                            for t in range(GROUP):
                                last = nc.tensor.matmul(pC[:, t * F:(t + 1) * F], gT[:, t * P:(t + 1) * P], bc[:],
                                                        start=True, stop=True)
                            last.then_inc(base_ready, 1)
                        for b, (t0, t1) in enumerate(banks):
                            pe.wait_ge(hidden_ready, HID * g + done[len(sizes) - 1, 0 if t1 <= 3 else 1])
                            if e == 0:
                                pe.wait_ge(base_added, BANKS * g + b + 1)
                            else:
                                pe.wait_ge(combined, OUT * g + BANKS * (e - 1) + b + 1)
                            for t in range(t0, t1):
                                for k in range(KC):
                                    last = nc.tensor.matmul(pC[:, t * F:(t + 1) * F],
                                                            last_h[:, k, t * P:(t + 1) * P], wc[:, e, k, :],
                                                            start=(k == 0), stop=(k == KC - 1))
                            last.then_inc(expert_out, 1)

            @block.vector
            def _(dve):
                dve.wait_ge(const_loaded, 16 * len(loads))
                dve.wait_ge(pool_set, 1)
                dve.tensor_scalar(before[:], steps[:], 0.0, None, ALU.is_lt)
                if n_bn:
                    dve.wait_ge(bn_std, n_bn)
                    for i, b in enumerate(bn):
                        if b is not None:
                            g_, be_, m_, sd_ = b
                            dve.reciprocal(sd_[:], sd_[:])
                            dve.drain()
                            dve.tensor_tensor(hs[i][:], g_[:], sd_[:], ALU.mult)
                            dve.tensor_tensor(hb[i][:], hb[i][:], m_[:], ALU.subtract)
                            dve.drain()
                            dve.tensor_tensor(hb[i][:], hb[i][:], hs[i][:], ALU.mult)
                            dve.drain()
                            dve.tensor_tensor(hb[i][:], hb[i][:], be_[:], ALU.add)
                    dve.drain().then_inc(bn_ready, 1)
                else:
                    dve.drain()
                with dve.Fori(0, GROUPS) as g:
                    dve.wait_ge(x_loaded, 16 * g + 16)
                    for i in range(norms):
                        of = x if i == 0 else xn
                        for t in range(GROUP):
                            dve.bn_stats(stats[:, t, :], of[:, t, :])
                        dve.drain()
                        for t in range(GROUP):
                            last = dve.bn_aggr(mv[:, t, :], stats[:, t, :])
                        last.then_inc(var_ready, 1)
                        dve.wait_ge(std_ready, norms * g + i + 1)
                        dve.reciprocal(rstd[:], std[:])
                        dve.drain()
                        for t in range(GROUP):
                            last = dve.tensor_scalar(xn[:, t, :], of[:, t, :], mv[:, t, 0:1], rstd[:, t:t + 1],
                                                     ALU.subtract, ALU.mult)
                        if i == 1:
                            dve.drain()
                            every = [P, GROUP, F]
                            dve.tensor_tensor(xn[:], xn[:], gamma[:].rearrange("p (a n) -> p a n", a=1).to_broadcast(every), ALU.mult)
                            dve.drain()
                            last = dve.tensor_tensor(xn[:], xn[:], beta[:].rearrange("p (a n) -> p a n", a=1).to_broadcast(every), ALU.add)
                        last.then_inc(xn_ready, 1)
                        dve.wait_ge(xn_ready, norms * g + i + 1)
                    ge = [P, GROUP, Ex]

                    def wide(v):
                        return v[:].rearrange("p (t a) -> p t a", a=1).to_broadcast(ge)

                    dve.wait_ge(logits_ready, g + 1)
                    dve.tensor_tensor(z[:], pR[:, 0:GROUP * Ex].rearrange("p (t e) -> p t e", e=Ex),
                                      rb[:].rearrange("p (a e) -> p a e", a=1).to_broadcast(ge),
                                      ALU.add).then_inc(logits_read, 1)
                    dve.drain()
                    for i in range(exps):
                        if i == exps - 1 and gate != "softmax":
                            for t in range(GROUP):
                                pairs = [P, Ex, Ex]
                                zj = z[:, t, :].rearrange("p (a e) -> p a e", a=1).to_broadcast(pairs)
                                ze = z[:, t, :].rearrange("p (e a) -> p e a", a=1).to_broadcast(pairs)
                                dve.tensor_tensor(over[:], zj, ze, ALU.is_gt)
                                dve.tensor_tensor(same[:], zj, ze, ALU.is_equal)
                                dve.drain()
                                dve.tensor_tensor(same[:], same[:], before[:], ALU.mult)
                                dve.drain()
                                dve.tensor_tensor(over[:], over[:], same[:], ALU.add)
                                dve.drain()
                                dve.tensor_reduce(sel[:, t, :], over[:], AX.X, ALU.add)
                                dve.drain()
                                dve.tensor_scalar(sel[:, t, :], sel[:, t, :], 1.5, None, ALU.is_lt)
                        dve.tensor_reduce(top[:], z[:], AX.X, ALU.max)
                        dve.drain()
                        dve.tensor_tensor(z2[:], z[:], wide(top), ALU.subtract).then_inc(shifted, 1)
                        dve.wait_ge(exp_ready, exps * g + i + 1)
                        if i == exps - 1 and gate != "softmax":
                            dve.tensor_tensor(ex[:], ex[:], sel[:], ALU.mult)
                            dve.drain()
                        dve.tensor_reduce(total[:], ex[:], AX.X, ALU.add)
                        dve.drain()
                        dve.reciprocal(total[:], total[:])
                        dve.drain()
                        to = gates if i == exps - 1 else z
                        last = dve.tensor_tensor(to[:], ex[:], wide(total), ALU.mult)
                        if i < exps - 1:
                            dve.drain()
                    last.then_inc(gates_ready, 1)
                    dve.wait_ge(gT_turned, g + 1)
                    dve.tensor_copy(gT[:], pC[0:Ex, 0:GROUP * P]).then_inc(gT_ready, 1)
                    dve.wait_ge(base_ready, g + 1)
                    dve.wait_ge(stored, 16 * g)
                    for t0, t1 in banks:
                        dve.tensor_tensor(acc[:, t0:t1, :], x[:, t0:t1, :],
                                          pC[:, t0 * F:t1 * F].rearrange("p (t n) -> p t n", n=F),
                                          ALU.add).then_inc(base_added, 1)
                    dve.wait_ge(base_added, BANKS * g + BANKS)
                    for e in range(Ex):
                        for b, (t0, t1) in enumerate(banks):
                            dve.wait_ge(expert_out, OUT * g + BANKS * e + b + 1)
                            if e:
                                dve.wait_ge(combined, OUT * g + BANKS * (e - 1) + b + 1)
                            for t in range(t0, t1):
                                last = dve.scalar_tensor_tensor(acc[:, t, :], pC[:, t * F:(t + 1) * F],
                                                                gates[:, t, e:e + 1], acc[:, t, :],
                                                                ALU.mult, ALU.add)
                            last.then_inc(combined, 1)


def ffn0(nc, a, x, out, beside):
    p = "L0_ffn_"
    moe_phase(nc, "ffn0", a["ident"], x, out,
              (a[p + "router_w1"], a[p + "router_b1"], a[p + "router_w2"], a[p + "router_b2"]),
              "softmax_top2_softmax", a[p + "expert_w1"],
              [(ACT.Relu, a[p + "expert_b1"]), (ACT.Relu, a[p + "expert_b2"])],
              a[p + "expert_w2"], a[p + "expert_w3"], a[p + "expert_b3"], beside=beside)


def ffn1(nc, a, x, out, beside):
    p = "L1_ffn_"
    moe_phase(nc, "ffn1", a["ident"], x, out, (a[p + "Wr"], a[p + "br"]), "softmax", a[p + "W1"],
              [(ACT.Relu, *(a[p + n + str(i)] for n in ("b", "g", "be", "m", "v"))) for i in (1, 2)],
              a[p + "W2"], a[p + "Wo"], a[p + "bo"], beside=beside)


def ffn3(nc, a, x, out):
    p = "L3_ffn_"
    moe_phase(nc, "ffn3", a["ident"], x, out, (a[p + "Wr"], a[p + "br"]), "top2_softmax", a[p + "W1"],
              [(ACT.Gelu, a[p + "b1"])], None, a[p + "W2"], a[p + "b2"],
              inner_norm=(a[p + "gamma"], a[p + "beta"]))


R = 4
SETS = 4
SLOTS = 64
MAIN = SLOTS // R
LOOP_TILES = TILES + 1
ALL_TILES = TILES + 2
ROWS = LOOP_TILES * P
COLS = -(-E // P)
N_MAIN, N_EXTRA, BASE, EXTRA_BASE, USES = 0, 1, 2, 3, 4
NODE, START, DEGREE, TARGET = 0, 1, 2, 3


def order_phase(nc, name, a, key_dram, order_dram, keys_dram, perm, counts):
    BLOCK = 13
    BLOCKS = COLS // BLOCK
    assert BLOCKS * BLOCK == COLS and BLOCKS % 2 == 0
    with ExitStack() as ctx:
        s = Scope(nc, ctx, name)
        key = s.sb("key", [P, COLS], i32)
        part = s.sb("part", [P, COLS], i32)
        low = s.sb("low", [P, COLS], bf16)
        high = s.sb("high", [P, COLS], bf16)
        iota_low = s.sb("iota_low", [P, P], bf16)
        one_low = [s.sb(f"one_low{u}", [P, BLOCK, P], bf16) for u in range(2)]
        one_high = [s.sb(f"one_high{u}", [P, BLOCK, TILES], bf16) for u in range(2)]
        zero = s.sb("zero", [P, P], bf16)
        before = s.sb("before", [P, P])
        ones = s.sb("ones", [P, P])
        node = s.sb("node", [P, ALL_TILES], i32)
        nodef = s.sb("nodef", [P, TILES])
        target = s.sb("target", [P, ALL_TILES], i32)
        deg = s.sb("deg", [P, TILES])
        total = s.sb("total", [P, TILES])
        start = s.sb("start", [P, TILES])
        onesf = s.sb("onesf", [P, ALL_TILES])
        sortkey = s.sb("sortkey", [P, TILES])
        every = s.sb("every", [P, TILES * P])
        above = s.sb("above", [P, TILES * P], bf16)
        rankf = s.sb("rankf", [P, TILES])
        rank = s.sb("rank", [P, TILES], i32)
        record = s.sb("record", [P, TILES, 4], i32)
        spare = s.sb("spare", [P, 2, 4], i32)
        degf = s.sb("degf", [P, TILES])
        most = s.sb("most", [P, TILES])
        bodies = s.sb("bodies", [P, ALL_TILES], i32)
        work = s.sb("work", [P, ALL_TILES], i32)
        workf = s.sb("workf", [P, ALL_TILES])
        sumf = s.sb("sumf", [P, ALL_TILES])
        p_deg = s.ps("p_deg", [P, 512])
        p_sum = s.ps("p_sum", [P, 512])
        key_loaded = s.sem("key_loaded")
        const_loaded = s.sem("const_loaded")
        pool_set = s.sem("pool_set")
        zero_set = s.sem("zero_set")
        hot_ready = [s.sem(f"hot_ready{u}") for u in range(2)]
        hot_used = [s.sem(f"hot_used{u}") for u in range(2)]
        deg_summed = s.sem("deg_summed")
        deg_ready = s.sem("deg_ready")
        prefix_ready = s.sem("prefix_ready")
        sortkey_ready = s.sem("sortkey_ready")
        sortkey_stored = s.sem("sortkey_stored")
        every_loaded = s.sem("every_loaded")
        record_ready = s.sem("record_ready")
        scattered = s.sem("scattered")
        perm_loaded = s.sem("perm_loaded")
        degf_ready = s.sem("degf_ready")
        most_ready = s.sem("most_ready")
        done = s.sem("done")
        with nc.Block() as block:

            @block.sync
            def _(sp):
                sp.dma_start(key[:], key_dram.rearrange("(p t) -> p t", p=P)).then_inc(key_loaded, 16)
                sp.dma_start(before[:], a["before"]).then_inc(const_loaded, 16)
                sp.wait_ge(sortkey_ready, 1)
                sp.dma_start(keys_dram.rearrange("(k p) -> p k", p=P), sortkey[:],
                             allow_slow_non_contiguous=True).then_inc(sortkey_stored, 16)
                sp.wait_ge(sortkey_stored, 16)
                sp.dma_start(every[:], across(keys_dram, TILES * P)).then_inc(every_loaded, 16)
                sp.wait_ge(scattered, 16 * TILES)
                sp.dma_start(perm[:, 0:TILES, :], order_dram.rearrange("(k p) c -> p k c", p=P)).then_inc(perm_loaded, 16)

            @block.gpsimd
            def _(pool):
                pool.iota(iota_low[:], [[1, P]], base=0, channel_multiplier=0, allow_small_or_imprecise_dtypes=True)
                pool.iota(node[:], [[P, ALL_TILES]], base=0, channel_multiplier=1)
                pool.memset(ones[:], 1.0)
                pool.memset(onesf[:], 1.0)
                pool.memset(spare[:], 0)
                pool.drain().then_inc(pool_set, 1)
                for k in range(TILES):
                    if k == 0:
                        pool.wait_ge(record_ready, 1)
                    pool.indirect_dma_start(out=order_dram, in_=record[:, k, :], in_offset=None,
                                            out_offset=bass.IndirectOffsetOnAxis(ap=rank[:, k:k + 1], axis=0))\
                        .then_inc(scattered, 16)
                pool.wait_ge(degf_ready, 1)
                pool.partition_all_reduce(most[:], degf[:], P, bass.bass_isa.ReduceOp.max).then_inc(most_ready, 1)
                pool.wait_ge(scattered, 16 * TILES)

            @block.tensor
            def _(pe):
                pe.wait_ge(zero_set, 1)
                nc.tensor.matmul(p_deg[:, 0:TILES], zero[:], zero[:, 0:TILES], start=True, stop=False)
                with pe.Fori(0, BLOCKS // 2) as i:
                    for u in range(2):
                        pe.wait_ge(hot_ready[u], i + 1)
                        for t in range(BLOCK):
                            last = nc.tensor.matmul(p_deg[:, 0:TILES], one_low[u][:, t, :], one_high[u][:, t, :],
                                                    start=False, stop=False)
                        last.then_inc(hot_used[u], 1)
                nc.tensor.matmul(p_deg[:, 0:TILES], zero[:], zero[:, 0:TILES], start=False, stop=True).then_inc(deg_summed, 1)
                pe.wait_ge(const_loaded, 16)
                pe.wait_ge(pool_set, 1)
                pe.wait_ge(deg_ready, 1)
                nc.tensor.matmul(p_sum[:, 0:TILES], before[:], deg[:], start=True, stop=True)
                nc.tensor.matmul(p_sum[:, 256:256 + TILES], ones[:], deg[:], start=True, stop=True)\
                    .then_inc(prefix_ready, 1)

            @block.vector
            def _(dve):
                dve.memset(zero[:], 0.0).then_inc(zero_set, 1)
                dve.wait_ge(key_loaded, 16)
                dve.wait_ge(pool_set, 1)
                dve.tensor_scalar(part[:], key[:], P - 1, None, ALU.bitwise_and)
                dve.drain()
                dve.tensor_copy(low[:], part[:])
                dve.drain()
                dve.tensor_scalar(part[:], key[:], 7, None, ALU.logical_shift_right)
                dve.drain()
                dve.tensor_copy(high[:], part[:])
                dve.drain()
                with dve.Fori(0, BLOCKS // 2) as i:
                    for u in range(2):
                        dve.wait_ge(hot_used[u], i)
                        at = bass.ds((i * 2 + u) * BLOCK, BLOCK)
                        dve.tensor_tensor(one_low[u][:], iota_low[:].rearrange("p (a n) -> p a n", a=1).to_broadcast([P, BLOCK, P]),
                                          low[:, at].rearrange("p (t a) -> p t a", a=1).to_broadcast([P, BLOCK, P]),
                                          ALU.is_equal)
                        dve.tensor_tensor(one_high[u][:], iota_low[:, 0:TILES].rearrange("p (a n) -> p a n", a=1).to_broadcast([P, BLOCK, TILES]),
                                          high[:, at].rearrange("p (t a) -> p t a", a=1).to_broadcast([P, BLOCK, TILES]),
                                          ALU.is_equal)
                        dve.drain().then_inc(hot_ready[u], 1)
                dve.wait_ge(deg_summed, 1)
                dve.tensor_copy(deg[:], p_deg[:, 0:TILES]).then_inc(deg_ready, 1)
                dve.tensor_copy(nodef[:], node[:, 0:TILES])
                dve.drain()
                dve.tensor_scalar(sortkey[:], deg[:], 4000.0, 4096.0, ALU.min, ALU.mult)
                dve.drain()
                dve.tensor_tensor(sortkey[:], sortkey[:], nodef[:], ALU.add)
                dve.drain().then_inc(sortkey_ready, 1)
                dve.wait_ge(prefix_ready, 1)
                dve.tensor_copy(total[:], p_sum[:, 256:256 + TILES])
                dve.drain()
                dve.tensor_tensor_scan(start[:], onesf[:, 0:TILES], total[:], 0.0, ALU.mult, ALU.add)
                dve.drain()
                dve.tensor_tensor(start[:], start[:], total[:], ALU.subtract)
                dve.drain()
                dve.tensor_tensor(start[:], start[:], p_sum[:, 0:TILES], ALU.add)
                dve.drain()
                dve.tensor_copy(record[:, :, NODE], node[:, 0:TILES])
                dve.tensor_copy(record[:, :, START], start[:])
                dve.tensor_copy(record[:, :, DEGREE], deg[:])
                dve.tensor_copy(record[:, :, TARGET], node[:, 0:TILES])
                dve.wait_ge(every_loaded, 16)
                for k in range(TILES):
                    dve.tensor_scalar(above[:], every[:], sortkey[:, k:k + 1], 0.0, ALU.is_gt, ALU.add,
                                      accum_out=rankf[:, k:k + 1])
                    dve.drain()
                dve.tensor_copy(rank[:], rankf[:])
                dve.drain().then_inc(record_ready, 1)
                for k in range(2):
                    dve.tensor_copy(perm[:, TILES + k, NODE:NODE + 1], node[:, 0:1])
                    dve.tensor_copy(perm[:, TILES + k, START:TARGET], spare[:, k, START:TARGET])
                    dve.tensor_copy(perm[:, TILES + k, TARGET:TARGET + 1], node[:, TILES:TILES + 1])
                dve.wait_ge(perm_loaded, 16)
                dve.tensor_copy(degf[:], perm[:, 0:TILES, DEGREE]).then_inc(degf_ready, 1)
                dve.wait_ge(most_ready, 1)
                dve.memset(workf[:], 1.0)
                dve.drain()
                dve.tensor_scalar(workf[:, 0:TILES], most[:], float(R - 1), float(R), ALU.add, ALU.max)
                dve.drain()
                dve.tensor_scalar(workf[:, TILES:ALL_TILES], workf[:, TILES:ALL_TILES], float(R - 1), None, ALU.add)
                dve.drain()
                dve.tensor_copy(bodies[:], workf[:])
                dve.drain()
                dve.tensor_scalar(bodies[:], bodies[:], R.bit_length() - 1, None, ALU.logical_shift_right)
                dve.drain()
                table = counts[:].rearrange("p (k c) -> p k c", c=8)
                dve.tensor_scalar(table[:, :, N_MAIN], bodies[0:1, :], float(MAIN), None, ALU.min)
                dve.tensor_scalar(table[:, :, N_EXTRA], bodies[0:1, :], float(MAIN), 0.0, ALU.subtract, ALU.max)
                dve.drain()

                def sum_before(to, of):
                    dve.tensor_copy(workf[0:1, :], of)
                    dve.drain()
                    dve.tensor_tensor_scan(sumf[0:1, :], onesf[0:1, :], workf[0:1, :], 0.0, ALU.mult, ALU.add)
                    dve.drain()
                    dve.tensor_tensor(sumf[0:1, :], sumf[0:1, :], workf[0:1, :], ALU.subtract)
                    dve.drain()
                    dve.tensor_copy(to, sumf[0:1, :])
                    dve.drain()

                sum_before(table[:, :, BASE], bodies[0:1, :])
                sum_before(table[:, :, EXTRA_BASE], table[:, :, N_EXTRA])
                for u in range(SETS):
                    dve.tensor_scalar(work[0:1, :], table[:, :, N_MAIN], float(SETS - 1 - u), None, ALU.add)
                    dve.drain()
                    dve.tensor_scalar(work[0:1, :], work[0:1, :], SETS.bit_length() - 1, None, ALU.logical_shift_right)
                    dve.drain()
                    sum_before(table[:, :, USES + u], work[0:1, :])
                dve.drain().then_inc(done, 1)
                dve.wait_ge(done, 1)


def neighbour_phase(nc, name, kind, a, perm, counts, table, own_table, res_table, src_dram, edge_dram, out_dram,
                    bias_dram=None, tables=()):
    attend, separable, weighted = (kind == k for k in ("attend", "separable", "weighted"))
    row = table.shape[1]
    own_row = own_table.shape[1] if own_table is not None else 0
    edge_row = edge_dram.shape[1] if edge_dram is not None else 0
    HEADS = {"attend": 8, "separable": 2, "weighted": 1}[kind]
    HD = F // HEADS
    MSG = HEADS * (HD + (not weighted))
    BIG = 1e30
    with ExitStack() as ctx:
        s = Scope(nc, ctx, name)
        node_at = [s.sb(f"node_at{u}", [P, 4], i32) for u in range(2)]
        target_at = [s.sb(f"target_at{u}", [P, 1], i32) for u in range(2)]
        index = [s.sb(f"index{u}", [P, SLOTS], i32) for u in range(2)]
        edge = [s.sb(f"edge{u}", [P, SLOTS * edge_row]) for u in range(2)] if edge_row else None
        own = [s.sb(f"own{u}", [P, own_row]) for u in range(2)] if own_row else None
        res = [s.sb(f"res{u}", [P, F]) for u in range(2)] if res_table is not None else None
        got = [s.sb(f"got{i}", [P, R, row]) for i in range(SETS)]
        start_x = s.sb("start_x", [P, 1], i32)
        index_x = s.sb("index_x", [P, R], i32)
        edge_x = s.sb("edge_x", [P, R * edge_row]) if edge_row else None
        slot = s.sb("slot", [P, SLOTS])
        degree = s.sb("degree", [P, 1])
        valid = s.sb("valid", [P, SLOTS])
        valid_x = s.sb("valid_x", [P, R])
        left = s.sb("left", [P, 1])
        filled = s.sb("filled", [P, 1])
        out = [s.sb(f"out{u}", [P, F]) for u in range(2)]
        msg = [s.sb(f"msg{v}", [P, R, HEADS, HD + (not weighted)]) for v in range(2)]
        ident = s.sb("ident", [P, P])
        if attend:
            q = s.sb("q", [P, F])
            prod = s.sb("prod", [P, R, F])
            score = s.sb("score", [P, R + 1, HEADS])
            peak = s.sb("peak", [P, HEADS])
            pen = s.sb("pen", [P, SLOTS])
            pen_x = s.sb("pen_x", [P, R])
            acc = s.sb("acc", [P, MSG])
            weight = [s.sb(f"weight{v}", [P, R + 1, HEADS]) for v in range(2)]
            inv = s.sb("inv", [P, HEADS])
        if separable:
            score = s.sb("score", [P, R, HEADS])
            reach = s.sb("reach", [P, SLOTS, HEADS])
            reach_x = s.sb("reach_x", [P, R, HEADS])
            pen = s.sb("pen", [P, SLOTS])
            pen_x = s.sb("pen_x", [P, R])
            inv = s.sb("inv", [P, HEADS])
            low = s.sb("low", [P, F])
            high = s.sb("high", [P, F])
            none = s.sb("none", [P, 1])
        if weighted:
            bias = s.sb("bias", [P, F])
            high = s.sb("high", [P, F])
        zero = s.sb("zero", [P, MSG])
        p_msg = [s.ps(f"p_msg{u}", [P, 512]) for u in range(2)]
        const_loaded = s.sem("const_loaded")
        pool_set = s.sem("pool_set")
        node_ready = s.sem("node_ready")
        index_loaded = [s.sem(f"index_loaded{u}") for u in range(2)]
        edge_loaded = [s.sem(f"edge_loaded{u}") for u in range(2)]
        own_loaded = [s.sem(f"own_loaded{u}") for u in range(2)]
        res_loaded = [s.sem(f"res_loaded{u}") for u in range(2)]
        sums_free = s.sem("sums_free")
        gathered = [s.sem(f"gathered{i}") for i in range(SETS)]
        released = [s.sem(f"released{i}") for i in range(SETS)]
        extra_done = s.sem("extra_done")
        start_x_ready = s.sem("start_x_ready")
        index_x_loaded = s.sem("index_x_loaded")
        edge_x_loaded = s.sem("edge_x_loaded")
        gathered_x = s.sem("gathered_x")
        pool_waited = s.sem("pool_waited")
        shifted = s.sem("shifted")
        weights_ready = s.sem("weights_ready")
        messages_ready = s.sem("messages_ready")
        summed = s.sem("summed")
        zeroed = s.sem("zeroed")
        tile_summed = s.sem("tile_summed")
        final_shifted = s.sem("final_shifted")
        final_exp = s.sem("final_exp")
        out_ready = s.sem("out_ready")
        scattered = [s.sem(f"scattered{u}") for u in range(2)]

        zeros, zero_tables = fill_zero(nc, s, pool_set)

        def rows_at(ap):
            return bass.IndirectOffsetOnAxis(ap=ap, axis=0)

        def count(eng, t, column, low, high):
            return eng.value_load(counts[0:1, bass.ds(t * 8 + column, 1)], min_val=low, max_val=high)

        def bodies(eng, pair, u, main, extra, between=None):
            t = pair * 2 + u
            n_main = count(eng, t, N_MAIN, 1, MAIN)
            n_extra = count(eng, t, N_EXTRA, 0, E)
            base = count(eng, t, BASE, 0, E)
            extra_base = count(eng, t, EXTRA_BASE, 0, E)
            uses = [count(eng, t, USES + i, 0, E) for i in range(SETS)] if eng is nc.vector else None
            main(0, 0, base, uses[0] if uses else None, True)
            for st in range(1, SETS):
                with eng.If(n_main > st):
                    main(st, st * R, base + st, uses[st] if uses else None, False)
            with eng.If(n_main > SETS):
                with eng.Fori(1, (n_main + SETS - 1) // SETS) as i:
                    for st in range(SETS):
                        with eng.If(i * SETS + st < n_main):
                            main(st, (i * SETS + st) * R, base + i * SETS + st, uses[st] + i if uses else None, False)
            if between:
                between(n_main, base + n_main)
            with eng.If(n_extra > 0):
                with eng.Fori(0, n_extra) as i:
                    extra(base + n_main + i, extra_base + i)

        with nc.Block() as block:

            @block.sync
            def _(sp):
                sp.dma_start(ident[:], a["ident"]).then_inc(const_loaded, 16)
                if weighted:
                    sp.dma_start(bias[:], across(bias_dram, F)).then_inc(const_loaded, 16)
                zero_tables(sp, tables)

            @block.gpsimd
            def _(pool):
                pool.iota(slot[:], [[1, SLOTS]], base=0, channel_multiplier=0, allow_small_or_imprecise_dtypes=True)
                pool.memset(zero[:], 0.0)
                pool.memset(zeros[:], 0.0)
                pool.drain().then_inc(pool_set, 1)

                def wait_apart(sem, value):
                    pool.wait_ge(sem, value)
                    pool.sem_inc(pool_waited, 1)

                def prefetch(u):
                    node = node_at[u][:, NODE:NODE + 1]
                    start = node_at[u][:, START:START + 1]
                    pool.indirect_dma_start(out=index[u][:], out_offset=None, in_=src_dram, in_offset=rows_at(start))\
                        .then_inc(index_loaded[u], 16)
                    if edge_row:
                        pool.indirect_dma_start(out=edge[u][:], out_offset=None, in_=edge_dram, in_offset=rows_at(start))\
                            .then_inc(edge_loaded[u], 16)
                    if own_row:
                        pool.indirect_dma_start(out=own[u][:], out_offset=None, in_=own_table, in_offset=rows_at(node))\
                            .then_inc(own_loaded[u], 16)
                    if res is not None:
                        pool.indirect_dma_start(out=res[u][:], out_offset=None, in_=res_table, in_offset=rows_at(node))\
                            .then_inc(res_loaded[u], 16)

                def scatter(u):
                    pool.indirect_dma_start(out=out_dram, in_=out[u][:], in_offset=None,
                                            out_offset=rows_at(target_at[u][:, 0:1])).then_inc(scattered[u], 16)

                pool.wait_ge(node_ready, 1)
                prefetch(0)
                with pool.Fori(0, LOOP_TILES // 2) as pair:
                    for u in range(2):
                        t = pair * 2 + u
                        n_main = count(pool, t, N_MAIN, 1, MAIN)
                        uses = [count(pool, t, USES + i, 0, E) for i in range(SETS)]
                        pool.wait_ge(index_loaded[u], 16 * pair + 16)

                        def gather(j):
                            st = j % SETS
                            wait_apart(released[st], uses[st] + j // SETS)
                            for r in range(R):
                                pool.indirect_dma_start(out=got[st][:, r, :], out_offset=None, in_=table,
                                                        in_offset=rows_at(index[u][:, j * R + r:j * R + r + 1]))\
                                    .then_inc(gathered[st], 16)

                        for j in range(MAIN):
                            if j == 0:
                                gather(j)
                            else:
                                with pool.If(n_main > j):
                                    gather(j)
                            if j == 4:
                                wait_apart(node_ready, t + 2)
                                prefetch(1 - u)
                        n_extra = count(pool, t, N_EXTRA, 0, E)
                        with pool.If(n_extra > 0):
                            extra_base = count(pool, t, EXTRA_BASE, 0, E)
                            with pool.Fori(0, n_extra) as i:
                                wait_apart(start_x_ready, extra_base + i + 1)
                                pool.indirect_dma_start(out=index_x[:], out_offset=None, in_=src_dram,
                                                        in_offset=rows_at(start_x[:, 0:1])).then_inc(index_x_loaded, 16)
                                if edge_row:
                                    pool.indirect_dma_start(out=edge_x[:], out_offset=None, in_=edge_dram,
                                                            in_offset=rows_at(start_x[:, 0:1])).then_inc(edge_x_loaded, 16)
                                wait_apart(index_x_loaded, (extra_base + i + 1) * 16)
                                for r in range(R):
                                    pool.indirect_dma_start(out=got[0][:, r, :], out_offset=None, in_=table,
                                                            in_offset=rows_at(index_x[:, r:r + 1])).then_inc(gathered_x, 16)
                            wait_apart(extra_done, extra_base + n_extra)
                        if u == 0:
                            with pool.If(pair > 0):
                                wait_apart(out_ready, t)
                                scatter(1)
                        else:
                            wait_apart(out_ready, t)
                            scatter(0)
                pool.wait_ge(out_ready, LOOP_TILES)
                scatter(1)
                for u in range(2):
                    pool.wait_ge(scattered[u], 16 * (LOOP_TILES // 2))
                pool.wait_ge(index_loaded[0], 16 * (LOOP_TILES // 2) + 16)
                if edge_row:
                    pool.wait_ge(edge_loaded[0], 16 * (LOOP_TILES // 2) + 16)
                if own_row:
                    pool.wait_ge(own_loaded[0], 16 * (LOOP_TILES // 2) + 16)
                if res is not None:
                    pool.wait_ge(res_loaded[0], 16 * (LOOP_TILES // 2) + 16)

            @block.scalar
            def _(act):
                if not weighted:
                    with act.Fori(0, LOOP_TILES // 2) as pair:
                        for u in range(2):

                            def body(b, v):
                                act.wait_ge(shifted, b + 1)
                                if attend:
                                    act.activation(weight[v][:], score[:], ACT.Exp).then_inc(weights_ready, 1)
                                else:
                                    act.activation(msg[v][:, :, :, HD], score[:], ACT.Exp, scale=-1.0)\
                                       .then_inc(weights_ready, 1)

                            bodies(act, pair, u, lambda st, slots, b, use, first: body(b, st % 2), lambda b, x: body(b, 0))
                            if separable:
                                act.wait_ge(final_shifted, pair * 2 + u + 1)
                                act.activation(low[:], low[:], ACT.Exp).then_inc(final_exp, 1)

            @block.tensor
            def _(pe):
                pe.wait_ge(const_loaded, 16 + 16 * weighted)
                pe.wait_ge(pool_set, 1)
                with pe.Fori(0, LOOP_TILES // 2) as pair:
                    for u in range(2):
                        if not attend:
                            pe.wait_ge(sums_free, pair * 2 + u + 1)
                            nc.tensor.matmul(p_msg[u][:, 0:MSG], ident[:], zero[:], start=True, stop=False)

                        def body(b, v):
                            pe.wait_ge(messages_ready, b + 1)
                            for r in range(R):
                                last = nc.tensor.matmul(p_msg[0 if attend else u][:, 0:MSG], ident[:],
                                                        msg[v][:, r].rearrange("p h d -> p (h d)"),
                                                        start=attend and r == 0, stop=attend and r == R - 1)
                            last.then_inc(summed, 1)

                        bodies(pe, pair, u, lambda st, slots, b, use, first: body(b, st % 2), lambda b, x: body(b, 0))
                        if not attend:
                            nc.tensor.matmul(p_msg[u][:, 0:MSG], ident[:], zero[:], start=False, stop=True)\
                                .then_inc(tile_summed, 1)

            @block.vector
            def _(dve):
                def heads(ap, n=HEADS):
                    return ap.rearrange("p (h d) -> p h d", h=n)

                def over(ap, shape, pattern, **kw):
                    return ap.rearrange(pattern, **kw).to_broadcast(shape)

                def set_node(u, t):
                    dve.tensor_copy(node_at[u][:].rearrange("p (a c) -> p a c", a=1), perm[:, bass.ds(t, 1), :])\
                        .then_inc(node_ready, 1)

                dve.wait_ge(pool_set, 1)
                dve.wait_ge(const_loaded, 16 + 16 * weighted)
                set_node(0, 0)
                dve.sem_inc(sums_free, 2)
                dve.sem_inc(summed, 1)
                with dve.Fori(0, LOOP_TILES // 2) as pair:
                    for u in range(2):
                        t = pair * 2 + u
                        dve.wait_ge(node_ready, t + 1)
                        dve.wait_ge(index_loaded[u], 16 * pair + 16)
                        dve.tensor_copy(degree[:], node_at[u][:, DEGREE:DEGREE + 1])
                        dve.wait_ge(scattered[u], 16 * pair)
                        dve.tensor_copy(target_at[u][:], node_at[u][:, TARGET:TARGET + 1])
                        if u == 0:
                            dve.wait_ge(index_loaded[1], 16 * pair)
                        set_node(1 - u, t + 1)
                        dve.drain()
                        dve.tensor_scalar(valid[:], slot[:], degree[:, 0:1], None, ALU.is_lt)
                        dve.tensor_scalar(filled[:], degree[:], 0.0, None, ALU.is_gt)
                        dve.tensor_scalar(left[:], degree[:], float(SLOTS), None, ALU.subtract)
                        dve.tensor_scalar(start_x[:], node_at[u][:, START:START + 1], float(SLOTS), float(E),
                                          ALU.add, ALU.min)
                        dve.drain()
                        if edge_row:
                            dve.wait_ge(edge_loaded[u], 16 * pair + 16)
                        if own_row:
                            dve.wait_ge(own_loaded[u], 16 * pair + 16)
                        if attend:
                            ev = edge[u][:].rearrange("p (s h) -> p s h", h=HEADS)
                            dve.tensor_tensor(ev, ev, over(valid[:], [P, SLOTS, HEADS], "p (s a) -> p s a", a=1), ALU.mult)
                            dve.tensor_scalar(pen[:], valid[:], 1.0, BIG, ALU.subtract, ALU.mult)
                            dve.tensor_scalar(q[:], own[u][:], float(HD) ** 0.5, None, ALU.mult)
                            dve.memset(acc[:], 0.0)
                            dve.memset(score[:, R, :], -BIG)
                            dve.drain()
                            dve.tensor_tensor(ev, ev, over(pen[:], [P, SLOTS, HEADS], "p (s a) -> p s a", a=1), ALU.add)
                            dve.drain()
                        if separable:
                            dve.tensor_scalar(pen[:], valid[:], 1.0, -BIG, ALU.subtract, ALU.mult)
                            dve.drain()
                            dve.tensor_tensor(reach[:], over(own[u][:, F:F + 2], [P, SLOTS, HEADS], "p (a h) -> p a h", a=1),
                                              over(pen[:], [P, SLOTS, HEADS], "p (s a) -> p s a", a=1), ALU.add)
                            dve.drain()
                        if weighted:
                            dve.tensor_tensor(edge[u][:], edge[u][:], valid[:], ALU.mult)
                            dve.drain()

                        def fold(b, v):
                            dve.tensor_tensor(heads(acc[:]), heads(acc[:]),
                                              over(weight[v][:, R, :], [P, HEADS, HD + 1], "p (h a) -> p h a", a=1), ALU.mult)
                            dve.drain()
                            dve.wait_ge(summed, b + 2)
                            dve.tensor_tensor(acc[:], acc[:], p_msg[0][:, 0:MSG], ALU.add)

                        def body(st, v, b, ev, first):
                            rows_ = got[st]
                            by_head = [P, R, HEADS, HD]
                            if attend:
                                dve.tensor_tensor(prod[:], rows_[:, :, 0:F], over(q[:], [P, R, F], "p (a n) -> p a n", a=1), ALU.mult)
                                dve.drain()
                                dve.tensor_reduce(score[:, 0:R, :].rearrange("p r h -> p (r h)"),
                                                  prod[:].rearrange("p r (h d) -> p (r h) d", d=HD), AX.X, ALU.add)
                                dve.drain()
                                flat = score[:, 0:R, :].rearrange("p r h -> p (r h)")
                                dve.tensor_tensor(flat, flat, ev, ALU.add)
                                dve.drain()
                                dve.tensor_reduce(peak[:], score[:].rearrange("p r h -> p h r"), AX.X, ALU.max)
                                dve.drain()
                                dve.tensor_tensor(score[:], score[:], over(peak[:], [P, R + 1, HEADS], "p (a h) -> p a h", a=1),
                                                  ALU.subtract).then_inc(shifted, 1)
                                if not first:
                                    fold(b - 1, 1 - v)
                                dve.wait_ge(weights_ready, b + 1)
                                dve.tensor_copy(score[:, R, :], peak[:])
                                dve.tensor_copy(msg[v][:, :, :, HD], weight[v][:, 0:R, :])
                                dve.tensor_tensor(msg[v][:, :, :, 0:HD],
                                                  rows_[:, :, F:2 * F].rearrange("p r (h d) -> p r h d", h=HEADS),
                                                  weight[v][:, 0:R, :].rearrange("p r (h a) -> p r h a", a=1).to_broadcast(by_head),
                                                  ALU.mult)
                            if separable:
                                dve.tensor_tensor(score[:], rows_[:, :, F + 2:F + 4], ev, ALU.add)
                                dve.drain()
                                dve.wait_ge(summed, b)
                                dve.scalar_tensor_tensor(score[:], score[:], 0.2, score[:], ALU.mult, ALU.max)\
                                   .then_inc(shifted, 1)
                                dve.wait_ge(weights_ready, b + 1)
                                dve.tensor_tensor(msg[v][:, :, :, 0:HD],
                                                  rows_[:, :, 0:F].rearrange("p r (h d) -> p r h d", h=HEADS),
                                                  msg[v][:, :, :, HD:HD + 1].to_broadcast(by_head), ALU.mult)
                            if weighted:
                                dve.wait_ge(summed, b)
                                dve.tensor_tensor(msg[v][:, :, 0, :], rows_[:, :, 0:F], over(ev, [P, R, F], "p (r a) -> p r a", a=1),
                                                  ALU.mult)
                            dve.drain().then_inc(messages_ready, 1)

                        def main(st, slots, b, use, first):
                            dve.wait_ge(gathered[st], (use + 1) * (16 * R))
                            if separable:
                                ev = reach[:, bass.ds(slots, R), :]
                            else:
                                ev = edge[u][:, bass.ds(slots * edge_row, R * edge_row)]
                            body(st, st % 2, b, ev, first)
                            dve.drain().then_inc(released[st], 1)

                        def last_fold(n_main, b):
                            with dve.If((n_main & 1) > 0):
                                fold(b - 1, 0)
                            with dve.If((n_main & 1) < 1):
                                fold(b - 1, 1)
                            dve.drain()

                        def extra(b, x):
                            dve.drain().then_inc(start_x_ready, 1)
                            dve.tensor_scalar(valid_x[:], slot[:, 0:R], left[:, 0:1], None, ALU.is_lt)
                            dve.drain()
                            dve.tensor_scalar(left[:], left[:], float(R), None, ALU.subtract)
                            by_slot = "p (r a) -> p r a"
                            if edge_row:
                                dve.wait_ge(edge_x_loaded, (x + 1) * 16)
                                ex = edge_x[:].rearrange("p (s h) -> p s h", s=R)
                                dve.tensor_tensor(ex, ex, over(valid_x[:], [P, R, edge_row], by_slot, a=1), ALU.mult)
                            if attend:
                                dve.tensor_scalar(pen_x[:], valid_x[:], 1.0, BIG, ALU.subtract, ALU.mult)
                                dve.drain()
                                dve.tensor_tensor(ex, ex, over(pen_x[:], [P, R, edge_row], by_slot, a=1), ALU.add)
                            if separable:
                                dve.tensor_scalar(pen_x[:], valid_x[:], 1.0, -BIG, ALU.subtract, ALU.mult)
                                dve.drain()
                                dve.tensor_tensor(reach_x[:], over(own[u][:, F:F + 2], [P, R, HEADS], "p (a h) -> p a h", a=1),
                                                  over(pen_x[:], [P, R, HEADS], by_slot, a=1), ALU.add)
                            dve.drain()
                            dve.wait_ge(gathered_x, (x + 1) * (16 * R))
                            dve.tensor_scalar(start_x[:], start_x[:], float(R), float(E), ALU.add, ALU.min)
                            dve.wait_ge(summed, b + 1)
                            body(0, 0, b, reach_x[:] if separable else edge_x[:], True)
                            if attend:
                                fold(b, 0)
                            dve.drain().then_inc(extra_done, 1)

                        bodies(dve, pair, u, main, extra, last_fold if attend else None)

                        if attend:
                            dve.reciprocal(inv[:], heads(acc[:])[:, :, HD])
                            dve.drain()
                            dve.tensor_scalar(inv[:], inv[:], filled[:, 0:1], None, ALU.mult)
                            dve.drain()
                            dve.tensor_tensor(heads(out[u][:]), heads(acc[:])[:, :, 0:HD],
                                              inv[:].rearrange("p (h a) -> p h a", a=1).to_broadcast([P, HEADS, HD]), ALU.mult)
                        if separable:
                            dve.wait_ge(tile_summed, t + 1)
                            dve.wait_ge(res_loaded[u], 16 * pair + 16)
                            dve.tensor_scalar(none[:], filled[:], -1.0, 1.0, ALU.mult, ALU.add)
                            dve.drain()
                            sums = heads(p_msg[u][:, 0:MSG])
                            dve.tensor_scalar(inv[:], sums[:, :, HD], none[:, 0:1], None, ALU.add)
                            dve.drain()
                            dve.reciprocal(inv[:], inv[:])
                            dve.drain()
                            dve.tensor_tensor(heads(high[:]), sums[:, :, 0:HD],
                                              inv[:].rearrange("p (h a) -> p h a", a=1).to_broadcast([P, HEADS, HD]), ALU.mult)
                            dve.drain()
                            dve.tensor_scalar(low[:], high[:], 0.0, None, ALU.min).then_inc(final_shifted, 1)
                            dve.scalar_tensor_tensor(high[:], high[:], 0.0, res[u][:], ALU.max, ALU.add)
                            dve.drain()
                            dve.wait_ge(final_exp, t + 1)
                            dve.scalar_tensor_tensor(out[u][:], low[:], -1.0, high[:], ALU.add, ALU.add)
                        if weighted:
                            dve.wait_ge(tile_summed, t + 1)
                            dve.wait_ge(res_loaded[u], 16 * pair + 16)
                            dve.tensor_tensor(high[:], p_msg[u][:, 0:F], bias[:], ALU.add)
                            dve.drain()
                            dve.scalar_tensor_tensor(out[u][:], high[:], 0.0, res[u][:], ALU.max, ALU.add)
                        dve.drain().then_inc(sums_free, 1)
                        dve.drain().then_inc(out_ready, 1)


CAP = 3e38


def fill_zero(nc, s, ready):
    zeros = s.sb("zeros", [P, NP])
    zeros_stored = s.sem("zeros_stored")

    def run(sp, tables):
        sp.wait_ge(ready, 1)
        for m in tables:
            for k in range(TILES):
                sp.dma_start(m[k * P * NP:(k + 1) * P * NP, :].rearrange("(p n) a -> p (n a)", p=P), zeros[:])\
                    .then_inc(zeros_stored, 16)
        sp.wait_ge(zeros_stored, 16 * TILES * len(tables))

    return zeros, run


def cells_phase(nc, name, perm, src_dram, weight_dram, cell_count, cell_weight, taken, weights):
    with ExitStack() as ctx:
        s = Scope(nc, ctx, name)
        slot = s.sb("slot", [P, SLOTS])
        nodef = s.sb("nodef", [P, TILES])
        rowf = s.sb("rowf", [P, TILES])
        degf = s.sb("degf", [P, TILES])
        pool_set = s.sem("pool_set")
        index_loaded = s.sem("index_loaded")
        weight_loaded = s.sem("weight_loaded")
        with nc.Block() as block:

            @block.gpsimd
            def _(pool):
                pool.iota(slot[:], [[1, SLOTS]], base=0, channel_multiplier=0, allow_small_or_imprecise_dtypes=True)
                pool.drain().then_inc(pool_set, 1)
                for to, of, sem in ((cell_weight, src_dram, index_loaded), (weights, weight_dram, weight_loaded)):
                    for k in range(TILES):
                        pool.indirect_dma_start(out=to[:, k, :], out_offset=None, in_=of,
                                                in_offset=bass.IndirectOffsetOnAxis(ap=perm[:, k, START:START + 1], axis=0))\
                            .then_inc(sem, 16)

            @block.vector
            def _(dve):
                def by_tile(v):
                    return v.rearrange("p (t a) -> p t a", a=1).to_broadcast([P, TILES, SLOTS])

                dve.tensor_copy(nodef[:], perm[:, 0:TILES, NODE])
                dve.tensor_copy(degf[:], perm[:, 0:TILES, DEGREE])
                dve.drain()
                dve.tensor_scalar(rowf[:], nodef[:], float(NP), None, ALU.mult)
                dve.wait_ge(pool_set, 1)
                dve.tensor_tensor(taken[:], slot[:].rearrange("p (a s) -> p a s", a=1).to_broadcast([P, TILES, SLOTS]),
                                  by_tile(degf[:]), ALU.is_lt)
                dve.drain()
                dve.wait_ge(index_loaded, 16 * TILES)
                dve.tensor_tensor(cell_count[:], cell_weight[:], by_tile(rowf[:]), ALU.add)
                dve.drain()
                dve.scalar_tensor_tensor(cell_weight[:], cell_weight[:], float(NP), by_tile(nodef[:]), ALU.mult, ALU.add)
                dve.wait_ge(weight_loaded, 16 * TILES)
                dve.tensor_tensor(weights[:], weights[:], taken[:], ALU.mult)
                dve.drain()


def spill_phase(nc, name, perm, counts, src_dram, weight_dram, count_table, weight_table):
    with ExitStack() as ctx:
        s = Scope(nc, ctx, name)
        record = s.sb("record", [P, 4], i32)
        nodef = s.sb("nodef", [P, 1])
        rowf = s.sb("rowf", [P, 1])
        edgef = s.sb("edgef", [P, 1])
        endf = s.sb("endf", [P, 1])
        edge = s.sb("edge", [P, 1], i32)
        source = s.sb("source", [P, 1], i32)
        weight = s.sb("weight", [P, 1])
        taken = s.sb("taken", [P, 1])
        cell_count = s.sb("cell_count", [P, 1], i32)
        cell_weight = s.sb("cell_weight", [P, 1], i32)
        edge_ready = s.sem("edge_ready")
        cells_ready = s.sem("cells_ready")
        source_loaded = s.sem("source_loaded")
        weight_loaded = s.sem("weight_loaded")
        count_added = s.sem("count_added")
        weight_added = s.sem("weight_added")
        pool_waited = s.sem("pool_waited")

        def rows_at(ap):
            return bass.IndirectOffsetOnAxis(ap=ap, axis=0)

        def slots(eng, body):
            total = eng.value_load(counts[0:1, (ALL_TILES - 1) * 8 + EXTRA_BASE:(ALL_TILES - 1) * 8 + EXTRA_BASE + 1],
                                   min_val=0, max_val=E)
            with eng.If(total > 0):
                with eng.Fori(0, TILES) as t:
                    n = eng.value_load(counts[0:1, bass.ds(t * 8 + N_EXTRA, 1)], min_val=0, max_val=E)
                    base = eng.value_load(counts[0:1, bass.ds(t * 8 + EXTRA_BASE, 1)], min_val=0, max_val=E)
                    with eng.If(n > 0):
                        body(t, n, base)
            return total

        with nc.Block() as block:

            @block.gpsimd
            def _(pool):
                def tile(t, n, base):
                    with pool.Fori(0, n * R) as i:
                        at = base * R + i + 1
                        pool.wait_ge(edge_ready, at)
                        pool.sem_inc(pool_waited, 1)
                        pool.indirect_dma_start(out=source[:], out_offset=None, in_=src_dram,
                                                in_offset=rows_at(edge[:, 0:1])).then_inc(source_loaded, 16)
                        pool.indirect_dma_start(out=weight[:], out_offset=None, in_=weight_dram,
                                                in_offset=rows_at(edge[:, 0:1])).then_inc(weight_loaded, 16)
                        pool.wait_ge(cells_ready, at)
                        pool.sem_inc(pool_waited, 1)
                        pool.indirect_dma_start(out=count_table, in_=taken[:], in_offset=None,
                                                out_offset=rows_at(cell_count[:, 0:1]), compute_op=ALU.add)\
                            .then_inc(count_added, 16)
                        pool.indirect_dma_start(out=weight_table, in_=weight[:], in_offset=None,
                                                out_offset=rows_at(cell_weight[:, 0:1]), compute_op=ALU.add)\
                            .then_inc(weight_added, 16)
                        pool.wait_ge(count_added, at * 16)
                        pool.wait_ge(weight_added, at * 16)

                slots(pool, tile)

            @block.vector
            def _(dve):
                def tile(t, n, base):
                    dve.tensor_copy(record[:].rearrange("p (a c) -> p a c", a=1), perm[:, bass.ds(t, 1), :])
                    dve.drain()
                    dve.tensor_copy(nodef[:], record[:, NODE:NODE + 1])
                    dve.tensor_copy(edgef[:], record[:, START:START + 1])
                    dve.drain()
                    dve.tensor_scalar(rowf[:], nodef[:], float(NP), None, ALU.mult)
                    dve.tensor_tensor(endf[:], edgef[:], record[:, DEGREE:DEGREE + 1], ALU.add)
                    dve.drain()
                    dve.tensor_scalar(edgef[:], edgef[:], float(SLOTS), None, ALU.add)
                    dve.drain()
                    with dve.Fori(0, n * R) as i:
                        at = base * R + i + 1
                        dve.tensor_scalar(edge[:], edgef[:], float(E), None, ALU.min)
                        dve.drain().then_inc(edge_ready, 1)
                        dve.wait_ge(source_loaded, at * 16)
                        dve.wait_ge(weight_loaded, at * 16)
                        dve.tensor_tensor(taken[:], edgef[:], endf[:], ALU.is_lt)
                        dve.tensor_tensor(cell_count[:], source[:], rowf[:], ALU.add)
                        dve.scalar_tensor_tensor(cell_weight[:], source[:], float(NP), nodef[:], ALU.mult, ALU.add)
                        dve.drain()
                        dve.tensor_tensor(weight[:], weight[:], taken[:], ALU.mult)
                        dve.tensor_scalar(edgef[:], edgef[:], 1.0, None, ALU.add)
                        dve.drain().then_inc(cells_ready, 1)
                        dve.wait_ge(count_added, at * 16)
                        dve.wait_ge(weight_added, at * 16)

                slots(dve, tile)


def add_cells(nc, s, counts, jobs):
    at = [s.sb(f"add_at{v}", [P, GROUP, 1], i32) for v in range(2)]
    value = [s.sb(f"add_value{v}", [P, GROUP, 1]) for v in range(2)]
    primed = s.sb("primed", [1, GROUP])
    added = [s.sem(f"added{k}") for k in range(GROUP)]
    picked = s.sem("picked")
    added_waited = s.sem("added_waited")

    def run(pool):
        for k in range(GROUP):
            pool.dma_start(primed[0:1, k:k + 1], jobs[0][0][2][0:1, :]).then_inc(added[k], 16)
        done = 1
        for (cells, values, table), g, part in jobs:
            tiles = slice(g * GROUP, (g + 1) * GROUP)
            n = pool.value_load(counts[0:1, g * GROUP * 8 + N_MAIN:g * GROUP * 8 + N_MAIN + 1], min_val=1, max_val=MAIN)
            first = n // 2 if part == 1 else 0
            bodies = {"all": n, 0: n // 2, 1: (n + 1) // 2}[part]

            def slots(i, done):
                for r in range(R):
                    v = r % 2
                    pool.tensor_copy(at[v][:], cells[:, tiles, bass.ds((first + i) * R + r, 1)]).then_inc(picked, 1)
                    pool.tensor_copy(value[v][:], values[:, tiles, bass.ds((first + i) * R + r, 1)]).then_inc(picked, 1)
                    so_far = i * R + (done + r)
                    pool.wait_ge(picked, so_far * 2)
                    pool.sem_inc(added_waited, 1)
                    for k in range(GROUP):
                        pool.wait_ge(added[k], so_far * 16)
                        pool.sem_inc(added_waited, 1)
                        pool.indirect_dma_start(out=table, in_=value[v][:, k, :], in_offset=None,
                                                out_offset=bass.IndirectOffsetOnAxis(ap=at[v][:, k, :], axis=0),
                                                compute_op=ALU.add).then_inc(added[k], 16)

            with pool.If(bodies > 0):
                with pool.Fori(0, bodies) as i:
                    slots(i, done)
            done = bodies * R + done
        for k in range(GROUP):
            pool.wait_ge(added[k], done * 16)

    return run


def dense_phase(nc, name, kind, a, rows_dram, table, x_dram, out_dram, numbers_dram=None, bias_dram=None,
                beside=None):
    separable = kind == "separable"
    HEADS = 2 if separable else 1
    HD = F // HEADS
    C = HD + separable
    PER = 512 // C
    PASSES = 3 if separable else 2
    BLOCKS = -(-TILES // PASSES)
    BANKS = -(-BLOCKS * HEADS // PER)
    row = rows_dram.shape[1]
    passes = [(b, min(b + BLOCKS, TILES)) for b in range(0, TILES, BLOCKS)]
    with ExitStack() as ctx:
        s = Scope(nc, ctx, name)
        h = s.sb("h", [P, TILES, row])
        cell = [s.sb(f"cell{k}", [P, BLOCKS * P]) for k in range(GROUP)]
        x = s.sb("x", [P, BLOCKS, F])
        zero = s.sb("zero", [P, 512])
        value = s.sb("value", [P, BLOCKS * HEADS, HD])
        p_sum = s.ps("p_sum", [P, BANKS * 512])
        if separable:
            hs = s.sb("hs", [P, TILES, HEADS, C])
            number = s.sb("number", [P, HEADS, NP])
            minus = s.sb("minus", [P, TILES, HEADS])
            minus_fifth = s.sb("minus_fifth", [P, TILES, HEADS])
            steep = [s.sb(f"steep{v}", [P, BLOCKS * P]) for v in range(HEADS)]
            flat = [s.sb(f"flat{v}", [P, BLOCKS * P]) for v in range(HEADS)]
            edge = [s.sb(f"edge{v}", [P, BLOCKS * P]) for v in range(HEADS)]
            inv = s.sb("inv", [P, BLOCKS * HEADS])
            none = s.sb("none", [P, BLOCKS * HEADS])
            low = s.sb("low", [P, BLOCKS * HEADS * HD])
        else:
            bias = s.sb("bias", [P, F])
        rows_loaded = s.sem("rows_loaded")
        const_loaded = s.sem("const_loaded")
        number_stored = s.sem("number_stored")
        number_loaded = s.sem("number_loaded")
        zero_set = s.sem("zero_set")
        rows_ready = s.sem("rows_ready")
        cell_loaded = [s.sem(f"cell_loaded{k}") for k in range(GROUP)]
        cell_used = [s.sem(f"cell_used{k}") for k in range(GROUP)]
        x_loaded = s.sem("x_loaded")
        exps_ready = s.sem("exps_ready")
        exps_used = s.sem("exps_used")
        edge_ready = s.sem("edge_ready")
        edge_used = s.sem("edge_used")
        pass_summed = s.sem("pass_summed")
        sums_read = s.sem("sums_read")
        low_ready = s.sem("low_ready")
        low_exp = s.sem("low_exp")
        out_ready = s.sem("out_ready")
        stored = s.sem("stored")
        add_more = beside(s) if beside else None
        cells_of = table.rearrange("(r c) a -> r (c a)", c=NP)

        def rows_of(dram, b0, b1):
            return dram[b0 * P:b1 * P, :].rearrange("(k p) n -> p k n", p=P)

        with nc.Block() as block:

            @block.sync
            def _(sp):
                sp.dma_start(h[:], rows_dram.rearrange("(k p) n -> p k n", p=P)).then_inc(rows_loaded, 16)
                if separable:
                    sp.wait_ge(rows_loaded, 16)
                    for v in range(HEADS):
                        sp.dma_start(numbers_dram[v * NP:(v + 1) * NP].rearrange("(k p) -> p k", p=P), h[:, :, F + v],
                                     allow_slow_non_contiguous=True).then_inc(number_stored, 16)
                    sp.wait_ge(number_stored, 16 * HEADS)
                    sp.dma_start(number[:].rearrange("p h n -> p (h n)"), across(numbers_dram, HEADS * NP))\
                        .then_inc(number_loaded, 16)
                else:
                    sp.dma_start(bias[:], across(bias_dram, F)).then_inc(const_loaded, 16)
                for n, (b0, b1) in enumerate(passes):
                    if n > 0:
                        sp.wait_ge(out_ready, n)
                        sp.dma_start(rows_of(out_dram, *passes[n - 1]), x[:, 0:passes[n - 1][1] - passes[n - 1][0], :])\
                            .then_inc(stored, 16)
                        sp.wait_ge(stored, 16 * n)
                    sp.dma_start(x[:, 0:b1 - b0, :], rows_of(x_dram, b0, b1)).then_inc(x_loaded, 16)
                sp.wait_ge(out_ready, PASSES)
                sp.dma_start(rows_of(out_dram, *passes[-1]), x[:, 0:passes[-1][1] - passes[-1][0], :]).then_inc(stored, 16)
                sp.wait_ge(stored, 16 * PASSES)

            def load_cells(eng):
                for n, (b0, b1) in enumerate(passes):
                    with eng.Fori(0, GROUPS) as g:
                        for k in range(GROUP):
                            eng.wait_ge(cell_used[k], g + (n * GROUPS + 1))
                            eng.dma_start(cell[k][:, 0:(b1 - b0) * P],
                                          cells_of[bass.ds((g * GROUP + k) * P, P), b0 * P:b1 * P])\
                                .then_inc(cell_loaded[k], 16)

            @block.gpsimd
            def _(pool):
                pool.memset(zero[:], 0.0)
                pool.drain().then_inc(zero_set, 1)
                for k in range(GROUP):
                    pool.sem_inc(cell_used[k], 1)
                if separable:
                    pool.sem_inc(exps_used, 2)
                    pool.sem_inc(edge_used, 2)
                if add_more:
                    add_more(pool)

            @block.scalar
            def _(act):
                if not separable:
                    load_cells(act)
                    return
                act.wait_ge(rows_ready, 1)
                act.wait_ge(number_loaded, 16)
                for n, (b0, b1) in enumerate(passes):
                    w = (b1 - b0) * P
                    with act.Fori(0, GROUPS) as g:
                        for k in range(GROUP):
                            act.wait_ge(cell_used[k], g + (n * GROUPS + 1))
                            act.dma_start(cell[k][:, 0:w], cells_of[bass.ds((g * GROUP + k) * P, P), b0 * P:b1 * P])\
                                .then_inc(cell_loaded[k], 16)
                            for v in range(HEADS):
                                act.wait_ge(exps_used, (g * GROUP + (n * TILES + k)) * HEADS + (v + 1))
                                of = number[:, v, b0 * P:b1 * P]
                                act.activation(steep[v][:, 0:w], of, ACT.Exp, scale=-1.0,
                                               bias=minus[:, bass.ds(g * GROUP + k, 1), v])
                                act.activation(flat[v][:, 0:w], of, ACT.Exp, scale=-0.2,
                                               bias=minus_fifth[:, bass.ds(g * GROUP + k, 1), v]).then_inc(exps_ready, 1)
                    act.wait_ge(low_ready, n + 1)
                    act.activation(low[:, 0:(b1 - b0) * F], low[:, 0:(b1 - b0) * F], ACT.Exp).then_inc(low_exp, 1)

            @block.tensor
            def _(pe):
                pe.wait_ge(zero_set, 1)
                pe.wait_ge(rows_ready, 1)
                for n, (b0, b1) in enumerate(passes):
                    if n > 0:
                        pe.wait_ge(sums_read, n)
                    for b in range(BANKS):
                        nc.tensor.matmul(p_sum[:, b * 512:b * 512 + PER * C], zero[:, 0:P], zero[:, 0:PER * C],
                                         start=True, stop=False)
                    with pe.Fori(0, GROUPS) as g:
                        for k in range(GROUP):
                            if not separable:
                                pe.wait_ge(cell_loaded[k], (g + (n * GROUPS + 1)) * 16)
                            for v in range(HEADS):
                                if separable:
                                    pe.wait_ge(edge_ready, (g * GROUP + (n * TILES + k)) * HEADS + (v + 1))
                                of = edge[v] if separable else cell[k]
                                for b in range(b1 - b0):
                                    unit = b * HEADS + v
                                    to = unit // PER * 512 + unit % PER * C
                                    rhs = hs[:, bass.ds(g * GROUP + k, 1), v, :] if separable else \
                                        h[:, bass.ds(g * GROUP + k, 1), :]
                                    last = nc.tensor.matmul(p_sum[:, to:to + C], of[:, b * P:(b + 1) * P],
                                                            rhs.rearrange("p a d -> p (a d)"), start=False, stop=False)
                                last.then_inc(edge_used if separable else cell_used[k], 1)
                    for b in range(BANKS):
                        last = nc.tensor.matmul(p_sum[:, b * 512:b * 512 + PER * C], zero[:, 0:P], zero[:, 0:PER * C],
                                                start=False, stop=True)
                    last.then_inc(pass_summed, 1)

            @block.vector
            def _(dve):
                dve.wait_ge(rows_loaded, 16)
                if separable:
                    dve.tensor_copy(hs[:, :, :, 0:HD], h[:, :, 0:F].rearrange("p t (h d) -> p t h d", h=HEADS))
                    dve.memset(hs[:, :, :, HD:C], 1.0)
                    dve.tensor_scalar(minus[:], h[:, :, F + HEADS:F + 2 * HEADS], -1.0, None, ALU.mult)
                    dve.tensor_scalar(minus_fifth[:], h[:, :, F + HEADS:F + 2 * HEADS], -0.2, None, ALU.mult)
                else:
                    dve.wait_ge(const_loaded, 16)
                dve.drain().then_inc(rows_ready, 1)
                for n, (b0, b1) in enumerate(passes):
                    w = (b1 - b0) * P
                    units = (b1 - b0) * HEADS
                    if separable:
                        with dve.Fori(0, GROUPS) as g:
                            for k in range(GROUP):
                                dve.wait_ge(cell_loaded[k], (g + (n * GROUPS + 1)) * 16)
                                for v in range(HEADS):
                                    unit = (g * GROUP + (n * TILES + k)) * HEADS + (v + 1)
                                    dve.wait_ge(exps_ready, unit)
                                    dve.scalar_tensor_tensor(steep[v][:, 0:w], steep[v][:, 0:w], CAP, flat[v][:, 0:w],
                                                             ALU.min, ALU.min)
                                    dve.drain()
                                    dve.wait_ge(edge_used, unit)
                                    dve.tensor_tensor(edge[v][:, 0:w], steep[v][:, 0:w], cell[k][:, 0:w], ALU.mult)\
                                       .then_inc(edge_ready, 1)
                                    dve.drain().then_inc(exps_used, 1)
                                dve.drain().then_inc(cell_used[k], 1)
                    dve.wait_ge(pass_summed, n + 1)
                    dve.wait_ge(x_loaded, 16 * (n + 1))
                    xf = x[:, 0:b1 - b0, :].rearrange("p b d -> p (b d)")
                    vf = value[:, 0:units, :].rearrange("p u d -> p (u d)")
                    if separable:
                        def parts(c0, c1):
                            return [(b * PER, min(b * PER + PER, units),
                                     p_sum[:, b * 512:b * 512 + PER * C].rearrange("p (u d) -> p u d", d=C)
                                     [:, 0:min(PER, units - b * PER), c0:c1]) for b in range(-(-units // PER))]

                        for u0, u1, of in parts(HD, C):
                            dve.tensor_copy(inv[:, u0:u1].rearrange("p (u a) -> p u a", a=1), of)
                        dve.drain()
                        dve.tensor_scalar(none[:, 0:units], inv[:, 0:units], 0.0, None, ALU.is_equal)
                        dve.drain()
                        dve.tensor_tensor(inv[:, 0:units], inv[:, 0:units], none[:, 0:units], ALU.add)
                        dve.drain()
                        dve.reciprocal(inv[:, 0:units], inv[:, 0:units])
                        dve.drain()
                        for u0, u1, of in parts(0, HD):
                            dve.tensor_tensor(value[:, u0:u1, :], of,
                                              inv[:, u0:u1].rearrange("p (u a) -> p u a", a=1).to_broadcast([P, u1 - u0, HD]),
                                              ALU.mult)
                        dve.drain().then_inc(sums_read, 1)
                        dve.tensor_scalar(low[:, 0:units * HD], vf, 0.0, None, ALU.min).then_inc(low_ready, 1)
                        dve.scalar_tensor_tensor(xf, vf, 0.0, xf, ALU.max, ALU.add)
                        dve.drain()
                        dve.wait_ge(low_exp, n + 1)
                        dve.scalar_tensor_tensor(xf, low[:, 0:units * HD], -1.0, xf, ALU.add, ALU.add)
                    else:
                        dve.tensor_tensor(value[:, 0:units, :], p_sum[:, 0:units * F].rearrange("p (u d) -> p u d", d=F),
                                          bias[:].rearrange("p (a d) -> p a d", a=1).to_broadcast([P, units, F]), ALU.add)
                        dve.drain().then_inc(sums_read, 1)
                        dve.scalar_tensor_tensor(xf, vf, 0.0, xf, ALU.max, ALU.add)
                    dve.drain().then_inc(out_ready, 1)


def mix_phase(nc, name, src_dram, dst_dram, table, x_dram, out_dram):
    HEADS = 4
    HD = F // HEADS
    row = table.shape[1]
    with ExitStack() as ctx:
        s = Scope(nc, ctx, name)
        left_at = s.sb("left_at", [P, TILES], i32)
        right_at = s.sb("right_at", [P, TILES], i32)
        left = s.sb("left", [P, TILES, row])
        right = s.sb("right", [P, TILES, row])
        x = s.sb("x", [P, TILES, F])
        score = s.sb("score", [P, TILES, HEADS])
        alpha = s.sb("alpha", [P, TILES, HEADS])
        top = s.sb("top", [P, TILES])
        mixed = s.sb("mixed", [P, GROUP, F])
        mean = s.sb("mean", [P, GROUP, HD])
        at_loaded = s.sem("at_loaded")
        x_loaded = s.sem("x_loaded")
        gathered = [s.sem(f"gathered{g}") for g in range(GROUPS)]
        shifted = s.sem("shifted")
        exp_ready = s.sem("exp_ready")
        out_ready = s.sem("out_ready")
        stored = s.sem("stored")
        with nc.Block() as block:

            @block.sync
            def _(sp):
                for to, of in ((left_at, src_dram), (right_at, dst_dram)):
                    sp.dma_start(to[:], of[0:NP, :].rearrange("(k p) a -> p (k a)", p=P),
                                 allow_slow_non_contiguous=True).then_inc(at_loaded, 16)
                sp.dma_start(x[:], x_dram.rearrange("(k p) n -> p k n", p=P)).then_inc(x_loaded, 16)
                for g in range(GROUPS):
                    sp.wait_ge(out_ready, g + 1)
                    sp.dma_start(out_dram[g * GROUP * P:(g + 1) * GROUP * P, :].rearrange("(k p) n -> p k n", p=P),
                                 x[:, g * GROUP:(g + 1) * GROUP, :]).then_inc(stored, 16)
                sp.wait_ge(stored, 16 * GROUPS)

            @block.gpsimd
            def _(pool):
                pool.wait_ge(at_loaded, 32)
                for k in range(TILES):
                    for to, at in ((left, left_at), (right, right_at)):
                        pool.indirect_dma_start(out=to[:, k, :], out_offset=None, in_=table,
                                                in_offset=bass.IndirectOffsetOnAxis(ap=at[:, k:k + 1], axis=0))\
                            .then_inc(gathered[k // GROUP], 16)

            @block.scalar
            def _(act):
                for g in range(GROUPS):
                    t = slice(g * GROUP, (g + 1) * GROUP)
                    act.wait_ge(shifted, g + 1)
                    act.activation(alpha[:, t, :], score[:, t, :], ACT.Exp).then_inc(exp_ready, 1)

            @block.vector
            def _(dve):
                for g in range(GROUPS):
                    t = slice(g * GROUP, (g + 1) * GROUP)

                    def by_tile(v):
                        return v.rearrange("p (t a) -> p t a", a=1).to_broadcast([P, GROUP, HEADS])

                    dve.wait_ge(gathered[g], 2 * GROUP * 16)
                    dve.tensor_tensor(score[:, t, :], left[:, t, F:F + HEADS], right[:, t, F + HEADS:F + 2 * HEADS], ALU.add)
                    dve.drain()
                    dve.scalar_tensor_tensor(score[:, t, :], score[:, t, :], 0.01, score[:, t, :], ALU.mult, ALU.max)
                    dve.drain()
                    dve.tensor_reduce(top[:, t], score[:, t, :], AX.X, ALU.max)
                    dve.drain()
                    dve.tensor_tensor(score[:, t, :], score[:, t, :], by_tile(top[:, t]), ALU.subtract).then_inc(shifted, 1)
                    dve.wait_ge(exp_ready, g + 1)
                    dve.tensor_reduce(top[:, t], alpha[:, t, :], AX.X, ALU.add)
                    dve.drain()
                    dve.reciprocal(top[:, t], top[:, t])
                    dve.drain()
                    dve.tensor_tensor(alpha[:, t, :], alpha[:, t, :], by_tile(top[:, t]), ALU.mult)
                    dve.drain()
                    dve.tensor_tensor(mixed[:].rearrange("p t (h d) -> p t h d", h=HEADS),
                                      right[:, t, 0:F].rearrange("p t (h d) -> p t h d", h=HEADS),
                                      alpha[:, t, :].rearrange("p t (h a) -> p t h a", a=1).to_broadcast([P, GROUP, HEADS, HD]),
                                      ALU.mult)
                    dve.drain()
                    dve.tensor_reduce(mean[:], mixed[:].rearrange("p t (h d) -> p t d h", h=HEADS), AX.X, ALU.add)
                    dve.drain()
                    if g == 0:
                        dve.wait_ge(x_loaded, 16)
                    xh = x[:, t, :].rearrange("p t (h d) -> p t h d", h=HEADS)
                    dve.tensor_tensor(xh, xh, mean[:].rearrange("p t (a d) -> p t a d", a=1).to_broadcast([P, GROUP, HEADS, HD]),
                                      ALU.add).then_inc(out_ready, 1)


def build_program(nc, a, out):
    def dram(name, shape, dt=fp32):
        return nc.dram_tensor(name, shape, dt, kind="Internal").ap()

    ident = a["ident"]
    order = dram("order", (NP, 4), i32)
    sort_keys = dram("sort_keys", (NP,))
    kv, q = dram("kv", (NP, 2 * F)), dram("q", (NP, F))
    attended = dram("attended", (ROWS, F))
    xs = [a["x"]] + [dram(f"x{i}", (NP, F)) for i in range(1, 8)]
    xt = dram("xt", (NP, F + 8))
    h = dram("h", (NP, F + 4))
    numbers = dram("numbers", (2 * NP,))
    hw = dram("hw", (NP, F))
    count_table = dram("count_table", (NP * NP, 1))
    weight_table = dram("weight_table", (NP * NP, 1))
    with nc.sbuf_tensor("perm", [P, ALL_TILES, 4], i32) as perm, \
            nc.sbuf_tensor("counts", [1, ALL_TILES * 8], i32) as counts, \
            nc.sbuf_tensor("cell_count", [P, TILES, SLOTS], i32) as cell_count, \
            nc.sbuf_tensor("cell_weight", [P, TILES, SLOTS], i32) as cell_weight, \
            nc.sbuf_tensor("taken", [P, TILES, SLOTS], fp32) as taken, \
            nc.sbuf_tensor("weights", [P, TILES, SLOTS], fp32) as weights:
        c, w = (cell_count, taken, count_table), (cell_weight, weights, weight_table)

        def adding(*jobs):
            return lambda s: add_cells(nc, s, counts, jobs)

        order_phase(nc, "order", a, a["dst_key"], order, sort_keys, perm, counts)
        cells_phase(nc, "cells", perm, a["src"], a["edge_weight"], cell_count, cell_weight, taken, weights)
        projection_phase(nc, "qkv", ident, xs[0], [a["L0_gnn_Wk"], a["L0_gnn_Wv"], a["L0_gnn_Wq"]], [kv, q])
        neighbour_phase(nc, "gnn0", "attend", a, perm, counts, kv, q, None, a["src"], a["edge_attr_8"], attended,
                        tables=(count_table, weight_table))
        spill_phase(nc, "spill", perm, counts, a["src"], a["edge_weight"], count_table, weight_table)
        projection_phase(nc, "wo", ident, attended, [a["L0_gnn_Wo"]], [xs[1]], res_dram=xs[0], layernorm=False,
                         beside=adding((w, 4, 0)))
        ffn0(nc, a, xs[1], xs[2], adding((c, 0, "all"), (c, 1, "all")))
        projection_phase(nc, "xt", ident, xs[2], [a["L1_gnn_weight"]], [xt],
                         dots=((a["L1_gnn_attn_l"], 4), (a["L1_gnn_attn_r"], 4)), beside=adding((c, 2, 0)))
        mix_phase(nc, "gnn1", a["src"], a["dst"], xt, xs[2], xs[3])
        ffn1(nc, a, xs[3], xs[4], adding((c, 2, 1), (c, 3, "all"), (c, 4, "all"), (w, 4, 1), (w, 3, 0)))
        projection_phase(nc, "h", ident, xs[4], [a["L2_gnn_W"]], [h], bias_dram=a["L2_gnn_b"],
                         dots=((a["L2_gnn_a_src"], 2), (a["L2_gnn_a_dst"], 2)), beside=adding((w, 3, 1)))
        dense_phase(nc, "gnn2", "separable", a, h, count_table, xs[4], xs[5], numbers_dram=numbers,
                    beside=adding((w, 0, "all"), (w, 1, "all")))
        projection_phase(nc, "ffn2", ident, xs[5], [a["L2_ffn_weight"]], [xs[6]], res_dram=xs[5],
                         bias_dram=a["L2_ffn_bias"], beside=adding((w, 2, 0)))
        projection_phase(nc, "hw", ident, xs[6], [a["L3_gnn_W"]], [hw], beside=adding((w, 2, 1)))
        dense_phase(nc, "gnn3", "weighted", a, hw, weight_table, xs[6], xs[7], bias_dram=a["L3_gnn_b"])
    ffn3(nc, a, xs[7], out)


def lay_out(inputs):
    import numpy as np

    a = {k: np.asarray(v) for k, v in inputs.items()}

    def padded(v, n, value=0):
        return np.concatenate([v, np.full((n - v.shape[0],) + v.shape[1:], value, v.dtype)])

    spare = E + 2 * P
    a["x"] = padded(a["x"], NP)
    a["dst_key"] = padded(a["dst"], COLS * P, 4095)
    for k in ("src", "dst", "edge_weight"):
        a[k] = padded(a[k].reshape(E, 1), spare)
    a["edge_attr_8"] = padded(a["edge_attr_8"], spare)
    for k in ("q", "k", "v", "o"):
        a[f"L0_gnn_W{k}"] = a[f"L0_gnn_W{k}"].T
    a["L1_gnn_attn_l"] = a["L1_gnn_attn_l"].reshape(F)
    a["L1_gnn_attn_r"] = a["L1_gnn_attn_r"].reshape(F)
    a["L2_gnn_W"] = a["L2_gnn_W"].reshape(F, F).T
    a["L2_gnn_b"] = a["L2_gnn_b"].reshape(F)
    vectors = a.pop("L2_gnn_a")
    a["L2_gnn_a_src"] = vectors[:, :F // 2].reshape(F)
    a["L2_gnn_a_dst"] = vectors[:, F // 2:].reshape(F)
    a["L2_ffn_weight"] = a["L2_ffn_weight"].T
    a["ident"] = np.eye(P, dtype=np.float32)
    a["before"] = np.triu(np.ones((P, P), np.float32), 1)
    return {k: np.ascontiguousarray(v) for k, v in a.items()}


def kernel(**inputs):
    import concourse.bacc as bacc
    from concourse.bass_utils import run_bass_kernel_spmd

    nc = bacc.Bacc("TRN2", target_bir_lowering=False, num_devices=1)
    laid = lay_out(inputs)
    arrays = {f"in_{k}": v for k, v in laid.items()}
    args = {k: nc.dram_tensor(f"in_{k}", v.shape, mybir.dt.from_np(v.dtype), kind="ExternalInput").ap()
            for k, v in laid.items()}
    out = nc.dram_tensor("out_x", (NP, F), fp32, kind="ExternalOutput").ap()
    build_program(nc, args, out)
    result = run_bass_kernel_spmd(nc, [arrays], core_ids=[0])
    return result.results[0]["out_x"][:N]
```

```python
import concourse.bass as bass
from concourse import mybir
from contextlib import ExitStack

fp32 = mybir.dt.float32
i32 = mybir.dt.int32
bf16 = mybir.dt.bfloat16
ALU = mybir.AluOpType
ACT = mybir.ActivationFunctionType
AX = mybir.AxisListType

P = 128
N = 3125
F = 256
E = 103125
TILES = -(-N // P)
NP = TILES * P
GROUP = 5
GROUPS = TILES // GROUP
EPS = 1e-5


class Scope:

    def __init__(self, nc, ctx, name):
        self.nc, self.ctx, self.name, self.sems = nc, ctx, name, []
        ctx.callback(self.clear)

    def sb(self, name, shape, dt=fp32):
        return self.ctx.enter_context(self.nc.sbuf_tensor(f"{self.name}_{name}", shape, dt))

    def ps(self, name, shape, dt=fp32):
        return self.ctx.enter_context(self.nc.psum_tensor(f"{self.name}_{name}", shape, dt))

    def sem(self, name):
        self.sems.append(self.nc.alloc_semaphore(f"{self.name}_{name}"))
        return self.sems[-1]

    def clear(self):
        self.nc.clear_and_free_semaphores(self.sems)
        self.nc.all_engine_barrier()


def rows(dram, g, n):
    return dram[bass.ds(g * n, n), :].rearrange("(t p) d -> p t d", p=P)


def across(vector, n):
    return vector.rearrange("(a n) -> a n", a=1).to_broadcast([P, n])


def projection_phase(nc, name, ident_dram, a_dram, w_drams, out_drams, res_dram=None, bias_dram=None,
                     layernorm=True, dots=(), beside=None):
    nout = sum(w.shape[1] for w in w_drams)
    row = sum(o.shape[1] for o in out_drams)
    cuts = [(n, min(n + 512, nout)) for n in range(0, nout, 512)]
    with ExitStack() as ctx:
        s = Scope(nc, ctx, name)
        ident = s.sb("ident", [P, P])
        w = s.sb("w", [P, 2, nout])
        bias = s.sb("bias", [P, nout]) if bias_dram is not None else None
        dotv = [s.sb(f"dotv{i}", [P, F]) for i in range(len(dots))]
        a = s.sb("a", [P, GROUP, F])
        res = s.sb("res", [P, GROUP, F]) if res_dram is not None else None
        stats = s.sb("stats", [P, GROUP, 6])
        mv = s.sb("mv", [P, GROUP, 2])
        std = s.sb("std", [P, GROUP])
        rstd = s.sb("rstd", [P, GROUP])
        epsb = s.sb("epsb", [P, 1])
        xn = s.sb("xn", [P, GROUP, F]) if layernorm else a
        xT = s.sb("xT", [P, GROUP, 2, P])
        prod = s.sb("prod", [P, F])
        og = s.sb("og", [P, GROUP, row])
        tp = s.ps("tp", [P, 3 * 512])
        po = [s.ps(f"po{i}", [P, 1024]) for i in range(2)]
        const_loaded = s.sem("const_loaded")
        eps_set = s.sem("eps_set")
        a_loaded = s.sem("a_loaded")
        res_loaded = s.sem("res_loaded")
        var_ready = s.sem("var_ready")
        std_ready = s.sem("std_ready")
        xn_ready = s.sem("xn_ready")
        turned = s.sem("turned")
        xT_ready = s.sem("xT_ready")
        product_ready = s.sem("product_ready")
        tile_out = s.sem("tile_out")
        stored = [s.sem(f"stored{i}") for i in range(len(out_drams))]
        n_const = 1 + len(w_drams) + (bias is not None) + len(dots)
        add_more, vector_more = beside(s) if beside else (None, None)

        def load(sp, g):
            sp.dma_start(a[:], rows(a_dram, g, GROUP * P)).then_inc(a_loaded, 16)

        def load_res(sp, g):
            if res is not None:
                sp.dma_start(res[:], rows(res_dram, g, GROUP * P)).then_inc(res_loaded, 16)

        def store(sp, g):
            at = 0
            for i, o in enumerate(out_drams):
                sp.dma_start(rows(o, g, GROUP * P), og[:, :, at:at + o.shape[1]]).then_inc(stored[i], 16)
                at += o.shape[1]

        with nc.Block() as block:

            @block.sync
            def _(sp):
                sp.dma_start(ident[:], ident_dram).then_inc(const_loaded, 16)
                at = 0
                for m in w_drams:
                    sp.dma_start(w[:, :, at:at + m.shape[1]], m.rearrange("(k p) n -> p k n", p=P))\
                        .then_inc(const_loaded, 16)
                    at += m.shape[1]
                if bias is not None:
                    sp.dma_start(bias[:], across(bias_dram, nout)).then_inc(const_loaded, 16)
                for v, (vec, _) in zip(dotv, dots):
                    sp.dma_start(v[:], across(vec, F)).then_inc(const_loaded, 16)
                load(sp, 0)
                load_res(sp, 0)
                with sp.Fori(0, GROUPS - 1) as g:
                    sp.wait_ge(turned, g + 1)
                    load(sp, g + 1)
                    sp.wait_ge(tile_out, GROUP * g + GROUP + 1)
                    load_res(sp, g + 1)
                    store(sp, g)
                sp.wait_ge(tile_out, GROUP * GROUPS + 1)
                store(sp, GROUPS - 1)
                for i in range(len(out_drams)):
                    sp.wait_ge(stored[i], 16 * GROUPS + 16)

            @block.gpsimd
            def _(pool):
                pool.memset(epsb[:], EPS).then_inc(eps_set, 1)
                for sem in (xT_ready, product_ready, tile_out):
                    pool.sem_inc(sem, 1)
                for sem in stored:
                    pool.sem_inc(sem, 16)
                if add_more:
                    add_more(pool)

            @block.scalar
            def _(act):
                act.wait_ge(eps_set, 1)
                with act.Fori(0, GROUPS) as g:
                    if layernorm:
                        act.wait_ge(var_ready, g + 1)
                        act.activation(std[:], mv[:, :, 1], ACT.Sqrt, bias=epsb[:, 0:1]).then_inc(std_ready, 1)
                    act.wait_ge(turned, g + 1)
                    act.wait_ge(product_ready, GROUP * g + 1)
                    act.activation(xT[:].rearrange("p t k n -> p (t k n)"), tp[:, 0:2 * GROUP * P],
                                   ACT.Copy).then_inc(xT_ready, 1)

            @block.tensor
            def _(pe):
                pe.wait_ge(const_loaded, 16 * n_const)
                with pe.Fori(0, GROUPS) as g:
                    if layernorm:
                        pe.wait_ge(xn_ready, g + 1)
                    else:
                        pe.wait_ge(a_loaded, 16 * g + 16)
                    pe.wait_ge(xT_ready, g + 1)
                    for t in range(GROUP):
                        for k in range(2):
                            c = (t * 2 + k) * P
                            last = nc.tensor.transpose(tp[:, c:c + P], xn[:, t, k * P:(k + 1) * P], ident[:])
                    last.then_inc(turned, 1)
                    pe.wait_ge(xT_ready, g + 2)
                    for t in range(GROUP):
                        pe.wait_ge(tile_out, GROUP * g + max(t, 1))
                        for n0, n1 in cuts:
                            for k in range(2):
                                last = nc.tensor.matmul(po[t % 2][:, n0:n1], xT[:, t, k, :], w[:, k, n0:n1],
                                                        start=(k == 0), stop=(k == 1))
                        last.then_inc(product_ready, 1)

            @block.vector
            def _(dve):
                dve.wait_ge(const_loaded, 16 * n_const)
                with dve.Fori(0, GROUPS) as g:
                    if layernorm:
                        dve.wait_ge(a_loaded, 16 * g + 16)
                        for t in range(GROUP):
                            dve.bn_stats(stats[:, t, :], a[:, t, :])
                        dve.drain()
                        for t in range(GROUP):
                            last = dve.bn_aggr(mv[:, t, :], stats[:, t, :])
                        last.then_inc(var_ready, 1)
                        dve.wait_ge(std_ready, g + 1)
                        dve.reciprocal(rstd[:], std[:])
                        dve.drain()
                        for t in range(GROUP):
                            last = dve.tensor_scalar(xn[:, t, :], a[:, t, :], mv[:, t, 0:1], rstd[:, t:t + 1],
                                                     ALU.subtract, ALU.mult)
                        last.then_inc(xn_ready, 1)
                    if res is not None:
                        dve.wait_ge(res_loaded, 16 * g + 16)
                    for i in range(len(out_drams)):
                        dve.wait_ge(stored[i], 16 * g + 16)
                    for t in range(GROUP):
                        dve.wait_ge(product_ready, GROUP * g + t + 2)
                        src = po[t % 2][:, 0:nout]
                        out = og[:, t, 0:nout]
                        if bias is not None:
                            dve.tensor_tensor(out, src, bias[:], ALU.add)
                            if res is not None:
                                dve.drain()
                                dve.tensor_tensor(out, out, res[:, t, :], ALU.add)
                        elif res is not None:
                            dve.tensor_tensor(out, src, res[:, t, :], ALU.add)
                        else:
                            dve.tensor_copy(out, src)
                        at = nout
                        for v, (_, heads) in zip(dotv, dots):
                            dve.drain()
                            dve.tensor_tensor(prod[:], out, v[:], ALU.mult)
                            dve.drain()
                            dve.tensor_reduce(og[:, t, at:at + heads],
                                              prod[:].rearrange("p (h d) -> p h d", h=heads), AX.X, ALU.add)
                            at += heads
                        dve.drain().then_inc(tile_out, 1)
                if vector_more:
                    vector_more(dve)


def moe_phase(nc, name, ident_dram, x_dram, out_dram, router, gate, w1, hidden_act, w2, w3, b3, inner_norm=None,
              beside=None):
    Ex, _, H = w1.shape
    MB = H // P
    deep = w2 is not None
    KC = 2 if deep else MB
    halves = [(0, 3), (3, GROUP)]
    routed = len(router) == 4
    with ExitStack() as ctx:
        s = Scope(nc, ctx, name)
        ident = s.sb("ident", [P, P])
        wa = s.sb("wa", [P, Ex, 2, H])
        wb = s.sb("wb", [P, Ex, 2, F]) if deep else None
        wc = s.sb("wc", [P, Ex, KC, F])
        bc = s.sb("bc", [Ex, F])
        if routed:
            rw1 = s.sb("rw1", [P, 2, P])
            rb1 = s.sb("rb1", [P, 1])
            rw2 = s.sb("rw2", [P, Ex])
            rh = s.sb("rh", [P, GROUP * P])
        else:
            rw = s.sb("rw", [P, 2, Ex])
        rb = s.sb("rb", [P, Ex])
        sizes = [MB] + [2] * deep
        hb = [s.sb(f"hb{i}", [P, Ex, m]) for i, m in enumerate(sizes)]
        hs = [s.sb(f"hs{i}", [P, Ex, m]) if len(act) == 6 else None for i, (m, act) in enumerate(zip(sizes, hidden_act))]
        bn = [[s.sb(f"bn{i}{j}", [P, Ex, m]) for j in range(4)] if len(act) == 6 else None
              for i, (m, act) in enumerate(zip(sizes, hidden_act))]
        if inner_norm:
            gamma = s.sb("gamma", [P, F])
            beta = s.sb("beta", [P, F])
        epsb = s.sb("epsb", [P, 2])
        x = s.sb("x", [P, GROUP, F])
        stats = s.sb("stats", [P, GROUP, 6])
        mv = s.sb("mv", [P, GROUP, 2])
        std = s.sb("std", [P, GROUP])
        rstd = s.sb("rstd", [P, GROUP])
        xn = s.sb("xn", [P, GROUP, F])
        xT = s.sb("xT", [P, 2, GROUP * P])
        all_xT = s.sb("all_xT", [P, 2, NP])
        h1 = s.sb("h1", [P, MB, GROUP * P])
        h2 = s.sb("h2", [P, 2, GROUP * P]) if deep else None
        last_h = h2 if deep else h1
        acc = s.sb("acc", [P, GROUP, F])
        before = s.sb("before", [P, Ex, Ex])
        steps = s.sb("steps", [P, Ex, Ex], i32)
        z = s.sb("z", [P, TILES, Ex])
        z2 = s.sb("z2", [P, TILES, Ex])
        ex = s.sb("ex", [P, TILES, Ex])
        all_gates = s.sb("all_gates", [P, TILES, Ex])
        gates = s.sb("gates", [P, GROUP, Ex])
        top = s.sb("top", [P, TILES])
        total = s.sb("total", [P, TILES])
        if gate != "softmax":
            sel = s.sb("sel", [P, TILES, Ex])
            over = s.sb("over", [P, TILES, Ex, Ex])
            same = s.sb("same", [P, TILES, Ex, Ex])
        gT = s.sb("gT", [Ex, GROUP * P])
        pA = s.ps("pA", [P, 4, 512])
        pC = s.ps("pC", [P, 3 * 512])
        pR = s.ps("pR", [P, 512])
        const_loaded = s.sem("const_loaded")
        features_loaded = s.sem("features_loaded")
        weights_loaded = s.sem("weights_loaded")
        pool_set = s.sem("pool_set")
        bn_ready = s.sem("bn_ready")
        bn_std = s.sem("bn_std")
        x_loaded = s.sem("x_loaded")
        var_ready = s.sem("var_ready")
        std_ready = s.sem("std_ready")
        xn_ready = s.sem("xn_ready")
        turned = s.sem("turned")
        xT_ready = s.sem("xT_ready")
        router_hidden = s.sem("router_hidden")
        router_act = s.sem("router_act")
        logits_ready = s.sem("logits_ready")
        shifted = s.sem("shifted")
        exp_ready = s.sem("exp_ready")
        gates_ready = s.sem("gates_ready")
        gT_turned = s.sem("gT_turned")
        gT_ready = s.sem("gT_ready")
        base_ready = s.sem("base_ready")
        base_added = s.sem("base_added")
        hidden_product = s.sem("hidden_product")
        hidden_ready = s.sem("hidden_ready")
        expert_out = s.sem("expert_out")
        combined = s.sem("combined")
        stored = s.sem("stored")
        HID = Ex * 2 * (MB + 2 * deep)
        banks = [(0, 2), (2, 4), (4, 5)]
        BANKS = len(banks)
        OUT = Ex * BANKS
        norms = 2 if inner_norm else 1
        exps = 2 if gate == "softmax_top2_softmax" else 1
        n_bn = sum(b is not None for b in bn)
        loads = [(ident[:], ident_dram)]
        weight_loads = [(wa[:, e], w1[e].rearrange("(k p) n -> p k n", p=P)) for e in range(Ex)]
        weight_loads += [(wb[:, e], w2[e].rearrange("(k p) n -> p k n", p=P)) for e in range(Ex)] if deep else []
        weight_loads += [(wc[:, e], w3[e].rearrange("(k p) n -> p k n", p=P)) for e in range(Ex)]
        weight_loads += [(bc[:], b3)]
        if routed:
            loads += [(rw1[:], router[0].rearrange("(k p) n -> p k n", p=P)),
                      (rb1[:], router[1].rearrange("(p a) -> p a", a=1)), (rw2[:], router[2])]
        else:
            loads += [(rw[:], router[0].rearrange("(k p) n -> p k n", p=P))]
        loads += [(rb[:], across(router[-1], Ex))]
        if inner_norm:
            loads += [(gamma[:], across(inner_norm[0], F)), (beta[:], across(inner_norm[1], F))]
        by_feature = []
        for i, act in enumerate(hidden_act):
            by_feature += [(hb[i], act[1])]
            if len(act) == 6:
                by_feature += list(zip(bn[i], act[2:]))
        feature_loads = []
        for to, of in by_feature:
            feature_loads += [(to[:, e, :], of[e].rearrange("(m p) -> p m", p=P)) for e in range(Ex)]

        add_more, _ = beside(s) if beside else (None, None)

        with nc.Block() as block:

            @block.sync
            def _(sp):
                sp.dma_start(x[:], rows(x_dram, 0, GROUP * P)).then_inc(x_loaded, 16)
                for to, of in loads:
                    sp.dma_start(to, of, allow_slow_non_contiguous=True).then_inc(const_loaded, 16)
                for to, of in feature_loads:
                    sp.dma_start(to, of, allow_slow_non_contiguous=True).then_inc(features_loaded, 16)
                for g in range(1, GROUPS):
                    sp.wait_ge(xn_ready, norms * g)
                    sp.dma_start(x[:], rows(x_dram, g, GROUP * P)).then_inc(x_loaded, 16)
                    for to, of in weight_loads[g - 1::GROUPS - 1]:
                        sp.dma_start(to, of).then_inc(weights_loaded, 16)
                sp.wait_ge(xn_ready, norms * GROUPS)
                sp.dma_start(x[:], rows(x_dram, 0, GROUP * P)).then_inc(x_loaded, 16)
                with sp.Fori(0, GROUPS - 1) as g:
                    sp.wait_ge(base_added, BANKS * g + BANKS)
                    sp.dma_start(x[:], rows(x_dram, g + 1, GROUP * P)).then_inc(x_loaded, 16)
                    sp.wait_ge(combined, OUT * g + (OUT + 1))
                    sp.dma_start(rows(out_dram, g, GROUP * P), acc[:]).then_inc(stored, 16)
                sp.wait_ge(combined, OUT * GROUPS + 1)
                sp.dma_start(rows(out_dram, GROUPS - 1, GROUP * P), acc[:]).then_inc(stored, 16)
                sp.wait_ge(stored, 16 * GROUPS + 16)

            @block.gpsimd
            def _(pool):
                pool.memset(epsb[:, 0:1], EPS)
                pool.memset(epsb[:, 1:2], 1e-3)
                pool.iota(steps[:], [[-1, Ex], [1, Ex]], base=0, channel_multiplier=0)
                pool.drain().then_inc(pool_set, 1)
                for sem in (logits_ready, xT_ready, turned, hidden_ready, combined):
                    pool.sem_inc(sem, 1)
                pool.sem_inc(stored, 16)
                if add_more:
                    add_more(pool)

            @block.scalar
            def _(act):
                act.wait_ge(pool_set, 1)
                act.wait_ge(const_loaded, 16 * len(loads))
                if n_bn:
                    act.wait_ge(features_loaded, 16 * len(feature_loads))
                for b in bn:
                    if b is not None:
                        act.activation(b[3][:], b[3][:], ACT.Sqrt, bias=epsb[:, 1:2]).then_inc(bn_std, 1)
                if n_bn:
                    act.wait_ge(bn_ready, 1)
                with act.Fori(0, GROUPS) as g:
                    for i in range(norms):
                        act.wait_ge(var_ready, norms * g + i + 1)
                        act.activation(std[:], mv[:, :, 1], ACT.Sqrt, bias=epsb[:, 0:1]).then_inc(std_ready, 1)
                    act.wait_ge(turned, g + 2)
                    act.wait_ge(logits_ready, g + 1)
                    turned_rows = pC[:, 0:2 * GROUP * P].rearrange("p (t k n) -> p t k n", k=2, n=P)
                    act.activation(xT[:].rearrange("p k (t n) -> p t k n", n=P), turned_rows, ACT.Copy)
                    for k in range(2):
                        last = act.activation(all_xT[:, k, bass.ds(g * GROUP * P, GROUP * P)]
                                              .rearrange("p (t n) -> p t n", n=P), turned_rows[:, :, k, :], ACT.Copy)
                    last.then_inc(xT_ready, 1)
                    if routed:
                        for i, (t0, t1) in enumerate(halves):
                            act.wait_ge(router_hidden, 2 * g + i + 1)
                            act.activation(rh[:, t0 * P:t1 * P], pA[:, i, 0:(t1 - t0) * P], ACT.Relu,
                                           bias=rb1[:, 0:1]).then_inc(router_act, 1)
                for i in range(exps):
                    act.wait_ge(shifted, i + 1)
                    act.activation(ex[:], z2[:], ACT.Exp).then_inc(exp_ready, 1)
                act.wait_ge(features_loaded, 16 * len(feature_loads))
                with act.Fori(0, GROUPS) as g:
                    j = 0
                    for e in range(Ex):
                        for layer, m_n in enumerate(sizes):
                            to = (h1, h2)[layer]
                            for t0, t1 in halves:
                                for m in range(m_n):
                                    act.wait_ge(hidden_product, HID * g + j + 1)
                                    scale = hs[layer][:, e, m:m + 1] if hs[layer] is not None else 1.0
                                    act.activation(to[:, m, t0 * P:t1 * P], pA[:, j % 4, 0:(t1 - t0) * P],
                                                   hidden_act[layer][0], bias=hb[layer][:, e, m:m + 1],
                                                   scale=scale).then_inc(hidden_ready, 1)
                                    j += 1

            @block.tensor
            def _(pe):
                pe.wait_ge(const_loaded, 16 * len(loads))
                with pe.Fori(0, GROUPS) as g:
                    pe.wait_ge(xn_ready, norms * g + norms)
                    pe.wait_ge(xT_ready, g + 1)
                    for t in range(GROUP):
                        for k in range(2):
                            c = (t * 2 + k) * P
                            last = nc.tensor.transpose(pC[:, c:c + P], xn[:, t, k * P:(k + 1) * P], ident[:])
                    last.then_inc(turned, 1)
                    pe.wait_ge(xT_ready, g + 2)
                    if routed:
                        for i, (t0, t1) in enumerate(halves):
                            for k in range(2):
                                last = nc.tensor.matmul(pA[:, i, 0:(t1 - t0) * P], rw1[:, k, :],
                                                        xT[:, k, t0 * P:t1 * P], start=(k == 0), stop=(k == 1))
                            last.then_inc(router_hidden, 1)
                        pe.wait_ge(router_act, 2 * g + 2)
                    for t in range(GROUP):
                        logits = pR[:, bass.ds((g * GROUP + t) * Ex, Ex)]
                        if routed:
                            last = nc.tensor.matmul(logits, rh[:, t * P:(t + 1) * P], rw2[:], start=True, stop=True)
                        else:
                            for k in range(2):
                                last = nc.tensor.matmul(logits, xT[:, k, t * P:(t + 1) * P], rw[:, k, :],
                                                        start=(k == 0), stop=(k == 1))
                    last.then_inc(logits_ready, 1)
                pe.wait_ge(weights_loaded, 16 * len(weight_loads))
                with pe.Fori(0, GROUPS) as g:
                    pe.wait_ge(hidden_ready, HID * g + 1)
                    j = 0
                    for e in range(Ex):
                        done = {}
                        for layer, m_n in enumerate(sizes):
                            w = (wa, wb)[layer]
                            for h, (t0, t1) in enumerate(halves):
                                if layer:
                                    pe.wait_ge(hidden_ready, HID * g + (done[0, h] + 1))
                                for m in range(m_n):
                                    pe.wait_ge(hidden_ready, HID * g + max(j - 2, 1))
                                    for k in range(2):
                                        last = nc.tensor.matmul(pA[:, j % 4, 0:(t1 - t0) * P],
                                                                w[:, e, k, m * P:(m + 1) * P],
                                                                h1[:, k, t0 * P:t1 * P] if layer else
                                                                all_xT[:, k, bass.ds(g * GROUP * P + t0 * P, (t1 - t0) * P)],
                                                                start=(k == 0), stop=(k == 1))
                                    last.then_inc(hidden_product, 1)
                                    j += 1
                                done[layer, h] = j
                        if e == 0:
                            pe.wait_ge(gates_ready, g + 1)
                            pe.wait_ge(combined, OUT * g + 1)
                            for t in range(GROUP):
                                last = nc.tensor.transpose(pC[0:Ex, t * P:(t + 1) * P], gates[:, t, :], ident[:])
                            last.then_inc(gT_turned, 1)
                            pe.wait_ge(gT_ready, g + 1)
                            for t in range(GROUP):
                                last = nc.tensor.matmul(pC[:, t * F:(t + 1) * F], gT[:, t * P:(t + 1) * P], bc[:],
                                                        start=True, stop=True)
                            last.then_inc(base_ready, 1)
                        for b, (t0, t1) in enumerate(banks):
                            pe.wait_ge(hidden_ready, HID * g + (done[len(sizes) - 1, 0 if t1 <= 3 else 1] + 1))
                            if e == 0:
                                pe.wait_ge(base_added, BANKS * g + b + 1)
                            else:
                                pe.wait_ge(combined, OUT * g + (BANKS * (e - 1) + b + 2))
                            for t in range(t0, t1):
                                for k in range(KC):
                                    last = nc.tensor.matmul(pC[:, t * F:(t + 1) * F],
                                                            last_h[:, k, t * P:(t + 1) * P], wc[:, e, k, :],
                                                            start=(k == 0), stop=(k == KC - 1))
                            last.then_inc(expert_out, 1)

            @block.vector
            def _(dve):
                dve.wait_ge(const_loaded, 16 * len(loads))
                dve.wait_ge(pool_set, 1)
                dve.tensor_scalar(before[:], steps[:], 0.0, None, ALU.is_lt)
                if n_bn:
                    dve.wait_ge(features_loaded, 16 * len(feature_loads))
                    dve.wait_ge(bn_std, n_bn)
                    for i, b in enumerate(bn):
                        if b is not None:
                            g_, be_, m_, sd_ = b
                            dve.reciprocal(sd_[:], sd_[:])
                            dve.drain()
                            dve.tensor_tensor(hs[i][:], g_[:], sd_[:], ALU.mult)
                            dve.tensor_tensor(hb[i][:], hb[i][:], m_[:], ALU.subtract)
                            dve.drain()
                            dve.tensor_tensor(hb[i][:], hb[i][:], hs[i][:], ALU.mult)
                            dve.drain()
                            dve.tensor_tensor(hb[i][:], hb[i][:], be_[:], ALU.add)
                    dve.drain().then_inc(bn_ready, 1)
                else:
                    dve.drain()
                with dve.Fori(0, GROUPS) as g:
                    dve.wait_ge(x_loaded, 16 * g + 16)
                    dve.wait_ge(turned, g + 1)
                    for i in range(norms):
                        of = x if i == 0 else xn
                        for t in range(GROUP):
                            dve.bn_stats(stats[:, t, :], of[:, t, :])
                        dve.drain()
                        for t in range(GROUP):
                            last = dve.bn_aggr(mv[:, t, :], stats[:, t, :])
                        last.then_inc(var_ready, 1)
                        dve.wait_ge(std_ready, norms * g + i + 1)
                        dve.reciprocal(rstd[:], std[:])
                        dve.drain()
                        for t in range(GROUP):
                            last = dve.tensor_scalar(xn[:, t, :], of[:, t, :], mv[:, t, 0:1], rstd[:, t:t + 1],
                                                     ALU.subtract, ALU.mult)
                        if i == 1:
                            dve.drain()
                            every = [P, GROUP, F]
                            dve.tensor_tensor(xn[:], xn[:], gamma[:].rearrange("p (a n) -> p a n", a=1).to_broadcast(every), ALU.mult)
                            dve.drain()
                            last = dve.tensor_tensor(xn[:], xn[:], beta[:].rearrange("p (a n) -> p a n", a=1).to_broadcast(every), ALU.add)
                        last.then_inc(xn_ready, 1)
                        dve.wait_ge(xn_ready, norms * g + i + 1)
                ge = [P, TILES, Ex]

                def wide(v):
                    return v[:].rearrange("p (t a) -> p t a", a=1).to_broadcast(ge)

                dve.wait_ge(logits_ready, GROUPS + 1)
                dve.tensor_tensor(z[:], pR[:, 0:TILES * Ex].rearrange("p (t e) -> p t e", e=Ex),
                                  rb[:].rearrange("p (a e) -> p a e", a=1).to_broadcast(ge), ALU.add)
                dve.drain()
                for i in range(exps):
                    if i == exps - 1 and gate != "softmax":
                        pairs = [P, TILES, Ex, Ex]
                        zj = z[:].rearrange("p t (a e) -> p t a e", a=1).to_broadcast(pairs)
                        ze = z[:].rearrange("p t (e a) -> p t e a", a=1).to_broadcast(pairs)
                        dve.tensor_tensor(over[:], zj, ze, ALU.is_gt)
                        dve.tensor_tensor(same[:], zj, ze, ALU.is_equal)
                        dve.drain()
                        dve.tensor_tensor(same[:], same[:], before[:].rearrange("p (a e) f -> p a e f", a=1).to_broadcast(pairs),
                                          ALU.mult)
                        dve.drain()
                        dve.tensor_tensor(over[:], over[:], same[:], ALU.add)
                        dve.drain()
                        dve.tensor_reduce(sel[:], over[:], AX.X, ALU.add)
                        dve.drain()
                        dve.tensor_scalar(sel[:], sel[:], 1.5, None, ALU.is_lt)
                    dve.tensor_reduce(top[:], z[:], AX.X, ALU.max)
                    dve.drain()
                    dve.tensor_tensor(z2[:], z[:], wide(top), ALU.subtract).then_inc(shifted, 1)
                    dve.wait_ge(exp_ready, i + 1)
                    if i == exps - 1 and gate != "softmax":
                        dve.tensor_tensor(ex[:], ex[:], sel[:], ALU.mult)
                        dve.drain()
                    dve.tensor_reduce(total[:], ex[:], AX.X, ALU.add)
                    dve.drain()
                    dve.reciprocal(total[:], total[:])
                    dve.drain()
                    dve.tensor_tensor((all_gates if i == exps - 1 else z)[:], ex[:], wide(total), ALU.mult)
                    dve.drain()
                with dve.Fori(0, GROUPS) as g:
                    dve.drain()
                    dve.tensor_copy(gates[:], all_gates[:, bass.ds(g * GROUP, GROUP), :]).then_inc(gates_ready, 1)
                    dve.wait_ge(x_loaded, 16 * g + 16 * (GROUPS + 1))
                    dve.wait_ge(gT_turned, g + 1)
                    dve.tensor_copy(gT[:], pC[0:Ex, 0:GROUP * P]).then_inc(gT_ready, 1)
                    dve.wait_ge(base_ready, g + 1)
                    dve.wait_ge(stored, 16 * g + 16)
                    for t0, t1 in banks:
                        dve.tensor_tensor(acc[:, t0:t1, :], x[:, t0:t1, :],
                                          pC[:, t0 * F:t1 * F].rearrange("p (t n) -> p t n", n=F),
                                          ALU.add).then_inc(base_added, 1)
                    dve.wait_ge(base_added, BANKS * g + BANKS)
                    for e in range(Ex):
                        for b, (t0, t1) in enumerate(banks):
                            dve.wait_ge(expert_out, OUT * g + BANKS * e + b + 1)
                            if e:
                                dve.wait_ge(combined, OUT * g + (BANKS * (e - 1) + b + 2))
                            for t in range(t0, t1):
                                last = dve.scalar_tensor_tensor(acc[:, t, :], pC[:, t * F:(t + 1) * F],
                                                                gates[:, t, e:e + 1], acc[:, t, :],
                                                                ALU.mult, ALU.add)
                            last.then_inc(combined, 1)


def ffn0(nc, a, x, out, beside):
    p = "L0_ffn_"
    moe_phase(nc, "ffn0", a["ident"], x, out,
              (a[p + "router_w1"], a[p + "router_b1"], a[p + "router_w2"], a[p + "router_b2"]),
              "softmax_top2_softmax", a[p + "expert_w1"],
              [(ACT.Relu, a[p + "expert_b1"]), (ACT.Relu, a[p + "expert_b2"])],
              a[p + "expert_w2"], a[p + "expert_w3"], a[p + "expert_b3"], beside=beside)


def ffn1(nc, a, x, out, beside):
    p = "L1_ffn_"
    moe_phase(nc, "ffn1", a["ident"], x, out, (a[p + "Wr"], a[p + "br"]), "softmax", a[p + "W1"],
              [(ACT.Relu, *(a[p + n + str(i)] for n in ("b", "g", "be", "m", "v"))) for i in (1, 2)],
              a[p + "W2"], a[p + "Wo"], a[p + "bo"], beside=beside)


def ffn3(nc, a, x, out):
    p = "L3_ffn_"
    moe_phase(nc, "ffn3", a["ident"], x, out, (a[p + "Wr"], a[p + "br"]), "top2_softmax", a[p + "W1"],
              [(ACT.Gelu, a[p + "b1"])], None, a[p + "W2"], a[p + "b2"],
              inner_norm=(a[p + "gamma"], a[p + "beta"]))


R = 8
SETS = 4
SLOTS = 64
MAIN = SLOTS // R
LOOP_TILES = TILES + 1
ALL_TILES = TILES + 3
ROWS = LOOP_TILES * P
COLS = -(-E // P)
N_MAIN, N_EXTRA, BASE, EXTRA_BASE, USES, HEAD, STEPS = 0, 1, 2, 3, 4, 5, 6
STEP = 4
USE_BITS = 24 // SETS
assert MAIN < 16 and MAIN // SETS * LOOP_TILES < 2 ** USE_BITS
NODE, START, DEGREE, TARGET = 0, 1, 2, 3


def set_of(body, odd):
    return (body + odd * SETS // 2) % SETS


def body_of(the_set, odd):
    return (the_set - odd * SETS // 2) % SETS


def order_phase(nc, name, a, key_dram, order_dram, keys_dram, perm, counts, tables=()):
    BLOCK = 13
    BLOCKS = COLS // BLOCK
    assert BLOCKS * BLOCK == COLS and BLOCKS % 2 == 0
    with ExitStack() as ctx:
        s = Scope(nc, ctx, name)
        key = s.sb("key", [P, COLS], i32)
        part = s.sb("part", [P, COLS], i32)
        low = s.sb("low", [P, COLS], bf16)
        high = s.sb("high", [P, COLS], bf16)
        iota_low = s.sb("iota_low", [P, P], bf16)
        one_low = [s.sb(f"one_low{u}", [P, BLOCK, P], bf16) for u in range(2)]
        one_high = [s.sb(f"one_high{u}", [P, BLOCK, TILES], bf16) for u in range(2)]
        zero = s.sb("zero", [P, P], bf16)
        before = s.sb("before", [P, P])
        ones = s.sb("ones", [P, P])
        node = s.sb("node", [P, ALL_TILES], i32)
        nodef = s.sb("nodef", [P, TILES])
        target = s.sb("target", [P, ALL_TILES], i32)
        deg = s.sb("deg", [P, TILES])
        total = s.sb("total", [P, TILES])
        start = s.sb("start", [P, TILES])
        onesf = s.sb("onesf", [P, ALL_TILES])
        sortkey = s.sb("sortkey", [P, TILES])
        every = s.sb("every", [P, TILES * P])
        above = s.sb("above", [P, TILES * P], bf16)
        rankf = s.sb("rankf", [P, TILES])
        rank = s.sb("rank", [P, TILES], i32)
        record = s.sb("record", [P, TILES, 4], i32)
        spare = s.sb("spare", [P, 3, 4], i32)
        degf = s.sb("degf", [P, TILES])
        most = s.sb("most", [P, TILES])
        bodies = s.sb("bodies", [P, ALL_TILES], i32)
        work = s.sb("work", [P, ALL_TILES], i32)
        steps = s.sb("steps", [P, TILES], i32)
        workf = s.sb("workf", [P, ALL_TILES])
        sumf = s.sb("sumf", [P, ALL_TILES])
        s_packed = s.sb("s_packed", [P, ALL_TILES])
        p_deg = s.ps("p_deg", [P, 512])
        p_sum = s.ps("p_sum", [P, 512])
        key_loaded = s.sem("key_loaded")
        const_loaded = s.sem("const_loaded")
        pool_set = s.sem("pool_set")
        zero_set = s.sem("zero_set")
        hot_ready = [s.sem(f"hot_ready{u}") for u in range(2)]
        hot_used = [s.sem(f"hot_used{u}") for u in range(2)]
        deg_summed = s.sem("deg_summed")
        deg_ready = s.sem("deg_ready")
        prefix_ready = s.sem("prefix_ready")
        sortkey_ready = s.sem("sortkey_ready")
        sortkey_stored = s.sem("sortkey_stored")
        every_loaded = s.sem("every_loaded")
        record_ready = s.sem("record_ready")
        scattered = s.sem("scattered")
        perm_loaded = s.sem("perm_loaded")
        degf_ready = s.sem("degf_ready")
        most_ready = s.sem("most_ready")
        done = s.sem("done")
        zeros, zero_tables = fill_zero(nc, s, pool_set)
        with nc.Block() as block:

            @block.scalar
            def _(act):
                zero_tables(act, tables[:1])
                act.wait_ge(every_loaded, 16)
                zero_tables(act, tables[1:])

            @block.sync
            def _(sp):
                sp.dma_start(key[:], key_dram.rearrange("(p t) -> p t", p=P)).then_inc(key_loaded, 16)
                sp.dma_start(before[:], a["before"]).then_inc(const_loaded, 16)
                sp.wait_ge(sortkey_ready, 1)
                sp.dma_start(keys_dram.rearrange("(k p) -> p k", p=P), sortkey[:],
                             allow_slow_non_contiguous=True).then_inc(sortkey_stored, 16)
                sp.wait_ge(sortkey_stored, 16)
                sp.dma_start(every[:], across(keys_dram, TILES * P)).then_inc(every_loaded, 16)
                sp.wait_ge(scattered, 16 * TILES)
                sp.dma_start(perm[:, 0:TILES, :], order_dram.rearrange("(k p) c -> p k c", p=P)).then_inc(perm_loaded, 16)

            @block.gpsimd
            def _(pool):
                pool.iota(iota_low[:], [[1, P]], base=0, channel_multiplier=0, allow_small_or_imprecise_dtypes=True)
                pool.iota(node[:], [[P, ALL_TILES]], base=0, channel_multiplier=1)
                pool.memset(ones[:], 1.0)
                pool.memset(onesf[:], 1.0)
                pool.memset(spare[:], 0)
                pool.memset(zeros[:], 0.0)
                pool.drain().then_inc(pool_set, 1)
                for k in range(TILES):
                    if k == 0:
                        pool.wait_ge(record_ready, 1)
                    pool.indirect_dma_start(out=order_dram, in_=record[:, k, :], in_offset=None,
                                            out_offset=bass.IndirectOffsetOnAxis(ap=rank[:, k:k + 1], axis=0))\
                        .then_inc(scattered, 16)
                pool.wait_ge(degf_ready, 1)
                pool.partition_all_reduce(most[:], degf[:], P, bass.bass_isa.ReduceOp.max).then_inc(most_ready, 1)
                pool.wait_ge(scattered, 16 * TILES)

            @block.tensor
            def _(pe):
                pe.wait_ge(zero_set, 1)
                for u in range(2):
                    pe.sem_inc(hot_used[u], 1)
                nc.tensor.matmul(p_deg[:, 0:TILES], zero[:], zero[:, 0:TILES], start=True, stop=False)
                with pe.Fori(0, BLOCKS // 2) as i:
                    for u in range(2):
                        pe.wait_ge(hot_ready[u], i + 1)
                        for t in range(BLOCK):
                            last = nc.tensor.matmul(p_deg[:, 0:TILES], one_low[u][:, t, :], one_high[u][:, t, :],
                                                    start=False, stop=False)
                        last.then_inc(hot_used[u], 1)
                nc.tensor.matmul(p_deg[:, 0:TILES], zero[:], zero[:, 0:TILES], start=False, stop=True).then_inc(deg_summed, 1)
                pe.wait_ge(const_loaded, 16)
                pe.wait_ge(pool_set, 1)
                pe.wait_ge(deg_ready, 1)
                nc.tensor.matmul(p_sum[:, 0:TILES], before[:], deg[:], start=True, stop=True)
                nc.tensor.matmul(p_sum[:, 256:256 + TILES], ones[:], deg[:], start=True, stop=True)\
                    .then_inc(prefix_ready, 1)

            @block.vector
            def _(dve):
                dve.memset(zero[:], 0.0).then_inc(zero_set, 1)
                dve.wait_ge(key_loaded, 16)
                dve.wait_ge(pool_set, 1)
                dve.tensor_scalar(part[:], key[:], P - 1, None, ALU.bitwise_and)
                dve.drain()
                dve.tensor_copy(low[:], part[:])
                dve.drain()
                dve.tensor_scalar(part[:], key[:], 7, None, ALU.logical_shift_right)
                dve.drain()
                dve.tensor_copy(high[:], part[:])
                dve.drain()
                with dve.Fori(0, BLOCKS // 2) as i:
                    for u in range(2):
                        dve.wait_ge(hot_used[u], i + 1)
                        at = bass.ds((i * 2 + u) * BLOCK, BLOCK)
                        dve.tensor_tensor(one_low[u][:], iota_low[:].rearrange("p (a n) -> p a n", a=1).to_broadcast([P, BLOCK, P]),
                                          low[:, at].rearrange("p (t a) -> p t a", a=1).to_broadcast([P, BLOCK, P]),
                                          ALU.is_equal)
                        dve.tensor_tensor(one_high[u][:], iota_low[:, 0:TILES].rearrange("p (a n) -> p a n", a=1).to_broadcast([P, BLOCK, TILES]),
                                          high[:, at].rearrange("p (t a) -> p t a", a=1).to_broadcast([P, BLOCK, TILES]),
                                          ALU.is_equal)
                        dve.drain().then_inc(hot_ready[u], 1)
                dve.wait_ge(deg_summed, 1)
                dve.tensor_copy(deg[:], p_deg[:, 0:TILES]).then_inc(deg_ready, 1)
                dve.tensor_copy(nodef[:], node[:, 0:TILES])
                dve.drain()
                dve.tensor_scalar(sortkey[:], deg[:], 4000.0, 4096.0, ALU.min, ALU.mult)
                dve.drain()
                dve.tensor_tensor(sortkey[:], sortkey[:], nodef[:], ALU.add)
                dve.drain().then_inc(sortkey_ready, 1)
                dve.wait_ge(prefix_ready, 1)
                dve.tensor_copy(total[:], p_sum[:, 256:256 + TILES])
                dve.drain()
                dve.tensor_tensor_scan(start[:], onesf[:, 0:TILES], total[:], 0.0, ALU.mult, ALU.add)
                dve.drain()
                dve.tensor_tensor(start[:], start[:], total[:], ALU.subtract)
                dve.drain()
                dve.tensor_tensor(start[:], start[:], p_sum[:, 0:TILES], ALU.add)
                dve.drain()
                dve.tensor_copy(record[:, :, NODE], node[:, 0:TILES])
                dve.tensor_copy(record[:, :, START], start[:])
                dve.tensor_copy(record[:, :, DEGREE], deg[:])
                dve.tensor_copy(record[:, :, TARGET], node[:, 0:TILES])
                dve.wait_ge(every_loaded, 16)
                for k in range(TILES):
                    dve.tensor_scalar(above[:], every[:], sortkey[:, k:k + 1], 0.0, ALU.is_gt, ALU.add,
                                      accum_out=rankf[:, k:k + 1])
                    dve.drain()
                dve.tensor_copy(rank[:], rankf[:])
                dve.drain().then_inc(record_ready, 1)
                for k in range(3):
                    dve.tensor_copy(perm[:, TILES + k, NODE:NODE + 1], node[:, 0:1])
                    dve.tensor_copy(perm[:, TILES + k, START:TARGET], spare[:, k, START:TARGET])
                    dve.tensor_copy(perm[:, TILES + k, TARGET:TARGET + 1], node[:, TILES:TILES + 1])
                dve.wait_ge(perm_loaded, 16)
                dve.tensor_copy(degf[:], perm[:, 0:TILES, DEGREE]).then_inc(degf_ready, 1)
                dve.wait_ge(most_ready, 1)
                dve.memset(workf[:], 1.0)
                dve.drain()
                dve.tensor_scalar(workf[:, 0:TILES], most[:], float(R - 1), float(R), ALU.add, ALU.max)
                dve.drain()
                dve.tensor_scalar(workf[:, TILES:ALL_TILES], workf[:, TILES:ALL_TILES], float(R - 1), None, ALU.add)
                dve.drain()
                dve.tensor_copy(bodies[:], workf[:])
                dve.drain()
                dve.tensor_scalar(bodies[:], bodies[:], R.bit_length() - 1, None, ALU.logical_shift_right)
                dve.drain()
                table = counts[:].rearrange("p (k c) -> p k c", c=8)
                dve.tensor_scalar(table[:, :, N_MAIN], bodies[0:1, :], float(MAIN), None, ALU.min)
                dve.tensor_scalar(table[:, :, N_EXTRA], bodies[0:1, :], float(MAIN), 0.0, ALU.subtract, ALU.max)
                dve.drain()

                dve.tensor_scalar(workf[:, 0:TILES], most[:], 1.0, float(SLOTS), ALU.max, ALU.min)
                dve.drain()
                dve.tensor_scalar(steps[:], workf[:, 0:TILES], float(STEP - 1), None, ALU.add)
                dve.drain()
                dve.tensor_scalar(steps[:], steps[:], STEP.bit_length() - 1, None, ALU.logical_shift_right)
                dve.drain()
                dve.tensor_copy(table[:, 0:TILES, STEPS], steps[0:1, :])
                dve.drain()

                def sum_before(to, of):
                    dve.tensor_copy(workf[0:1, :], of)
                    dve.drain()
                    dve.tensor_tensor_scan(sumf[0:1, :], onesf[0:1, :], workf[0:1, :], 0.0, ALU.mult, ALU.add)
                    dve.drain()
                    dve.tensor_tensor(sumf[0:1, :], sumf[0:1, :], workf[0:1, :], ALU.subtract)
                    dve.drain()
                    dve.tensor_copy(to, sumf[0:1, :])
                    dve.drain()

                packed = s_packed[0:1, :]
                sum_before(table[:, :, BASE], bodies[0:1, :])
                dve.tensor_scalar(packed, sumf[0:1, :], 2.0, None, ALU.mult)
                dve.tensor_scalar(workf[0:1, :], table[:, :, N_EXTRA], 0.0, None, ALU.is_gt)
                dve.drain()
                dve.tensor_tensor(packed, packed, workf[0:1, :], ALU.add)
                dve.drain()
                dve.scalar_tensor_tensor(packed, packed, 16.0, table[:, :, N_MAIN], ALU.mult, ALU.add)
                dve.drain()
                dve.tensor_copy(table[:, :, HEAD], packed)
                dve.drain()
                dve.memset(packed, 0.0)
                sum_before(table[:, :, EXTRA_BASE], table[:, :, N_EXTRA])
                for u in range(SETS):
                    for odd in range(2):
                        first = body_of(u, odd)
                        dve.tensor_scalar(work[0:1, odd::2], table[:, odd::2, N_MAIN], float(SETS - 1 - first), None, ALU.add)
                    dve.drain()
                    dve.tensor_scalar(work[0:1, :], work[0:1, :], SETS.bit_length() - 1, None, ALU.logical_shift_right)
                    dve.drain()
                    sum_before(table[:, :, USES], work[0:1, :])
                    dve.scalar_tensor_tensor(packed, sumf[0:1, :], float(2 ** (u * USE_BITS)), packed, ALU.mult, ALU.add)
                    dve.drain()
                dve.tensor_copy(table[:, :, USES], packed)
                dve.drain().then_inc(done, 1)
                dve.wait_ge(done, 1)


def attention_phase(nc, name, a, perm, counts, kv_dram, q_dram, src_dram, edge_dram, out_dram):
    HEADS = 8
    HD = F // HEADS
    ROW = kv_dram.shape[1]
    MSG = HEADS * (HD + 1)
    BIG = 1e30
    with ExitStack() as ctx:
        s = Scope(nc, ctx, name)
        node_at = [s.sb(f"node_at{u}", [P, 4], i32) for u in range(2)]
        target_at = [s.sb(f"target_at{u}", [P, 1], i32) for u in range(2)]
        index = [s.sb(f"index{u}", [P, SLOTS], i32) for u in range(2)]
        edge = [s.sb(f"edge{u}", [P, SLOTS * HEADS]) for u in range(2)]
        own = [s.sb(f"own{u}", [P, F]) for u in range(2)]
        filled = [s.sb(f"filled{u}", [P, 1]) for u in range(2)]
        out = [s.sb(f"out{u}", [P, F]) for u in range(2)]
        got = [s.sb(f"got{i}", [P, R, ROW]) for i in range(SETS)]
        start_x = s.sb("start_x", [P, 1], i32)
        index_x = s.sb("index_x", [P, R], i32)
        edge_x = s.sb("edge_x", [P, R * HEADS])
        slot = s.sb("slot", [P, SLOTS])
        degree = s.sb("degree", [P, 1])
        valid = s.sb("valid", [P, SLOTS])
        valid_x = s.sb("valid_x", [P, R])
        pen = s.sb("pen", [P, SLOTS])
        pen_x = s.sb("pen_x", [P, R])
        left = s.sb("left", [P, 1])
        msg = [s.sb(f"msg{v}", [P, R, HEADS, HD + 1]) for v in range(2)]
        weight = [s.sb(f"weight{v}", [P, R + 1, HEADS]) for v in range(2)]
        ident = s.sb("ident", [P, P])
        q = s.sb("q", [P, F])
        prod = s.sb("prod", [P, R, F])
        score = s.sb("score", [P, R + 1, HEADS])
        peak = s.sb("peak", [P, HEADS])
        acc = s.sb("acc", [P, MSG])
        inv = s.sb("inv", [P, HEADS])
        primed = s.sb("primed", [1, 2])
        p_msg = s.ps("p_msg", [P, 512])
        const_loaded = s.sem("const_loaded")
        pool_set = s.sem("pool_set")
        node_ready = s.sem("node_ready")
        index_loaded = [s.sem(f"index_loaded{u}") for u in range(2)]
        edge_loaded = [s.sem(f"edge_loaded{u}") for u in range(2)]
        own_loaded = [s.sem(f"own_loaded{u}") for u in range(2)]
        gathered = [s.sem(f"gathered{i}") for i in range(SETS)]
        released = [s.sem(f"released{i}") for i in range(SETS)]
        extra_done = s.sem("extra_done")
        start_x_ready = s.sem("start_x_ready")
        index_x_loaded = s.sem("index_x_loaded")
        edge_x_loaded = s.sem("edge_x_loaded")
        gathered_x = s.sem("gathered_x")
        pool_waited = s.sem("pool_waited")
        shifted = s.sem("shifted")
        weights_ready = s.sem("weights_ready")
        messages_ready = s.sem("messages_ready")
        summed = s.sem("summed")
        out_ready = s.sem("out_ready")
        scattered = [s.sem(f"scattered{u}") for u in range(2)]

        def rows_at(ap):
            return bass.IndirectOffsetOnAxis(ap=ap, axis=0)

        def count(eng, t, column, low, high):
            return eng.value_load(counts[0:1, bass.ds(t * 8 + column, 1)], min_val=low, max_val=high)

        def unpack(eng, t):
            head = count(eng, t, HEAD, 1, 32 * E)
            return head & 15, head & 16, head // 32

        def uses_of(eng, t):
            packed = count(eng, t, USES, 0, 2 ** 24 - 1)
            return [(packed // 2 ** (i * USE_BITS)) & (2 ** USE_BITS - 1) for i in range(SETS)]

        def main_bodies(eng, u, n_main, base, uses, main):
            for j in range(MAIN):
                def run():
                    st = set_of(j, u)
                    main(st, j * R, base + j, j % 2, uses[st] + j // SETS if uses else None, j == 0)

                if j == 0:
                    run()
                else:
                    with eng.If(n_main > j):
                        run()

        def extra_bodies(eng, t, has_extra, first, extra, before=None):
            with eng.If(has_extra > 0):
                n_extra = count(eng, t, N_EXTRA, 1, E)
                extra_base = count(eng, t, EXTRA_BASE, 0, E)
                if before:
                    before()
                with eng.Fori(0, n_extra) as i:
                    extra(first + i, extra_base + i)

        with nc.Block() as block:

            @block.sync
            def _(sp):
                sp.dma_start(ident[:], a["ident"]).then_inc(const_loaded, 16)

            @block.gpsimd
            def _(pool):
                pool.iota(slot[:], [[1, SLOTS]], base=0, channel_multiplier=0, allow_small_or_imprecise_dtypes=True)
                pool.drain().then_inc(pool_set, 1)
                for i in range(SETS):
                    pool.sem_inc(released[i], 1)

                def wait_apart(sem, value):
                    pool.wait_ge(sem, value)
                    pool.sem_inc(pool_waited, 1)

                def prefetch(u):
                    node = node_at[u][:, NODE:NODE + 1]
                    start = node_at[u][:, START:START + 1]
                    pool.indirect_dma_start(out=index[u][:], out_offset=None, in_=src_dram, in_offset=rows_at(start))\
                        .then_inc(index_loaded[u], 16)
                    pool.indirect_dma_start(out=edge[u][:], out_offset=None, in_=edge_dram, in_offset=rows_at(start))\
                        .then_inc(edge_loaded[u], 16)
                    pool.indirect_dma_start(out=own[u][:], out_offset=None, in_=q_dram, in_offset=rows_at(node))\
                        .then_inc(own_loaded[u], 16)

                def scatter(u):
                    pool.indirect_dma_start(out=out_dram, in_=out[u][:], in_offset=None,
                                            out_offset=rows_at(target_at[u][:, 0:1])).then_inc(scattered[u], 16)

                for u in range(2):
                    pool.dma_start(primed[0:1, u:u + 1], edge_dram[0:1, 0:1]).then_inc(scattered[u], 16)
                pool.wait_ge(node_ready, 1)
                prefetch(0)
                with pool.Fori(0, LOOP_TILES // 2) as pair:
                    for u in range(2):
                        t = pair * 2 + u
                        n_main, has_extra, base = unpack(pool, t)
                        uses = uses_of(pool, t)
                        pool.wait_ge(index_loaded[u], 16 * pair + 16)

                        def gather(j):
                            st = set_of(j, u)
                            wait_apart(released[st], uses[st] + (j // SETS + 1))
                            for r in range(R):
                                pool.indirect_dma_start(out=got[st][:, r, :], out_offset=None, in_=kv_dram,
                                                        in_offset=rows_at(index[u][:, j * R + r:j * R + r + 1]))\
                                    .then_inc(gathered[st], 16)

                        for j in range(MAIN):
                            if j == 0:
                                gather(j)
                            else:
                                with pool.If(n_main > j):
                                    gather(j)
                            if j == MAIN // 4:
                                wait_apart(node_ready, t + 2)
                                prefetch(1 - u)

                        def extra(b, x):
                            wait_apart(start_x_ready, x + 1)
                            pool.indirect_dma_start(out=index_x[:], out_offset=None, in_=src_dram,
                                                    in_offset=rows_at(start_x[:, 0:1])).then_inc(index_x_loaded, 16)
                            pool.indirect_dma_start(out=edge_x[:], out_offset=None, in_=edge_dram,
                                                    in_offset=rows_at(start_x[:, 0:1])).then_inc(edge_x_loaded, 16)
                            wait_apart(index_x_loaded, (x + 1) * 16)
                            for r in range(R):
                                pool.indirect_dma_start(out=got[0][:, r, :], out_offset=None, in_=kv_dram,
                                                        in_offset=rows_at(index_x[:, r:r + 1])).then_inc(gathered_x, 16)
                            wait_apart(extra_done, x + 1)

                        extra_bodies(pool, t, has_extra, base + n_main, extra)
                        if u == 0:
                            with pool.If(pair > 0):
                                wait_apart(out_ready, t)
                                scatter(1)
                        else:
                            wait_apart(out_ready, t)
                            scatter(0)
                pool.wait_ge(out_ready, LOOP_TILES)
                scatter(1)
                for u in range(2):
                    pool.wait_ge(scattered[u], 16 * (LOOP_TILES // 2) + 16)
                for sem in (index_loaded[0], edge_loaded[0], own_loaded[0]):
                    pool.wait_ge(sem, 16 * (LOOP_TILES // 2) + 16)

            @block.scalar
            def _(act):
                with act.Fori(0, LOOP_TILES // 2) as pair:
                    for u in range(2):

                        def body(b, v):
                            act.wait_ge(shifted, b + 1)
                            act.activation(weight[v][:], score[:], ACT.Exp).then_inc(weights_ready, 1)

                        n_main, has_extra, base = unpack(act, pair * 2 + u)
                        main_bodies(act, u, n_main, base, None, lambda its, slots, b, v, use, first: body(b, v))
                        extra_bodies(act, pair * 2 + u, has_extra, base + n_main, lambda b, x: body(b, 0))

            @block.tensor
            def _(pe):
                pe.wait_ge(const_loaded, 16)
                with pe.Fori(0, LOOP_TILES // 2) as pair:
                    for u in range(2):

                        def body(b, v):
                            pe.wait_ge(messages_ready, b + 1)
                            for r in range(R):
                                last = nc.tensor.matmul(p_msg[:, 0:MSG], ident[:],
                                                        msg[v][:, r].rearrange("p h d -> p (h d)"),
                                                        start=(r == 0), stop=(r == R - 1))
                            last.then_inc(summed, 1)

                        n_main, has_extra, base = unpack(pe, pair * 2 + u)
                        main_bodies(pe, u, n_main, base, None, lambda its, slots, b, v, use, first: body(b, v))
                        extra_bodies(pe, pair * 2 + u, has_extra, base + n_main, lambda b, x: body(b, 0))

            @block.vector
            def _(dve):
                def heads(ap):
                    return ap.rearrange("p (h d) -> p h d", h=HEADS)

                def over(ap, shape, pattern, **kw):
                    return ap.rearrange(pattern, **kw).to_broadcast(shape)

                def set_node(u, t):
                    dve.tensor_copy(node_at[u][:].rearrange("p (a c) -> p a c", a=1), perm[:, bass.ds(t, 1), :])\
                        .then_inc(node_ready, 1)

                def begin(u, pair, t):
                    dve.wait_ge(node_ready, t + 1)
                    dve.wait_ge(index_loaded[u], 16 * pair + 16)
                    dve.wait_ge(edge_loaded[u], 16 * pair + 16)
                    dve.wait_ge(own_loaded[u], 16 * pair + 16)
                    dve.tensor_copy(degree[:], node_at[u][:, DEGREE:DEGREE + 1])
                    dve.wait_ge(scattered[u], 16 * pair + 16)
                    dve.tensor_copy(target_at[u][:], node_at[u][:, TARGET:TARGET + 1])
                    set_node(1 - u, t + 1)
                    dve.drain()
                    dve.tensor_scalar(valid[:], slot[:], degree[:, 0:1], None, ALU.is_lt)
                    dve.tensor_scalar(filled[u][:], degree[:], 0.0, None, ALU.is_gt)
                    dve.tensor_scalar(left[:], degree[:], float(SLOTS), None, ALU.subtract)
                    dve.tensor_scalar(start_x[:], node_at[u][:, START:START + 1], float(SLOTS), float(E),
                                      ALU.add, ALU.min)
                    dve.tensor_scalar(q[:], own[u][:], float(HD) ** 0.5, None, ALU.mult)
                    dve.memset(score[:, R, :], -BIG)
                    dve.drain()
                    ev = edge[u][:].rearrange("p (s h) -> p s h", h=HEADS)
                    dve.tensor_tensor(ev, ev, over(valid[:], [P, SLOTS, HEADS], "p (s a) -> p s a", a=1), ALU.mult)
                    dve.tensor_scalar(pen[:], valid[:], 1.0, BIG, ALU.subtract, ALU.mult)
                    dve.drain()
                    dve.tensor_tensor(ev, ev, over(pen[:], [P, SLOTS, HEADS], "p (s a) -> p s a", a=1), ALU.add)
                    dve.drain()

                def fold(b, v):
                    dve.tensor_tensor(heads(acc[:]), heads(acc[:]),
                                      over(weight[v][:, R, :], [P, HEADS, HD + 1], "p (h a) -> p h a", a=1), ALU.mult)
                    dve.drain()
                    dve.wait_ge(summed, b + 1)
                    dve.tensor_tensor(acc[:], acc[:], p_msg[:, 0:MSG], ALU.add)

                def body(rows_, v, b, ev, first):
                    dve.tensor_tensor(prod[:], rows_[:, :, 0:F], over(q[:], [P, R, F], "p (a n) -> p a n", a=1), ALU.mult)
                    dve.drain()
                    flat = score[:, 0:R, :].rearrange("p r h -> p (r h)")
                    dve.tensor_reduce(flat, prod[:].rearrange("p r (h d) -> p (r h) d", d=HD), AX.X, ALU.add)
                    dve.drain()
                    dve.tensor_tensor(flat, flat, ev, ALU.add)
                    dve.drain()
                    dve.tensor_reduce(peak[:], score[:].rearrange("p r h -> p h r"), AX.X, ALU.max)
                    dve.drain()
                    dve.tensor_tensor(score[:], score[:], over(peak[:], [P, R + 1, HEADS], "p (a h) -> p a h", a=1),
                                      ALU.subtract).then_inc(shifted, 1)
                    if not first:
                        fold(b - 1, 1 - v)
                    dve.wait_ge(weights_ready, b + 1)
                    dve.tensor_copy(score[:, R, :], peak[:])
                    dve.tensor_copy(msg[v][:, :, :, HD], weight[v][:, 0:R, :])
                    dve.tensor_tensor(msg[v][:, :, :, 0:HD],
                                      rows_[:, :, F:2 * F].rearrange("p r (h d) -> p r h d", h=HEADS),
                                      weight[v][:, 0:R, :].rearrange("p r (h a) -> p r h a", a=1)
                                      .to_broadcast([P, R, HEADS, HD]), ALU.mult)
                    dve.drain().then_inc(messages_ready, 1)

                def last_fold(n_main, b):
                    with dve.If((n_main & 1) > 0):
                        fold(b, 0)
                    with dve.If((n_main & 1) < 1):
                        fold(b, 1)
                    dve.drain()

                dve.wait_ge(pool_set, 1)
                dve.wait_ge(const_loaded, 16)
                set_node(0, 0)
                begin(0, 0, 0)
                dve.memset(acc[:], 0.0)
                dve.drain()
                with dve.Fori(0, LOOP_TILES // 2) as pair:
                    for u in range(2):
                        t = pair * 2 + u

                        def main(its, slots, b, v, use, first):
                            dve.wait_ge(gathered[its], (use + 1) * (16 * R))
                            body(got[its], v, b, edge[u][:, slots * HEADS:(slots + R) * HEADS], first)
                            dve.drain().then_inc(released[its], 1)

                        def extra(b, x):
                            dve.drain().then_inc(start_x_ready, 1)
                            dve.tensor_scalar(valid_x[:], slot[:, 0:R], left[:, 0:1], None, ALU.is_lt)
                            dve.drain()
                            dve.tensor_scalar(left[:], left[:], float(R), None, ALU.subtract)
                            dve.wait_ge(edge_x_loaded, (x + 1) * 16)
                            ex = edge_x[:].rearrange("p (s h) -> p s h", s=R)
                            dve.tensor_tensor(ex, ex, over(valid_x[:], [P, R, HEADS], "p (r a) -> p r a", a=1), ALU.mult)
                            dve.tensor_scalar(pen_x[:], valid_x[:], 1.0, BIG, ALU.subtract, ALU.mult)
                            dve.drain()
                            dve.tensor_tensor(ex, ex, over(pen_x[:], [P, R, HEADS], "p (r a) -> p r a", a=1), ALU.add)
                            dve.drain()
                            dve.wait_ge(gathered_x, (x + 1) * (16 * R))
                            dve.tensor_scalar(start_x[:], start_x[:], float(R), float(E), ALU.add, ALU.min)
                            dve.wait_ge(summed, b)
                            body(got[0], 0, b, edge_x[:], True)
                            fold(b, 0)
                            dve.drain().then_inc(extra_done, 1)

                        n_main, has_extra, base = unpack(dve, t)
                        main_bodies(dve, u, n_main, base, uses_of(dve, t), main)
                        extra_bodies(dve, t, has_extra, base + n_main, extra,
                                     before=lambda: last_fold(n_main, base + n_main - 1))
                        begin(1 - u, pair + u, t + 1)
                        with dve.If(has_extra < 1):
                            last_fold(n_main, base + n_main - 1)
                        dve.reciprocal(inv[:], heads(acc[:])[:, :, HD])
                        dve.drain()
                        dve.tensor_scalar(inv[:], inv[:], filled[u][:, 0:1], None, ALU.mult)
                        dve.drain()
                        dve.tensor_tensor(heads(out[u][:]), heads(acc[:])[:, :, 0:HD],
                                          over(inv[:], [P, HEADS, HD], "p (h a) -> p h a", a=1), ALU.mult)
                        dve.drain().then_inc(out_ready, 1)
                        dve.memset(acc[:], 0.0)
                        dve.drain()


CAP = 3e38


def fill_zero(nc, s, ready):
    zeros = s.sb("zeros", [P, NP])
    zeros_stored = s.sem("zeros_stored")
    so_far = []

    def run(eng, tables):
        eng.wait_ge(ready, 1)
        for m in tables:
            for k in range(TILES):
                eng.dma_start(m[k * P * NP:(k + 1) * P * NP, :].rearrange("(p n) a -> p (n a)", p=P), zeros[:])\
                    .then_inc(zeros_stored, 16)
            so_far.append(m)
        eng.wait_ge(zeros_stored, 16 * TILES * len(so_far))

    return zeros, run


def find_cells(nc, s, perm, src_dram, weight_dram, cell_count, cell_weight, taken, weights):
    slot = s.sb("slot", [P, SLOTS])
    nodef = s.sb("nodef", [P, TILES])
    rowf = s.sb("rowf", [P, TILES])
    degf = s.sb("degf", [P, TILES])
    slot_set = s.sem("slot_set")
    slot_index_loaded = s.sem("slot_index_loaded")
    slot_weight_loaded = s.sem("slot_weight_loaded")

    def by_tile(v):
        return v.rearrange("p (t a) -> p t a", a=1).to_broadcast([P, TILES, SLOTS])

    def gather(pool):
        pool.iota(slot[:], [[1, SLOTS]], base=0, channel_multiplier=0, allow_small_or_imprecise_dtypes=True)\
            .then_inc(slot_set, 1)
        for to, of, sem in ((cell_weight, src_dram, slot_index_loaded), (weights, weight_dram, slot_weight_loaded)):
            for k in range(TILES):
                pool.indirect_dma_start(out=to[:, k, :], out_offset=None, in_=of,
                                        in_offset=bass.IndirectOffsetOnAxis(ap=perm[:, k, START:START + 1], axis=0))\
                    .then_inc(sem, 16)

    def compute(dve):
        dve.tensor_copy(nodef[:], perm[:, 0:TILES, NODE])
        dve.tensor_copy(degf[:], perm[:, 0:TILES, DEGREE])
        dve.drain()
        dve.tensor_scalar(rowf[:], nodef[:], float(NP), None, ALU.mult)
        dve.wait_ge(slot_set, 1)
        dve.tensor_tensor(taken[:], slot[:].rearrange("p (a s) -> p a s", a=1).to_broadcast([P, TILES, SLOTS]),
                          by_tile(degf[:]), ALU.is_lt)
        dve.drain()
        dve.wait_ge(slot_index_loaded, 16 * TILES)
        dve.tensor_tensor(cell_count[:], cell_weight[:], by_tile(rowf[:]), ALU.add)
        dve.drain()
        dve.scalar_tensor_tensor(cell_weight[:], cell_weight[:], float(NP), by_tile(nodef[:]), ALU.mult, ALU.add)
        dve.wait_ge(slot_weight_loaded, 16 * TILES)
        dve.tensor_tensor(weights[:], weights[:], taken[:], ALU.mult)
        dve.drain()

    return gather, compute


def spill_phase(nc, name, perm, counts, src_dram, weight_dram, count_table, weight_table):
    with ExitStack() as ctx:
        s = Scope(nc, ctx, name)
        record = s.sb("record", [P, 4], i32)
        nodef = s.sb("nodef", [P, 1])
        rowf = s.sb("rowf", [P, 1])
        edgef = s.sb("edgef", [P, 1])
        endf = s.sb("endf", [P, 1])
        edge = s.sb("edge", [P, 1], i32)
        source = s.sb("source", [P, 1], i32)
        weight = s.sb("weight", [P, 1])
        taken = s.sb("taken", [P, 1])
        cell_count = s.sb("cell_count", [P, 1], i32)
        cell_weight = s.sb("cell_weight", [P, 1], i32)
        edge_ready = s.sem("edge_ready")
        cells_ready = s.sem("cells_ready")
        source_loaded = s.sem("source_loaded")
        weight_loaded = s.sem("weight_loaded")
        count_added = s.sem("count_added")
        weight_added = s.sem("weight_added")
        pool_waited = s.sem("pool_waited")

        def rows_at(ap):
            return bass.IndirectOffsetOnAxis(ap=ap, axis=0)

        def slots(eng, body):
            total = eng.value_load(counts[0:1, (ALL_TILES - 1) * 8 + EXTRA_BASE:(ALL_TILES - 1) * 8 + EXTRA_BASE + 1],
                                   min_val=0, max_val=E)
            with eng.If(total > 0):
                with eng.Fori(0, TILES) as t:
                    n = eng.value_load(counts[0:1, bass.ds(t * 8 + N_EXTRA, 1)], min_val=0, max_val=E)
                    base = eng.value_load(counts[0:1, bass.ds(t * 8 + EXTRA_BASE, 1)], min_val=0, max_val=E)
                    with eng.If(n > 0):
                        body(t, n, base)
            return total

        with nc.Block() as block:

            @block.gpsimd
            def _(pool):
                def tile(t, n, base):
                    with pool.Fori(0, n * R) as i:
                        at = base * R + i + 1
                        pool.wait_ge(edge_ready, at)
                        pool.sem_inc(pool_waited, 1)
                        pool.indirect_dma_start(out=source[:], out_offset=None, in_=src_dram,
                                                in_offset=rows_at(edge[:, 0:1])).then_inc(source_loaded, 16)
                        pool.indirect_dma_start(out=weight[:], out_offset=None, in_=weight_dram,
                                                in_offset=rows_at(edge[:, 0:1])).then_inc(weight_loaded, 16)
                        pool.wait_ge(cells_ready, at)
                        pool.sem_inc(pool_waited, 1)
                        pool.indirect_dma_start(out=count_table, in_=taken[:], in_offset=None,
                                                out_offset=rows_at(cell_count[:, 0:1]), compute_op=ALU.add)\
                            .then_inc(count_added, 16)
                        pool.indirect_dma_start(out=weight_table, in_=weight[:], in_offset=None,
                                                out_offset=rows_at(cell_weight[:, 0:1]), compute_op=ALU.add)\
                            .then_inc(weight_added, 16)
                        pool.wait_ge(count_added, at * 16)
                        pool.wait_ge(weight_added, at * 16)

                slots(pool, tile)

            @block.vector
            def _(dve):
                def tile(t, n, base):
                    dve.tensor_copy(record[:].rearrange("p (a c) -> p a c", a=1), perm[:, bass.ds(t, 1), :])
                    dve.drain()
                    dve.tensor_copy(nodef[:], record[:, NODE:NODE + 1])
                    dve.tensor_copy(edgef[:], record[:, START:START + 1])
                    dve.drain()
                    dve.tensor_scalar(rowf[:], nodef[:], float(NP), None, ALU.mult)
                    dve.tensor_tensor(endf[:], edgef[:], record[:, DEGREE:DEGREE + 1], ALU.add)
                    dve.drain()
                    dve.tensor_scalar(edgef[:], edgef[:], float(SLOTS), None, ALU.add)
                    dve.drain()
                    with dve.Fori(0, n * R) as i:
                        at = base * R + i + 1
                        dve.tensor_scalar(edge[:], edgef[:], float(E), None, ALU.min)
                        dve.drain().then_inc(edge_ready, 1)
                        dve.wait_ge(source_loaded, at * 16)
                        dve.wait_ge(weight_loaded, at * 16)
                        dve.tensor_tensor(taken[:], edgef[:], endf[:], ALU.is_lt)
                        dve.tensor_tensor(cell_count[:], source[:], rowf[:], ALU.add)
                        dve.scalar_tensor_tensor(cell_weight[:], source[:], float(NP), nodef[:], ALU.mult, ALU.add)
                        dve.drain()
                        dve.tensor_tensor(weight[:], weight[:], taken[:], ALU.mult)
                        dve.tensor_scalar(edgef[:], edgef[:], 1.0, None, ALU.add)
                        dve.drain().then_inc(cells_ready, 1)
                        dve.wait_ge(count_added, at * 16)
                        dve.wait_ge(weight_added, at * 16)

                slots(dve, tile)


def add_cells(nc, s, counts, jobs):
    at = [s.sb(f"add_at{v}", [P, GROUP, 1], i32) for v in range(2)]
    value = [s.sb(f"add_value{v}", [P, GROUP, 1]) for v in range(2)]
    primed = s.sb("primed", [1, GROUP])
    added = [s.sem(f"added{k}") for k in range(GROUP)]
    picked = s.sem("picked")
    added_waited = s.sem("added_waited")

    def run(pool):
        for k in range(GROUP):
            pool.dma_start(primed[0:1, k:k + 1], jobs[0][0][2][0:1, :]).then_inc(added[k], 16)
        done = 1
        for (cells, values, table), g, part in jobs:
            tiles = slice(g * GROUP, (g + 1) * GROUP)
            n = pool.value_load(counts[0:1, g * GROUP * 8 + STEPS:g * GROUP * 8 + STEPS + 1], min_val=1, max_val=SLOTS // STEP)
            first = n // 2 if part == 1 else 0
            steps = {"all": n, 0: n // 2, 1: (n + 1) // 2}[part]

            def slots(i, done):
                for r in range(STEP):
                    v = r % 2
                    pool.tensor_copy(at[v][:], cells[:, tiles, bass.ds((first + i) * STEP + r, 1)]).then_inc(picked, 1)
                    pool.tensor_copy(value[v][:], values[:, tiles, bass.ds((first + i) * STEP + r, 1)]).then_inc(picked, 1)
                    so_far = i * STEP + (done + r)
                    pool.wait_ge(picked, so_far * 2)
                    pool.sem_inc(added_waited, 1)
                    for k in range(GROUP):
                        pool.wait_ge(added[k], so_far * 16)
                        pool.sem_inc(added_waited, 1)
                        pool.indirect_dma_start(out=table, in_=value[v][:, k, :], in_offset=None,
                                                out_offset=bass.IndirectOffsetOnAxis(ap=at[v][:, k, :], axis=0),
                                                compute_op=ALU.add).then_inc(added[k], 16)

            with pool.If(steps > 0):
                with pool.Fori(0, steps) as i:
                    slots(i, done)
            done = steps * STEP + done
        for k in range(GROUP):
            pool.wait_ge(added[k], done * 16)

    return run, None


def dense_phase(nc, name, kind, a, rows_dram, table, x_dram, out_dram, numbers_dram=None, bias_dram=None,
                beside=None):
    separable = kind == "separable"
    HEADS = 2 if separable else 1
    HD = F // HEADS
    C = HD + separable
    PER = 512 // C
    PASSES = 3 if separable else 2
    BLOCKS = -(-TILES // PASSES)
    BANKS = -(-BLOCKS * HEADS // PER)
    row = rows_dram.shape[1]
    passes = [(b, min(b + BLOCKS, TILES)) for b in range(0, TILES, BLOCKS)]
    with ExitStack() as ctx:
        s = Scope(nc, ctx, name)
        h = s.sb("h", [P, TILES, row])
        cell = [s.sb(f"cell{k}", [P, BLOCKS * P]) for k in range(GROUP)]
        x = s.sb("x", [P, BLOCKS, F])
        zero = s.sb("zero", [P, 512])
        value = s.sb("value", [P, BLOCKS * HEADS, HD])
        p_sum = s.ps("p_sum", [P, BANKS * 512])
        if separable:
            hs = s.sb("hs", [P, TILES, HEADS, C])
            number = s.sb("number", [P, HEADS, NP])
            minus = s.sb("minus", [P, TILES, HEADS])
            minus_fifth = s.sb("minus_fifth", [P, TILES, HEADS])
            steep = [s.sb(f"steep{v}", [P, BLOCKS * P]) for v in range(HEADS)]
            flat = [s.sb(f"flat{v}", [P, BLOCKS * P]) for v in range(HEADS)]
            edge = [s.sb(f"edge{v}", [P, BLOCKS * P]) for v in range(HEADS)]
            inv = s.sb("inv", [P, BLOCKS * HEADS])
            none = s.sb("none", [P, BLOCKS * HEADS])
            low = s.sb("low", [P, BLOCKS * HEADS * HD])
        else:
            bias = s.sb("bias", [P, F])
        rows_loaded = s.sem("rows_loaded")
        const_loaded = s.sem("const_loaded")
        number_stored = s.sem("number_stored")
        number_loaded = s.sem("number_loaded")
        zero_set = s.sem("zero_set")
        rows_ready = s.sem("rows_ready")
        cell_loaded = [s.sem(f"cell_loaded{k}") for k in range(GROUP)]
        cell_used = [s.sem(f"cell_used{k}") for k in range(GROUP)]
        x_loaded = s.sem("x_loaded")
        exps_ready = s.sem("exps_ready")
        exps_used = s.sem("exps_used")
        edge_ready = s.sem("edge_ready")
        edge_used = s.sem("edge_used")
        pass_summed = s.sem("pass_summed")
        sums_read = s.sem("sums_read")
        low_ready = s.sem("low_ready")
        low_exp = s.sem("low_exp")
        out_ready = s.sem("out_ready")
        stored = s.sem("stored")
        add_more, _ = beside(s) if beside else (None, None)
        cells_of = table.rearrange("(r c) a -> r (c a)", c=NP)

        def rows_of(dram, b0, b1):
            return dram[b0 * P:b1 * P, :].rearrange("(k p) n -> p k n", p=P)

        with nc.Block() as block:

            @block.sync
            def _(sp):
                sp.dma_start(h[:], rows_dram.rearrange("(k p) n -> p k n", p=P)).then_inc(rows_loaded, 16)
                if separable:
                    sp.wait_ge(rows_loaded, 16)
                    for v in range(HEADS):
                        sp.dma_start(numbers_dram[v * NP:(v + 1) * NP].rearrange("(k p) -> p k", p=P), h[:, :, F + v],
                                     allow_slow_non_contiguous=True).then_inc(number_stored, 16)
                    sp.wait_ge(number_stored, 16 * HEADS)
                    sp.dma_start(number[:].rearrange("p h n -> p (h n)"), across(numbers_dram, HEADS * NP))\
                        .then_inc(number_loaded, 16)
                else:
                    sp.dma_start(bias[:], across(bias_dram, F)).then_inc(const_loaded, 16)
                for n, (b0, b1) in enumerate(passes):
                    if n > 0:
                        sp.wait_ge(out_ready, n)
                        sp.dma_start(rows_of(out_dram, *passes[n - 1]), x[:, 0:passes[n - 1][1] - passes[n - 1][0], :])\
                            .then_inc(stored, 16)
                        sp.wait_ge(stored, 16 * n)
                    sp.dma_start(x[:, 0:b1 - b0, :], rows_of(x_dram, b0, b1)).then_inc(x_loaded, 16)
                sp.wait_ge(out_ready, PASSES)
                sp.dma_start(rows_of(out_dram, *passes[-1]), x[:, 0:passes[-1][1] - passes[-1][0], :]).then_inc(stored, 16)
                sp.wait_ge(stored, 16 * PASSES)

            def load_cells(eng):
                for n, (b0, b1) in enumerate(passes):
                    with eng.Fori(0, GROUPS) as g:
                        for k in range(GROUP):
                            eng.wait_ge(cell_used[k], g + (n * GROUPS + 1))
                            eng.dma_start(cell[k][:, 0:(b1 - b0) * P],
                                          cells_of[bass.ds((g * GROUP + k) * P, P), b0 * P:b1 * P])\
                                .then_inc(cell_loaded[k], 16)

            @block.gpsimd
            def _(pool):
                pool.memset(zero[:], 0.0)
                pool.drain().then_inc(zero_set, 1)
                for k in range(GROUP):
                    pool.sem_inc(cell_used[k], 1)
                if separable:
                    pool.sem_inc(exps_used, 2)
                    pool.sem_inc(edge_used, 2)
                if add_more:
                    add_more(pool)

            @block.scalar
            def _(act):
                if not separable:
                    load_cells(act)
                    return
                act.wait_ge(rows_ready, 1)
                act.wait_ge(number_loaded, 16)
                for n, (b0, b1) in enumerate(passes):
                    w = (b1 - b0) * P
                    with act.Fori(0, GROUPS) as g:
                        for k in range(GROUP):
                            act.wait_ge(cell_used[k], g + (n * GROUPS + 1))
                            act.dma_start(cell[k][:, 0:w], cells_of[bass.ds((g * GROUP + k) * P, P), b0 * P:b1 * P])\
                                .then_inc(cell_loaded[k], 16)
                            for v in range(HEADS):
                                act.wait_ge(exps_used, (g * GROUP + (n * TILES + k)) * HEADS + (v + 1))
                                of = number[:, v, b0 * P:b1 * P]
                                act.activation(steep[v][:, 0:w], of, ACT.Exp, scale=-1.0,
                                               bias=minus[:, bass.ds(g * GROUP + k, 1), v])
                                act.activation(flat[v][:, 0:w], of, ACT.Exp, scale=-0.2,
                                               bias=minus_fifth[:, bass.ds(g * GROUP + k, 1), v]).then_inc(exps_ready, 1)
                    act.wait_ge(low_ready, n + 1)
                    act.activation(low[:, 0:(b1 - b0) * F], low[:, 0:(b1 - b0) * F], ACT.Exp).then_inc(low_exp, 1)

            @block.tensor
            def _(pe):
                pe.wait_ge(zero_set, 1)
                pe.wait_ge(rows_ready, 1)
                for n, (b0, b1) in enumerate(passes):
                    if n > 0:
                        pe.wait_ge(sums_read, n)
                    for b in range(BANKS):
                        nc.tensor.matmul(p_sum[:, b * 512:b * 512 + PER * C], zero[:, 0:P], zero[:, 0:PER * C],
                                         start=True, stop=False)
                    with pe.Fori(0, GROUPS) as g:
                        for k in range(GROUP):
                            if not separable:
                                pe.wait_ge(cell_loaded[k], (g + (n * GROUPS + 1)) * 16)
                            for v in range(HEADS):
                                if separable:
                                    pe.wait_ge(edge_ready, (g * GROUP + (n * TILES + k)) * HEADS + (v + 1))
                                of = edge[v] if separable else cell[k]
                                for b in range(b1 - b0):
                                    unit = b * HEADS + v
                                    to = unit // PER * 512 + unit % PER * C
                                    rhs = hs[:, bass.ds(g * GROUP + k, 1), v, :] if separable else \
                                        h[:, bass.ds(g * GROUP + k, 1), :]
                                    last = nc.tensor.matmul(p_sum[:, to:to + C], of[:, b * P:(b + 1) * P],
                                                            rhs.rearrange("p a d -> p (a d)"), start=False, stop=False)
                                last.then_inc(edge_used if separable else cell_used[k], 1)
                    for b in range(BANKS):
                        last = nc.tensor.matmul(p_sum[:, b * 512:b * 512 + PER * C], zero[:, 0:P], zero[:, 0:PER * C],
                                                start=False, stop=True)
                    last.then_inc(pass_summed, 1)

            @block.vector
            def _(dve):
                dve.wait_ge(rows_loaded, 16)
                if separable:
                    dve.tensor_copy(hs[:, :, :, 0:HD], h[:, :, 0:F].rearrange("p t (h d) -> p t h d", h=HEADS))
                    dve.memset(hs[:, :, :, HD:C], 1.0)
                    dve.tensor_scalar(minus[:], h[:, :, F + HEADS:F + 2 * HEADS], -1.0, None, ALU.mult)
                    dve.tensor_scalar(minus_fifth[:], h[:, :, F + HEADS:F + 2 * HEADS], -0.2, None, ALU.mult)
                else:
                    dve.wait_ge(const_loaded, 16)
                dve.drain().then_inc(rows_ready, 1)
                for n, (b0, b1) in enumerate(passes):
                    w = (b1 - b0) * P
                    units = (b1 - b0) * HEADS
                    if separable:
                        with dve.Fori(0, GROUPS) as g:
                            for k in range(GROUP):
                                dve.wait_ge(cell_loaded[k], (g + (n * GROUPS + 1)) * 16)
                                for v in range(HEADS):
                                    unit = (g * GROUP + (n * TILES + k)) * HEADS + (v + 1)
                                    dve.wait_ge(exps_ready, unit)
                                    dve.scalar_tensor_tensor(steep[v][:, 0:w], steep[v][:, 0:w], CAP, flat[v][:, 0:w],
                                                             ALU.min, ALU.min)
                                    dve.drain()
                                    dve.wait_ge(edge_used, unit)
                                    dve.tensor_tensor(edge[v][:, 0:w], steep[v][:, 0:w], cell[k][:, 0:w], ALU.mult)\
                                       .then_inc(edge_ready, 1)
                                    dve.drain().then_inc(exps_used, 1)
                                dve.drain().then_inc(cell_used[k], 1)
                    dve.wait_ge(pass_summed, n + 1)
                    dve.wait_ge(x_loaded, 16 * (n + 1))
                    xf = x[:, 0:b1 - b0, :].rearrange("p b d -> p (b d)")
                    vf = value[:, 0:units, :].rearrange("p u d -> p (u d)")
                    if separable:
                        def parts(c0, c1):
                            return [(b * PER, min(b * PER + PER, units),
                                     p_sum[:, b * 512:b * 512 + PER * C].rearrange("p (u d) -> p u d", d=C)
                                     [:, 0:min(PER, units - b * PER), c0:c1]) for b in range(-(-units // PER))]

                        for u0, u1, of in parts(HD, C):
                            dve.tensor_copy(inv[:, u0:u1].rearrange("p (u a) -> p u a", a=1), of)
                        dve.drain()
                        dve.tensor_scalar(none[:, 0:units], inv[:, 0:units], 0.0, None, ALU.is_equal)
                        dve.drain()
                        dve.tensor_tensor(inv[:, 0:units], inv[:, 0:units], none[:, 0:units], ALU.add)
                        dve.drain()
                        dve.reciprocal(inv[:, 0:units], inv[:, 0:units])
                        dve.drain()
                        for u0, u1, of in parts(0, HD):
                            dve.tensor_tensor(value[:, u0:u1, :], of,
                                              inv[:, u0:u1].rearrange("p (u a) -> p u a", a=1).to_broadcast([P, u1 - u0, HD]),
                                              ALU.mult)
                        dve.drain().then_inc(sums_read, 1)
                        dve.tensor_scalar(low[:, 0:units * HD], vf, 0.0, None, ALU.min).then_inc(low_ready, 1)
                        dve.scalar_tensor_tensor(xf, vf, 0.0, xf, ALU.max, ALU.add)
                        dve.drain()
                        dve.wait_ge(low_exp, n + 1)
                        dve.scalar_tensor_tensor(xf, low[:, 0:units * HD], -1.0, xf, ALU.add, ALU.add)
                    else:
                        dve.tensor_tensor(value[:, 0:units, :], p_sum[:, 0:units * F].rearrange("p (u d) -> p u d", d=F),
                                          bias[:].rearrange("p (a d) -> p a d", a=1).to_broadcast([P, units, F]), ALU.add)
                        dve.drain().then_inc(sums_read, 1)
                        dve.scalar_tensor_tensor(xf, vf, 0.0, xf, ALU.max, ALU.add)
                    dve.drain().then_inc(out_ready, 1)


def mix_phase(nc, name, src_dram, dst_dram, table, x_dram, out_dram):
    HEADS = 4
    HD = F // HEADS
    row = table.shape[1]
    with ExitStack() as ctx:
        s = Scope(nc, ctx, name)
        left_at = s.sb("left_at", [P, TILES], i32)
        right_at = s.sb("right_at", [P, TILES], i32)
        left = s.sb("left", [P, TILES, row])
        right = s.sb("right", [P, TILES, row])
        x = s.sb("x", [P, TILES, F])
        score = s.sb("score", [P, TILES, HEADS])
        alpha = s.sb("alpha", [P, TILES, HEADS])
        top = s.sb("top", [P, TILES])
        mixed = s.sb("mixed", [P, GROUP, F])
        mean = s.sb("mean", [P, GROUP, HD])
        at_loaded = s.sem("at_loaded")
        x_loaded = s.sem("x_loaded")
        gathered = [s.sem(f"gathered{g}") for g in range(GROUPS)]
        shifted = s.sem("shifted")
        exp_ready = s.sem("exp_ready")
        out_ready = s.sem("out_ready")
        stored = s.sem("stored")
        with nc.Block() as block:

            @block.sync
            def _(sp):
                for to, of in ((left_at, src_dram), (right_at, dst_dram)):
                    sp.dma_start(to[:], of[0:NP, :].rearrange("(k p) a -> p (k a)", p=P),
                                 allow_slow_non_contiguous=True).then_inc(at_loaded, 16)
                sp.dma_start(x[:], x_dram.rearrange("(k p) n -> p k n", p=P)).then_inc(x_loaded, 16)
                for g in range(GROUPS):
                    sp.wait_ge(out_ready, g + 1)
                    sp.dma_start(out_dram[g * GROUP * P:(g + 1) * GROUP * P, :].rearrange("(k p) n -> p k n", p=P),
                                 x[:, g * GROUP:(g + 1) * GROUP, :]).then_inc(stored, 16)
                sp.wait_ge(stored, 16 * GROUPS)

            @block.gpsimd
            def _(pool):
                pool.wait_ge(at_loaded, 32)
                for k in range(TILES):
                    for to, at in ((left, left_at), (right, right_at)):
                        pool.indirect_dma_start(out=to[:, k, :], out_offset=None, in_=table,
                                                in_offset=bass.IndirectOffsetOnAxis(ap=at[:, k:k + 1], axis=0))\
                            .then_inc(gathered[k // GROUP], 16)

            @block.scalar
            def _(act):
                for g in range(GROUPS):
                    t = slice(g * GROUP, (g + 1) * GROUP)
                    act.wait_ge(shifted, g + 1)
                    act.activation(alpha[:, t, :], score[:, t, :], ACT.Exp).then_inc(exp_ready, 1)

            @block.vector
            def _(dve):
                for g in range(GROUPS):
                    t = slice(g * GROUP, (g + 1) * GROUP)

                    def by_tile(v):
                        return v.rearrange("p (t a) -> p t a", a=1).to_broadcast([P, GROUP, HEADS])

                    dve.wait_ge(gathered[g], 2 * GROUP * 16)
                    dve.tensor_tensor(score[:, t, :], left[:, t, F:F + HEADS], right[:, t, F + HEADS:F + 2 * HEADS], ALU.add)
                    dve.drain()
                    dve.scalar_tensor_tensor(score[:, t, :], score[:, t, :], 0.01, score[:, t, :], ALU.mult, ALU.max)
                    dve.drain()
                    dve.tensor_reduce(top[:, t], score[:, t, :], AX.X, ALU.max)
                    dve.drain()
                    dve.tensor_tensor(score[:, t, :], score[:, t, :], by_tile(top[:, t]), ALU.subtract).then_inc(shifted, 1)
                    dve.wait_ge(exp_ready, g + 1)
                    dve.tensor_reduce(top[:, t], alpha[:, t, :], AX.X, ALU.add)
                    dve.drain()
                    dve.reciprocal(top[:, t], top[:, t])
                    dve.drain()
                    dve.tensor_tensor(alpha[:, t, :], alpha[:, t, :], by_tile(top[:, t]), ALU.mult)
                    dve.drain()
                    dve.tensor_tensor(mixed[:].rearrange("p t (h d) -> p t h d", h=HEADS),
                                      right[:, t, 0:F].rearrange("p t (h d) -> p t h d", h=HEADS),
                                      alpha[:, t, :].rearrange("p t (h a) -> p t h a", a=1).to_broadcast([P, GROUP, HEADS, HD]),
                                      ALU.mult)
                    dve.drain()
                    dve.tensor_reduce(mean[:], mixed[:].rearrange("p t (h d) -> p t d h", h=HEADS), AX.X, ALU.add)
                    dve.drain()
                    if g == 0:
                        dve.wait_ge(x_loaded, 16)
                    xh = x[:, t, :].rearrange("p t (h d) -> p t h d", h=HEADS)
                    dve.tensor_tensor(xh, xh, mean[:].rearrange("p t (a d) -> p t a d", a=1).to_broadcast([P, GROUP, HEADS, HD]),
                                      ALU.add).then_inc(out_ready, 1)


def build_program(nc, a, out):
    def dram(name, shape, dt=fp32):
        return nc.dram_tensor(name, shape, dt, kind="Internal").ap()

    ident = a["ident"]
    order = dram("order", (NP, 4), i32)
    sort_keys = dram("sort_keys", (NP,))
    kv, q = dram("kv", (NP, 2 * F)), dram("q", (NP, F))
    attended = dram("attended", (ROWS, F))
    xs = [a["x"]] + [dram(f"x{i}", (NP, F)) for i in range(1, 8)]
    xt = dram("xt", (NP, F + 8))
    h = dram("h", (NP, F + 4))
    numbers = dram("numbers", (2 * NP,))
    hw = dram("hw", (NP, F))
    count_table = dram("count_table", (NP * NP, 1))
    weight_table = dram("weight_table", (NP * NP, 1))
    with nc.sbuf_tensor("perm", [P, ALL_TILES, 4], i32) as perm, \
            nc.sbuf_tensor("counts", [1, ALL_TILES * 8], i32) as counts, \
            nc.sbuf_tensor("cell_count", [P, TILES, SLOTS], i32) as cell_count, \
            nc.sbuf_tensor("cell_weight", [P, TILES, SLOTS], i32) as cell_weight, \
            nc.sbuf_tensor("taken", [P, TILES, SLOTS], fp32) as taken, \
            nc.sbuf_tensor("weights", [P, TILES, SLOTS], fp32) as weights:
        c, w = (cell_count, taken, count_table), (cell_weight, weights, weight_table)

        def adding(*jobs):
            return lambda s: add_cells(nc, s, counts, jobs)

        order_phase(nc, "order", a, a["dst_key"], order, sort_keys, perm, counts, (count_table, weight_table))
        projection_phase(nc, "qkv", ident, xs[0], [a["L0_gnn_Wk"], a["L0_gnn_Wv"], a["L0_gnn_Wq"]], [kv, q],
                         beside=lambda s: find_cells(nc, s, perm, a["src"], a["edge_weight"], cell_count, cell_weight,
                                                     taken, weights))
        attention_phase(nc, "gnn0", a, perm, counts, kv, q, a["src"], a["edge_attr_8"], attended)
        spill_phase(nc, "spill", perm, counts, a["src"], a["edge_weight"], count_table, weight_table)
        projection_phase(nc, "wo", ident, attended, [a["L0_gnn_Wo"]], [xs[1]], res_dram=xs[0], layernorm=False,
                         beside=adding((w, 4, 0)))
        ffn0(nc, a, xs[1], xs[2], adding((c, 0, "all"), (c, 1, 0), (w, 3, 0)))
        projection_phase(nc, "xt", ident, xs[2], [a["L1_gnn_weight"]], [xt],
                         dots=((a["L1_gnn_attn_l"], 4), (a["L1_gnn_attn_r"], 4)), beside=adding((c, 1, 1)))
        mix_phase(nc, "gnn1", a["src"], a["dst"], xt, xs[2], xs[3])
        ffn1(nc, a, xs[3], xs[4], adding((c, 2, "all"), (c, 3, "all"), (c, 4, "all"), (w, 4, 1)))
        projection_phase(nc, "h", ident, xs[4], [a["L2_gnn_W"]], [h], bias_dram=a["L2_gnn_b"],
                         dots=((a["L2_gnn_a_src"], 2), (a["L2_gnn_a_dst"], 2)), beside=adding((w, 1, 0)))
        dense_phase(nc, "gnn2", "separable", a, h, count_table, xs[4], xs[5], numbers_dram=numbers,
                    beside=adding((w, 0, "all"), (w, 2, 0), (w, 3, 1)))
        projection_phase(nc, "ffn2", ident, xs[5], [a["L2_ffn_weight"]], [xs[6]], res_dram=xs[5],
                         bias_dram=a["L2_ffn_bias"], beside=adding((w, 1, 1)))
        projection_phase(nc, "hw", ident, xs[6], [a["L3_gnn_W"]], [hw], beside=adding((w, 2, 1)))
        dense_phase(nc, "gnn3", "weighted", a, hw, weight_table, xs[6], xs[7], bias_dram=a["L3_gnn_b"])
    ffn3(nc, a, xs[7], out)


def lay_out(inputs):
    import numpy as np

    a = {k: np.asarray(v) for k, v in inputs.items()}

    def padded(v, n, value=0):
        return np.concatenate([v, np.full((n - v.shape[0],) + v.shape[1:], value, v.dtype)])

    spare = E + 2 * P
    a["x"] = padded(a["x"], NP)
    a["dst_key"] = padded(a["dst"], COLS * P, 4095)
    for k in ("src", "dst", "edge_weight"):
        a[k] = padded(a[k].reshape(E, 1), spare)
    a["edge_attr_8"] = padded(a["edge_attr_8"], spare)
    for k in ("q", "k", "v", "o"):
        a[f"L0_gnn_W{k}"] = a[f"L0_gnn_W{k}"].T
    a["L1_gnn_attn_l"] = a["L1_gnn_attn_l"].reshape(F)
    a["L1_gnn_attn_r"] = a["L1_gnn_attn_r"].reshape(F)
    a["L2_gnn_W"] = a["L2_gnn_W"].reshape(F, F).T
    a["L2_gnn_b"] = a["L2_gnn_b"].reshape(F)
    vectors = a.pop("L2_gnn_a")
    a["L2_gnn_a_src"] = vectors[:, :F // 2].reshape(F)
    a["L2_gnn_a_dst"] = vectors[:, F // 2:].reshape(F)
    a["L2_ffn_weight"] = a["L2_ffn_weight"].T
    a["ident"] = np.eye(P, dtype=np.float32)
    a["before"] = np.triu(np.ones((P, P), np.float32), 1)
    return {k: np.ascontiguousarray(v) for k, v in a.items()}


def kernel(**inputs):
    import concourse.bacc as bacc
    from concourse.bass_utils import run_bass_kernel_spmd

    nc = bacc.Bacc("TRN2", target_bir_lowering=False, num_devices=1)
    laid = lay_out(inputs)
    arrays = {f"in_{k}": v for k, v in laid.items()}
    args = {k: nc.dram_tensor(f"in_{k}", v.shape, mybir.dt.from_np(v.dtype), kind="ExternalInput").ap()
            for k, v in laid.items()}
    out = nc.dram_tensor("out_x", (NP, F), fp32, kind="ExternalOutput").ap()
    build_program(nc, args, out)
    result = run_bass_kernel_spmd(nc, [arrays], core_ids=[0])
    return result.results[0]["out_x"][:N]
```
